# Optimizing a Trainium2 kernel written in Bass

```python
import numpy as np
import jax
import jax.numpy as jnp

def _softmax(x, axis=-1):
    return jax.nn.softmax(x, axis=axis)

def _gelu(x):
    return jax.nn.gelu(x, approximate=True)

def _silu(x):
    return jax.nn.silu(x)

def _sigmoid(x):
    return jax.nn.sigmoid(x)

def _layernorm(x, axis=-1, eps=1e-05):
    m = jnp.mean(x, axis=axis, keepdims=True)
    v = jnp.var(x, axis=axis, keepdims=True)
    return (x - m) / jnp.sqrt(v + eps)

def _scatter_add(tgt, idx, src, axis=0):
    return tgt.at[idx].add(src)

def _segment_sum(src, seg, n):
    return jax.ops.segment_sum(src, seg, n)
kernel_name = 'mk_pixart_seq_d2_seqx_r4_0077da'

def setup_inputs(seed: int=0):
    np.random.seed(seed)
    _w = jnp.asarray

    def _rec_inputs():
        import jax
        import jax.numpy as jnp
        _rk = jax.random.key(seed)
        x = 7.22e-05 + 1 * jax.random.normal(jax.random.fold_in(_rk, 1), (4, 1024, 256), jnp.float32)
        _lenS = 1024 - jax.random.randint(jax.random.fold_in(_rk, 7), (4,), 0, max(1, 1024 // 4) + 1, jnp.int32)
        _lenS2 = 64 - jax.random.randint(jax.random.fold_in(_rk, 8), (4,), 0, max(1, 64 // 4) + 1, jnp.int32)
        cond_1024 = 0.000887014 + 1.03683 * jax.random.normal(jax.random.fold_in(_rk, 11), (4, 256), jnp.float32)
        _ctx_1024P = jax.random.normal(jax.random.fold_in(_rk, 12), (4, 16, 256), jnp.float32)
        _ctx_1024c = jax.random.dirichlet(jax.random.fold_in(_rk, 512), 0.3 * jnp.ones((16,), jnp.float32), (4, 64))
        _ctx_1024t = jnp.einsum('bsk,bkd->bsd', _ctx_1024c, _ctx_1024P)
        _ctx_1024t = _ctx_1024t * jax.lax.rsqrt(jnp.mean(jnp.square(_ctx_1024t)) + 1e-12) * 0.953939
        ctx_1024 = 0.00086875 + 0.999764 * (_ctx_1024t + 0.3 * jax.random.normal(jax.random.fold_in(_rk, 612), (4, 64, 256), jnp.float32))
        return (x, cond_1024, ctx_1024)
    x, cond_1024, ctx_1024 = _rec_inputs()

    def _L0_xcond_setup():
        import jax, jax.numpy as jnp
        import numpy as np
        C = 256
        H = 16
        D = C // H
        WIN = 128
        SHIFT = 64
        TOPK = 16
        HID = 1024
        EPS = 1e-06

        def _ln(x):
            x32 = x.astype(jnp.float32)
            m = x32.mean(-1, keepdims=True)
            v = jnp.mean((x32 - m) ** 2, axis=-1, keepdims=True)
            return ((x32 - m) * jax.lax.rsqrt(v + EPS)).astype(x.dtype)

        def _self_attn(h, w_qkv, b_qkv, w_so, b_so):
            B, L, _ = h.shape
            qkv = h @ w_qkv + b_qkv
            qkv = jnp.roll(qkv, -SHIFT, axis=1)
            nw = L // WIN
            qkv = qkv.reshape(B, nw, WIN, 3, H, D)
            q, k, v = (qkv[:, :, :, 0], qkv[:, :, :, 1], qkv[:, :, :, 2])
            scores = jnp.einsum('bnqhd,bnkhd->bnhqk', q, k) / jnp.sqrt(jnp.float32(D)).astype(h.dtype)
            attn = jax.nn.softmax(scores, axis=-1)
            o = jnp.einsum('bnhqk,bnkhd->bnqhd', attn, v).reshape(B, L, C)
            o = jnp.roll(o, SHIFT, axis=1)
            return o @ w_so + b_so

        def _topk_cross_attn(h, ctx, w_q, b_q, w_kv, b_kv, w_co, b_co):
            B, L, _ = h.shape
            Lc = ctx.shape[1]
            q = (h @ w_q + b_q).reshape(B, L, H, D)
            kv = (ctx @ w_kv + b_kv).reshape(B, Lc, 2, H, D)
            k, v = (kv[:, :, 0], kv[:, :, 1])
            scores = jnp.einsum('bqhd,bkhd->bhqk', q, k) / jnp.sqrt(jnp.float32(D)).astype(h.dtype)
            top_s, top_i = jax.lax.top_k(scores, TOPK)
            attn = jax.nn.softmax(top_s, axis=-1)
            v_bh = jnp.transpose(v, (0, 2, 1, 3))
            vg = jnp.take_along_axis(v_bh[:, :, None, :, :], top_i[..., None], axis=3)
            o = jnp.einsum('bhqk,bhqkd->bqhd', attn, vg).reshape(B, L, C)
            return o @ w_co + b_co

        def _swiglu(h, w_m1, b_m1, w_m2, b_m2):
            u = h @ w_m1 + b_m1
            a, b = (u[..., :HID], u[..., HID:])
            return jax.nn.silu(a) * b @ w_m2 + b_m2
        key = jax.random.key(seed)
        ks = jax.random.split(key, 24)
        s = 0.02
        inp = {'x': jax.random.normal(ks[0], (2, 1024, C), jnp.float32), 'mod': jax.random.normal(ks[1], (2, C), jnp.float32), 'context': jax.random.normal(ks[2], (2, 256, C), jnp.float32), 'w_ada': jax.random.normal(ks[3], (C, 9 * C), jnp.float32) * s, 'b_ada': jnp.zeros((9 * C,), jnp.float32), 'w_qkv': jax.random.normal(ks[4], (C, 3 * C), jnp.float32) * s, 'b_qkv': jnp.zeros((3 * C,), jnp.float32), 'w_so': jax.random.normal(ks[5], (C, C), jnp.float32) * s, 'b_so': jnp.zeros((C,), jnp.float32), 'w_q': jax.random.normal(ks[6], (C, C), jnp.float32) * s, 'b_q': jnp.zeros((C,), jnp.float32), 'w_kv': jax.random.normal(ks[7], (C, 2 * C), jnp.float32) * s, 'b_kv': jnp.zeros((2 * C,), jnp.float32), 'w_co': jax.random.normal(ks[8], (C, C), jnp.float32) * s, 'b_co': jnp.zeros((C,), jnp.float32), 'w_m1': jax.random.normal(ks[9], (C, 2 * HID), jnp.float32) * s, 'b_m1': jnp.zeros((2 * HID,), jnp.float32), 'w_m2': jax.random.normal(ks[10], (HID, C), jnp.float32) * s, 'b_m2': jnp.zeros((C,), jnp.float32)}
        return inp
    _L0_xcond_all = _L0_xcond_setup()
    _L0_xcond_in = {k: v for k, v in _L0_xcond_all.items() if k in ('w_ada', 'b_ada', 'w_qkv', 'b_qkv', 'w_so', 'b_so', 'w_q', 'b_q', 'w_kv', 'b_kv', 'w_co', 'b_co', 'w_m1', 'b_m1', 'w_m2', 'b_m2')}
    del _L0_xcond_all

    def _L1_xcond_setup():
        import jax, jax.numpy as jnp
        import numpy as np
        EPS = 1e-05

        def _ada_ln(x, c, W_ss, b_ss):
            mu = jnp.mean(x, axis=-1, keepdims=True)
            var = jnp.mean((x - mu) ** 2, axis=-1, keepdims=True)
            h = (x - mu) / jnp.sqrt(var + EPS)
            ss = jax.nn.silu(c) @ W_ss + b_ss
            scale, bias = jnp.split(ss, 2, axis=-1)
            return (1.0 + scale)[:, None, :] * h + bias[:, None, :]
        key = jax.random.key(seed)
        ks = jax.random.split(key, 12)
        B, Lq, Lkv, H = (8, 512, 128, 256)
        s = 0.02
        return {'x_q': jax.random.normal(ks[0], (B, Lq, H), jnp.float32), 'x_kv': jax.random.normal(ks[1], (B, Lkv, H), jnp.float32), 't_vec': jax.random.normal(ks[2], (B, H), jnp.float32), 'Wq': jax.random.normal(ks[3], (H, H), jnp.float32) * s, 'bq': jnp.zeros((H,), jnp.float32), 'Wkv': jax.random.normal(ks[4], (H, 2 * H), jnp.float32) * s, 'bkv': jnp.zeros((2 * H,), jnp.float32), 'Wp': jax.random.normal(ks[5], (H, H), jnp.float32) * s, 'bp': jnp.zeros((H,), jnp.float32), 'Wss_q': jax.random.normal(ks[6], (H, 2 * H), jnp.float32) * s, 'bss_q': jnp.zeros((2 * H,), jnp.float32), 'Wss_kv': jax.random.normal(ks[7], (H, 2 * H), jnp.float32) * s, 'bss_kv': jnp.zeros((2 * H,), jnp.float32)}
    _L1_xcond_all = _L1_xcond_setup()
    _L1_xcond_in = {k: v for k, v in _L1_xcond_all.items() if k in ('Wq', 'bq', 'Wkv', 'bkv', 'Wp', 'bp', 'Wss_q', 'bss_q', 'Wss_kv', 'bss_kv')}
    del _L1_xcond_all
    return {'x': x, 'cond_1024': cond_1024, 'ctx_1024': ctx_1024, 'L0_xcond_w_ada': _L0_xcond_in['w_ada'], 'L0_xcond_b_ada': _L0_xcond_in['b_ada'], 'L0_xcond_w_qkv': _L0_xcond_in['w_qkv'], 'L0_xcond_b_qkv': _L0_xcond_in['b_qkv'], 'L0_xcond_w_so': _L0_xcond_in['w_so'], 'L0_xcond_b_so': _L0_xcond_in['b_so'], 'L0_xcond_w_q': _L0_xcond_in['w_q'], 'L0_xcond_b_q': _L0_xcond_in['b_q'], 'L0_xcond_w_kv': _L0_xcond_in['w_kv'], 'L0_xcond_b_kv': _L0_xcond_in['b_kv'], 'L0_xcond_w_co': _L0_xcond_in['w_co'], 'L0_xcond_b_co': _L0_xcond_in['b_co'], 'L0_xcond_w_m1': _L0_xcond_in['w_m1'], 'L0_xcond_b_m1': _L0_xcond_in['b_m1'], 'L0_xcond_w_m2': _L0_xcond_in['w_m2'], 'L0_xcond_b_m2': _L0_xcond_in['b_m2'], 'L1_xcond_Wq': _L1_xcond_in['Wq'], 'L1_xcond_bq': _L1_xcond_in['bq'], 'L1_xcond_Wkv': _L1_xcond_in['Wkv'], 'L1_xcond_bkv': _L1_xcond_in['bkv'], 'L1_xcond_Wp': _L1_xcond_in['Wp'], 'L1_xcond_bp': _L1_xcond_in['bp'], 'L1_xcond_Wss_q': _L1_xcond_in['Wss_q'], 'L1_xcond_bss_q': _L1_xcond_in['bss_q'], 'L1_xcond_Wss_kv': _L1_xcond_in['Wss_kv'], 'L1_xcond_bss_kv': _L1_xcond_in['bss_kv']}

def reference(x, cond_1024, ctx_1024, L0_xcond_w_ada, L0_xcond_b_ada, L0_xcond_w_qkv, L0_xcond_b_qkv, L0_xcond_w_so, L0_xcond_b_so, L0_xcond_w_q, L0_xcond_b_q, L0_xcond_w_kv, L0_xcond_b_kv, L0_xcond_w_co, L0_xcond_b_co, L0_xcond_w_m1, L0_xcond_b_m1, L0_xcond_w_m2, L0_xcond_b_m2, L1_xcond_Wq, L1_xcond_bq, L1_xcond_Wkv, L1_xcond_bkv, L1_xcond_Wp, L1_xcond_bp, L1_xcond_Wss_q, L1_xcond_bss_q, L1_xcond_Wss_kv, L1_xcond_bss_kv):
    import jax
    import jax.numpy as jnp

    def _L0_xcond_ref(x, mod, context, w_ada, b_ada, w_qkv, b_qkv, w_so, b_so, w_q, b_q, w_kv, b_kv, w_co, b_co, w_m1, b_m1, w_m2, b_m2):
        import jax, jax.numpy as jnp
        import numpy as np
        C = 256
        H = 16
        D = C // H
        WIN = 128
        SHIFT = 64
        TOPK = 16
        HID = 1024
        EPS = 1e-06

        def _ln(x):
            x32 = x.astype(jnp.float32)
            m = x32.mean(-1, keepdims=True)
            v = jnp.mean((x32 - m) ** 2, axis=-1, keepdims=True)
            return ((x32 - m) * jax.lax.rsqrt(v + EPS)).astype(x.dtype)

        def _self_attn(h, w_qkv, b_qkv, w_so, b_so):
            B, L, _ = h.shape
            qkv = h @ w_qkv + b_qkv
            qkv = jnp.roll(qkv, -SHIFT, axis=1)
            nw = L // WIN
            qkv = qkv.reshape(B, nw, WIN, 3, H, D)
            q, k, v = (qkv[:, :, :, 0], qkv[:, :, :, 1], qkv[:, :, :, 2])
            scores = jnp.einsum('bnqhd,bnkhd->bnhqk', q, k) / jnp.sqrt(jnp.float32(D)).astype(h.dtype)
            attn = jax.nn.softmax(scores, axis=-1)
            o = jnp.einsum('bnhqk,bnkhd->bnqhd', attn, v).reshape(B, L, C)
            o = jnp.roll(o, SHIFT, axis=1)
            return o @ w_so + b_so

        def _topk_cross_attn(h, ctx, w_q, b_q, w_kv, b_kv, w_co, b_co):
            B, L, _ = h.shape
            Lc = ctx.shape[1]
            q = (h @ w_q + b_q).reshape(B, L, H, D)
            kv = (ctx @ w_kv + b_kv).reshape(B, Lc, 2, H, D)
            k, v = (kv[:, :, 0], kv[:, :, 1])
            scores = jnp.einsum('bqhd,bkhd->bhqk', q, k) / jnp.sqrt(jnp.float32(D)).astype(h.dtype)
            top_s, top_i = jax.lax.top_k(scores, TOPK)
            attn = jax.nn.softmax(top_s, axis=-1)
            v_bh = jnp.transpose(v, (0, 2, 1, 3))
            vg = jnp.take_along_axis(v_bh[:, :, None, :, :], top_i[..., None], axis=3)
            o = jnp.einsum('bhqk,bhqkd->bqhd', attn, vg).reshape(B, L, C)
            return o @ w_co + b_co

        def _swiglu(h, w_m1, b_m1, w_m2, b_m2):
            u = h @ w_m1 + b_m1
            a, b = (u[..., :HID], u[..., HID:])
            return jax.nn.silu(a) * b @ w_m2 + b_m2
        m = jax.nn.silu(mod) @ w_ada + b_ada
        sh_msa, sc_msa, g_msa, sh_mca, sc_mca, g_mca, sh_mlp, sc_mlp, g_mlp = [m[:, i * C:(i + 1) * C][:, None, :] for i in range(9)]
        h = _ln(x) * (1 + sc_msa) + sh_msa
        h = _self_attn(h, w_qkv, b_qkv, w_so, b_so)
        x = x + h * g_msa
        h = _ln(x) * (1 + sc_mca) + sh_mca
        h = _topk_cross_attn(h, context, w_q, b_q, w_kv, b_kv, w_co, b_co)
        x = x + h * g_mca
        h = _ln(x) * (1 + sc_mlp) + sh_mlp
        h = _swiglu(h, w_m1, b_m1, w_m2, b_m2)
        x = x + h * g_mlp
        return x

    def _L1_xcond_ref(x_q, x_kv, t_vec, Wq, bq, Wkv, bkv, Wp, bp, Wss_q, bss_q, Wss_kv, bss_kv):
        import jax, jax.numpy as jnp
        import numpy as np
        EPS = 1e-05

        def _ada_ln(x, c, W_ss, b_ss):
            mu = jnp.mean(x, axis=-1, keepdims=True)
            var = jnp.mean((x - mu) ** 2, axis=-1, keepdims=True)
            h = (x - mu) / jnp.sqrt(var + EPS)
            ss = jax.nn.silu(c) @ W_ss + b_ss
            scale, bias = jnp.split(ss, 2, axis=-1)
            return (1.0 + scale)[:, None, :] * h + bias[:, None, :]
        B, Lq, H = x_q.shape
        Lkv = x_kv.shape[1]
        nh = 16
        dh = H // nh
        xq = _ada_ln(x_q, t_vec, Wss_q, bss_q)
        xkv = _ada_ln(x_kv, t_vec, Wss_kv, bss_kv)
        q = (xq @ Wq + bq).reshape(B, Lq, nh, dh)
        kv = (xkv @ Wkv + bkv).reshape(B, Lkv, 2, nh, dh)
        k = kv[:, :, 0]
        v = kv[:, :, 1]
        scores = jnp.einsum('bqhd,bkhd->bhqk', q, k) / jnp.sqrt(jnp.float32(dh))
        attn = jax.nn.softmax(scores, axis=-1)
        out = jnp.einsum('bhqk,bkhd->bqhd', attn, v).reshape(B, Lq, H)
        return x_q + (out @ Wp + bp)
    x = _L0_xcond_ref(x, cond_1024, ctx_1024, L0_xcond_w_ada, L0_xcond_b_ada, L0_xcond_w_qkv, L0_xcond_b_qkv, L0_xcond_w_so, L0_xcond_b_so, L0_xcond_w_q, L0_xcond_b_q, L0_xcond_w_kv, L0_xcond_b_kv, L0_xcond_w_co, L0_xcond_b_co, L0_xcond_w_m1, L0_xcond_b_m1, L0_xcond_w_m2, L0_xcond_b_m2)
    x = _L1_xcond_ref(x, ctx_1024, cond_1024, L1_xcond_Wq, L1_xcond_bq, L1_xcond_Wkv, L1_xcond_bkv, L1_xcond_Wp, L1_xcond_bp, L1_xcond_Wss_q, L1_xcond_bss_q, L1_xcond_Wss_kv, L1_xcond_bss_kv)
    return x

_drawn_inputs = setup_inputs


def setup_inputs(seed=0):
    import zlib

    import numpy as np

    out = dict(_drawn_inputs(seed))
    spreads = {'L0_xcond_b_ada': (0.0, 0.399),
     'L0_xcond_b_qkv': (0.0, 0.8),
     'L0_xcond_b_so': (0.0, 0.375),
     'L0_xcond_b_q': (0.0, 0.8),
     'L0_xcond_b_kv': (0.0, 0.8),
     'L0_xcond_b_co': (0.0, 0.396),
     'L0_xcond_b_m1': (0.0, 0.8),
     'L0_xcond_b_m2': (0.0, 1.429),
     'L1_xcond_bq': (0.0, 2.0),
     'L1_xcond_bkv': (0.0, 0.8),
     'L1_xcond_bp': (0.0, 0.642),
     'L1_xcond_bss_q': (0.0, 2.0),
     'L1_xcond_bss_kv': (0.0, 2.0)}
    factors = {'L0_xcond_w_qkv': 8.0,
     'L0_xcond_w_so': 6.101,
     'L0_xcond_w_q': 7.992,
     'L0_xcond_w_kv': 3.963,
     'L0_xcond_w_co': 3.569,
     'L0_xcond_w_m1': 6.127,
     'L0_xcond_w_m2': 6.11,
     'L1_xcond_Wq': 54.884,
     'L1_xcond_Wss_q': 62.453,
     'L1_xcond_Wkv': 3.861,
     'L1_xcond_Wp': 3.794,
     'L1_xcond_Wss_kv': 8.0}
    for name, (base, spread) in spreads.items():
        noise = np.random.default_rng([zlib.crc32(name.encode()), seed]).standard_normal(out[name].shape)
        drawn = base * np.exp(spread * noise) if base else spread * noise
        out[name] = jnp.asarray(drawn.astype(out[name].dtype))
    for name, factor in factors.items():
        out[name] = (out[name] * factor).astype(out[name].dtype)
    return out
```

```python
from contextlib import ExitStack

import concourse.bass as bass
from concourse import mybir

F32 = mybir.dt.float32
F32R = mybir.dt.float32r
BF16 = mybir.dt.bfloat16
ALU = mybir.AluOpType
ACT = mybir.ActivationFunctionType
AX_X = mybir.AxisListType.X

P = 128
B, L, C = 4, 1024, 256
LC = 64
H, D = 16, 16
SHIFT = 64
HID = 1024
TOPK = 16
KC = C // P
HPC = P // D
PAIRS = H // 2
W = 4
BT = W * P
BLKS = L // BT
J = HID // P
SCORE_SCALE = 1.0 / D ** 0.5
REPLACED = -3.0e38
EPS0, EPS1 = 1e-6, 1e-5

MSA, MCA, MLP, XQ, XKV = range(5)
NMOD = 5

CB = {}
_at = 0
for _name, _n in (("shift", NMOD * KC), ("scale", NMOD * KC), ("qk", 2 * KC), ("q2", KC), ("k0", KC),
                  ("m1", 2 * J), ("q3", KC), ("k1", KC)):
    CB[_name] = _at
    _at += _n
NCB = _at
ROWS = ("v_self", "p", "so", "co", "m2", "v0", "v1")


def before_loop():
    yield ("mod",)
    for i in range(2):
        yield ("gate", i)
    for a in range(2):
        if a == 1:
            for c in range(KC):
                yield ("Tc", c)
        for c in range(KC):
            yield ("kT", a, c)
        for u in range(B // 2):
            yield ("vc", a, u)


def in_loop():
    def transposed(n, b):
        for c in range(KC):
            yield ("T", n, b, c)

    def heads_in(b):
        yield from transposed(1, b)
        for i in range(2 * KC):
            yield ("qk", b, i)
        for u in range(2):
            yield ("v", b, u)

    def windows(b):
        for g in range(4):
            yield ("A", b, 0, g)
        for w in range(W):
            if w + 1 < W:
                for g in range(4):
                    yield ("A", b, w + 1, g)
            yield ("mT", b, w)
            for g in range(4):
                yield ("B", b, w, g)
            if w:
                yield ("PV", b, w - 1)
        yield ("PV", b, W - 1)
        for u in range(2):
            yield ("y", 1, b, u)

    def cross_in(b):
        yield from transposed(2, b)
        for c in range(KC):
            yield ("q2", b, c)

    def scores(b):
        for t in range(W):
            for c in range(KC):
                yield ("S", b, t, c)

    def weigh(b):
        for t in range(W):
            for c in range(KC):
                yield ("TP", b, t, c)
        yield from values(2, b)

    def values(n, b):
        for c in range(KC):
            yield ("D", n, b, c)
            yield ("O", n, b, c)

    def project(n, b):
        for u in range(2):
            yield ("y", n, b, u)

    def mlp(b):
        yield from transposed(3, b)
        for j in range(J):
            yield ("ua", b, j)
            yield ("ub", b, j)
        yield from project(3, b)

    def last(b):
        yield from transposed(4, b)
        for c in range(KC):
            yield ("q3", b, c)
        for t in range(W):
            for c in range(KC):
                yield ("A3", b, t, c)
        for p in range(PAIRS):
            yield ("B3", b, p)
            if p == 2:
                yield ("mT3", b)
        yield from values(4, b)
        yield from project(4, b)

    yield from heads_in(0)
    yield from windows(0)
    yield from heads_in(1)
    yield from cross_in(0)
    yield from scores(0)
    yield from windows(1)
    yield from weigh(0)
    yield from cross_in(1)
    yield from project(2, 0)
    yield from scores(1)
    yield from mlp(0)
    yield from weigh(1)
    yield from project(2, 1)
    yield from last(0)
    yield from mlp(1)
    yield from last(1)


NB = 8
PRE, LOOP = list(before_loop()), list(in_loop())
PRE_USES = [len(PRE[n::NB]) for n in range(NB)]
ROUNDS = [len(LOOP[n::NB]) for n in range(NB)]
PLACE = {key: (n % NB, n // NB) for n, key in enumerate(PRE)}
PLACE.update({key: (n % NB, PRE_USES[n % NB] + n // NB) for n, key in enumerate(LOOP)})
assert len(PLACE) == len(PRE) + len(LOOP)


class Chain:

    def __init__(self, eng, sem):
        self.eng, self.sem, self.n = eng, sem, 0

    def step(self, instruction):
        self.n += 1
        instruction.then_inc(self.sem, 1)

    def wait(self):
        self.eng.wait_ge(self.sem, self.n)

    def restart(self):
        self.eng.wait_ge(self.sem, self.n)
        self.eng.sem_clear(self.sem)
        self.n = 0


def build(nc, t_in, out):
    ctx = ExitStack()
    with ctx:
        def sb(name, shape, dt=F32):
            return ctx.enter_context(nc.sbuf_tensor(name, shape, dt))

        def sem(name):
            return ctx.enter_context(nc.semaphore(name))

        gate_d = nc.dram_tensor("gate_rows", [B, 3 * C], F32, kind="Internal").ap()
        kbd_d = nc.dram_tensor("keys_by_head", [2, B, P, KC * HPC * LC], F32, kind="Internal").ap()
        vbd_d = nc.dram_tensor("values_by_pair", [2, B, P, C], F32, kind="Internal").ap()

        w_qkv = sb("w_qkv", [P, KC, 3 * C])
        w_q2 = sb("w_q2", [P, KC, C])
        w_m1 = sb("w_m1", [P, KC, 2 * HID])
        w_q3 = sb("w_q3", [P, KC, C])
        w_p = sb("w_p", [P, KC, C])
        w_so = sb("w_so", [P, KC, C])
        w_co = sb("w_co", [P, KC, C])
        w_m2 = sb("w_m2", [P, J, C])
        chan = sb("chan", [P, NCB])
        rows = sb("rows", [P, 5, C])
        gate = sb("gate", [P, 3, C])
        gated_bias = sb("gated_bias", [P, 3, C])
        mod = sb("mod", [P, 2, NMOD, KC, B])
        cur = sb("cur", [P, 2, NMOD, KC])
        ident = sb("ident", [P, P])
        identb = sb("identb", [P, P], BF16)
        head_rows = sb("head_rows", [P, H, P], BF16)
        head_mask = sb("head_mask", [P, HPC])
        pair_mask = sb("pair_mask", [P, 2 * D])
        ones_half = sb("ones_half", [P, 2, 2 * D])
        minus_half = sb("minus_half", [P, W])
        xin = sb("xin", [P, W, C])
        x = sb("x", [P, BLKS, W, C])
        xh = sb("xh", [P, W, C])
        hT = sb("hT", [P, KC, BT])
        qk = sb("qk", [P, 2 * KC, BT])
        qr = sb("qr", [P, KC, BT], F32R)
        bd = sb("bd", [P, 2, HPC, 2 * KC, P])
        vpad = sb("vpad", [P, W, PAIRS, 4 * D])
        arena = sb("arena", [P, 12288])
        oT = sb("oT", [P, KC, BT])
        stats = sb("stats", [P, W, 6])
        mv = sb("mv", [P, W, 2])
        veps = sb("veps", [P, W])
        rstd = sb("rstd", [P, W])
        negm = sb("negm", [P, W, H])
        mst = sb("mst", [P, W, P], BF16)
        mTs = sb("mTs", [P, BT], BF16)
        rden = sb("rden", [P, 2, BT])
        top = sb("top", [P, H, TOPK])
        left = sb("left", [P, H, LC])
        eS = sb("eS", [P, H, LC])
        kbd = sb("kbd", [P, KC, HPC * LC])
        kbd1r = sb("kbd1r", [P, KC, HPC * LC], F32R)
        vbd0 = sb("vbd0", [P, PAIRS, 2 * D])
        vbd1 = sb("vbd1", [P, PAIRS, 2 * D])

        pT = arena[:, 0:4096]
        pT_self = pT.rearrange("p (n h q) -> p n h q", n=2, h=H)
        pT_cross = pT.rearrange("p (h q) -> p h q", h=PAIRS)
        S = arena[:, 4096:8192].rearrange("p (t n) -> p t n", t=W)
        hid = arena[:, 8192:12288].rearrange("p (j n) -> p j n", j=J)
        kT = hid[:, 0:KC, :]
        sa = rden
        q2T = hT
        at = [0]

        def early(n):
            at[0] += n
            return arena[:, at[0] - n:at[0]]

        w_ada = early(KC * 9 * C).rearrange("p (k n) -> p k n", k=KC)
        w_ss = [early(KC * 2 * C).rearrange("p (k n) -> p k n", k=KC) for _ in range(2)]
        w_kv = [early(KC * 2 * C).rearrange("p (k n) -> p k n", k=KC) for _ in range(2)]
        v_out = early(2 * B * C).rearrange("p (a b n) -> p a b n", a=2, b=B)
        src2 = early(KC * B * 2 * LC).rearrange("p (k b d n) -> p k b d n", k=KC, b=B, d=2)
        keysT = early(KC * B * LC).rearrange("p (k n) -> p k n", k=KC)
        srcT = hT[:, 0, :].rearrange("p (k n) -> p k n", k=KC)
        modT = hT[:, 1, :].rearrange("p (k n) -> p k n", k=KC)
        x_keys = x[:, 0].rearrange("p t n -> p (t n)").rearrange("p (c n) -> p c n", c=KC)
        keys_out = [kbd[:], x_keys, left[:].rearrange("p (c h) n -> p c (h n)", c=KC),
                    eS[:].rearrange("p (c h) n -> p c (h n)", c=KC)]
        ctx_rows = xin[:, 0:2, :]
        condT = rden[:, 0, 0:KC * B].rearrange("p (k b) -> p k b", k=KC)
        scondT = rden[:, 0, 16:16 + KC * B].rearrange("p (k b) -> p k b", k=KC)
        gate_in = oT[0:B, :, :].rearrange("p k n -> p (k n)")[:, 0:3 * C]
        gate_out = qk[0:B, 0:2, :].rearrange("p k n -> p (k n)")[:, 0:3 * C]
        vrow = [qk[:, KC, 0:C], qk[:, KC, C:2 * C]]
        head_rows_f = x[:].rearrange("p b t n -> p (b t n)")

        bank = [ctx.enter_context(nc.psum_tensor(f"bank{i}", [P, BT], F32)) for i in range(NB)]

        filled = [sem(f"filled{i}") for i in range(NB)]
        drained = [sem(f"drained{i}") for i in range(NB)]
        s_early = sem("early_inputs_loaded")
        s_consts = sem("constants_loaded")
        s_weights = sem("weights_loaded")
        s_silu_c = sem("condition_silu_done")
        s_mod = sem("modulations_done")
        s_gate = sem("gate_rows_done")
        s_src2 = sem("context_doubled")
        s_keys = sem("early_keys_done")
        s_keys_stored = sem("early_keys_stored")
        s_vals = sem("early_values_done")
        s_gate_stored = sem("gate_rows_stored")
        s_zero = sem("head_blocks_zeroed")
        s_const_ready = sem("constants_rounded")
        s_half = sem("exponent_set")
        s_xin = sem("x_loaded")
        s_g = sem("gate_loaded")
        s_wso, s_wco, s_wm2 = sem("w_so_loaded"), sem("w_co_loaded"), sem("w_m2_loaded")
        s_kv0, s_kv1 = sem("keys_values0_loaded"), sem("keys_values1_loaded")
        s_cur = sem("modulations_of_batch")
        s_gated = sem("gated_done")
        s_kr = sem("keys1_rounded")
        s_mv = sem("moments_done")
        s_rstd = sem("rstd_done")
        s_xh = sem("tiles_normalised")
        s_xb = sem("bias_added")
        s_qkr = sem("qk_rounded")
        s_q3r = sem("q3_rounded")
        s_bd = [sem("by_head_even"), sem("by_head_odd")]
        s_mst = sem("self_max_split")
        s_mst3 = sem("cross_max_split")
        s_rd1 = sem("self_denominators")
        s_rd = sem("cross_denominators")
        s_top8 = sem("top8_done")
        s_dif = sem("max_subtracted")
        s_exp = sem("topk_exp_done")
        s_prob = sem("topk_probs_done")
        s_store = [sem("stored0"), sem("stored1")]
        s_held = {nc.vector: sem("vector_held"), nc.gpsimd: sem("gpsimd_held")}
        s_dve, s_act, s_pool = sem("vector_step"), sem("scalar_step"), sem("gpsimd_step")

        def hold(eng):
            eng.sem_inc(s_held[eng], 1)

        def ps(key):
            return bank[PLACE[key][0]][:]

        def fill_wait(pe, key, it):
            b, n = PLACE[key]
            if n:
                pe.wait_ge(drained[b], it * ROUNDS[b] + n)

        def filled_wait(eng, key, it):
            b, n = PLACE[key]
            eng.wait_ge(filled[b], it * ROUNDS[b] + n + 1)

        def drained_wait(eng, key, it):
            b, n = PLACE[key]
            eng.wait_ge(drained[b], it * ROUNDS[b] + n + 1)

        def fill(ins, key):
            ins.then_inc(filled[PLACE[key][0]], 1)

        def drain(ins, key):
            ins.then_inc(drained[PLACE[key][0]], 1)

        ORDER = [(1, 0), (1, 1), (2, 0), (2, 1), (3, 0), (4, 0), (3, 1), (4, 1)]
        LN = {k: n for n, k in enumerate(ORDER)}
        NLN = len(ORDER)
        MOD_OF = {1: MSA, 2: MCA, 3: MLP, 4: XQ}
        TILES = BLKS * W

        block = ctx.enter_context(nc.Block())

        @block.sync
        def _(sp):
            def wv(name):
                return t_in[name].rearrange("(k p) n -> p k n", p=P)

            for dst, src in ((condT, t_in["condT"]), (srcT, t_in["ctxT"]), (ctx_rows, t_in["ctx_rows"]),
                             (chan[:], t_in["chan"]), (gate_in, t_in["gate_bias"].to_broadcast([B, 3 * C])),
                             (rows[:].rearrange("p r n -> p (r n)"), t_in["rows"][:, 0:5 * C].to_broadcast([P, 5 * C])),
                             (vrow[0], t_in["rows"][:, 5 * C:6 * C].to_broadcast([P, C])),
                             (vrow[1], t_in["rows"][:, 6 * C:7 * C].to_broadcast([P, C])),
                             (w_ada, wv("w_ada")), (w_ss[0], wv("Wss_q")), (w_ss[1], wv("Wss_kv")),
                             (w_kv[0], wv("w_kv")), (w_kv[1], wv("Wkv"))):
                sp.dma_start(dst, src).then_inc(s_early, 16)
            for dst, src in ((ident[:], t_in["ident"]), (head_rows_f, t_in["head_rows"]),
                             (head_mask[:], t_in["head_mask"]),
                             (pair_mask[:], t_in["pair_mask"]),
                             (ones_half[:].rearrange("p s n -> p (s n)"), t_in["ones_half"])):
                sp.dma_start(dst, src).then_inc(s_consts, 16)
            for dst, name in ((w_qkv, "w_qkv"), (w_q2, "w_q"), (w_m1, "w_m1"), (w_q3, "Wq"), (w_p, "Wp")):
                sp.dma_start(dst[:], wv(name)).then_inc(s_weights, 16)
            sp.wait_ge(s_gate, 2)
            sp.dma_start(gate_d, gate_out).then_inc(s_gate_stored, 16)
            for a in range(2):
                for b in range(B):
                    sp.wait_ge(s_keys, a * B + b + 1)
                    sp.dma_start(kbd_d[a, b].rearrange("p (c n) -> p c n", c=KC), keys_out[b]).then_inc(s_keys_stored, 16)
            sp.wait_ge(s_gate_stored, 16)
            sp.wait_ge(s_keys_stored, 2 * B * 16)
            sp.wait_ge(s_store[0], 16)
            sp.wait_ge(s_store[1], 16)
            sp.wait_ge(s_zero, 2)
            with sp.Fori(0, B) as it:
                x_d = t_in["x"]

                def load_bd(b, w):
                    if w >= 2:
                        filled_wait(sp, ("B", b, w - 2, 3), it)
                    elif b:
                        filled_wait(sp, ("B", b - 1, w + 2, 3), it)
                    if w == 0:
                        sp.wait_ge(s_qkr, (it * BLKS + b) * 4 + 4)
                    for h in range(HPC):
                        r = slice(h * D, (h + 1) * D)
                        sp.dma_start(bd[r, w % 2, h, :, :], qk[r, :, w * P:(w + 1) * P]).then_inc(s_bd[w % 2], 16)

                sp.wait_ge(s_xb, it * NLN + 1)
                sp.dma_start(xin[:], x_d[bass.ds(it * L + SHIFT, BT), :].rearrange("(t p) n -> p t n", p=P)).then_inc(s_xin, 16)
                filled_wait(sp, ("T", 1, 0, 0), it)
                sp.dma_start(gate[:].rearrange("p g n -> p (g n)"),
                             gate_d[bass.ds(it, 1), :].to_broadcast([P, 3 * C])).then_inc(s_g, 16)
                load_bd(0, 0)
                load_bd(0, 1)
                sp.dma_start(w_so[:], wv("w_so")).then_inc(s_wso, 16)
                sp.dma_start(kbd[:].rearrange("p c n -> p (c n)"), kbd_d[0][bass.ds(it, 1)].rearrange("a p n -> (a p) n")).then_inc(s_kv0, 16)
                sp.dma_start(vbd0[:].rearrange("p c n -> p (c n)"), vbd_d[0][bass.ds(it, 1)].rearrange("a p n -> (a p) n")).then_inc(s_kv0, 16)
                load_bd(0, 2)
                sp.wait_ge(s_xb, it * NLN + LN[1, 0] + 2)
                sp.dma_start(xin[:, 0:W - 1, :], x_d[bass.ds(it * L + BT + SHIFT, BT - P), :]
                             .rearrange("(t p) n -> p t n", p=P)).then_inc(s_xin, 16)
                sp.dma_start(xin[0:P - SHIFT, W - 1, :], x_d[bass.ds(it * L + L - P + SHIFT, P - SHIFT), :]).then_inc(s_xin, 16)
                sp.dma_start(xin[P - SHIFT:P, W - 1, :], x_d[bass.ds(it * L, SHIFT), :]).then_inc(s_xin, 16)
                load_bd(0, 3)
                sp.dma_start(w_co[:], wv("w_co")).then_inc(s_wco, 16)
                load_bd(1, 0)
                load_bd(1, 1)
                sp.dma_start(w_m2[:], wv("w_m2")).then_inc(s_wm2, 16)
                load_bd(1, 2)
                load_bd(1, 3)
                filled_wait(sp, ("S", 1, W - 1, KC - 1), it)
                sp.dma_start(kbd[:].rearrange("p c n -> p (c n)"), kbd_d[1][bass.ds(it, 1)].rearrange("a p n -> (a p) n")).then_inc(s_kv1, 16)
                sp.dma_start(vbd1[:].rearrange("p c n -> p (c n)"), vbd_d[1][bass.ds(it, 1)].rearrange("a p n -> (a p) n")).then_inc(s_kv1, 16)
            sp.wait_ge(s_store[0], (B + 1) * 16)
            sp.wait_ge(s_store[1], (3 * B + 1) * 16)

        @block.gpsimd
        def _(pool):
            own = Chain(pool, s_pool)

            def rstd_of(n, eps):
                hold(pool)
                own.step(nc.gpsimd.tensor_scalar(veps[:, 0:n], mv[:, 0:n, 1], eps, 0.0, ALU.add, ALU.add))
                own.wait()
                nc.gpsimd.tensor_tensor(rstd[:, 0:n], veps[:, 0:n], minus_half[:, 0:n], ALU.pow).then_inc(s_rstd, 1)

            own.step(nc.gpsimd.memset(minus_half[:], -0.5))
            own.wait()
            nc.gpsimd.memset(bd[:, 0], 0.0).then_inc(s_zero, 1)
            pool.sem_inc(s_xb, 1)
            pool.wait_ge(s_mv, 1)
            rstd_of(B // 2, EPS1)
            for a in range(2):
                pool.wait_ge(s_vals, 2 * (a + 1))
                pool.dma_start(vbd_d[a].rearrange("b p n -> p b n"), v_out[:, a]).then_inc(s_store[a], 16)
            own.restart()
            with pool.Fori(0, B) as it:
                def rstd_step(n, b):
                    pool.wait_ge(s_mv, it * NLN + LN[n, b] + 2)
                    rstd_of(W, EPS1 if n == 4 else EPS0)

                def add_bias(n, b):
                    pool.wait_ge(s_xh, (it * NLN + LN[n, b]) * W + W + 2)
                    src = x[:, b]
                    if n == 1:
                        src = xin[:]
                        pool.wait_ge(s_store[b], it * (48 if b else 16) + 16)
                    row = rows[:, 1, :] if n == 4 else gated_bias[:, n - 1, :]
                    nc.gpsimd.tensor_tensor(x[:, b], src, row.unsqueeze(1).to_broadcast([P, W, C]), ALU.add).then_inc(s_xb, 1)

                def round_qk(b):
                    for c in range(KC):
                        drained_wait(pool, ("qk", b, c), it)
                        hold(pool)
                        nc.gpsimd.tensor_scalar(qr[:, c, :], qk[:, c, :], 1.0, 0.0, ALU.mult, ALU.add).then_inc(s_qkr, 1)
                    for c in range(KC):
                        drained_wait(pool, ("qk", b, KC + c), it)
                        hold(pool)
                        nc.gpsimd.tensor_scalar(qk[:, KC + c, :].bitcast(F32R), kT[:, c, :], 1.0, 0.0,
                                                ALU.mult, ALU.add).then_inc(s_qkr, 1)

                def round_q3(b):
                    for c in range(KC):
                        drained_wait(pool, ("q3", b, c), it)
                        hold(pool)
                        nc.gpsimd.tensor_scalar(qr[:, c, :], qk[:, c, :], 1.0, 0.0, ALU.mult, ALU.add).then_inc(s_q3r, 1)

                def gate_weight(w, layer, loaded, n):
                    pool.wait_ge(loaded, it * 16 + 16)
                    for k in range(0, n, KC):
                        i = nc.gpsimd.tensor_tensor(w[:, k:k + KC, :], w[:, k:k + KC, :],
                                                    gate[:, layer, :].unsqueeze(1).to_broadcast([P, KC, C]), ALU.mult)
                    i.then_inc(s_gated, 1)

                def subtract_max(b, t):
                    n = b * W + t
                    pool.wait_ge(s_top8, it * TILES + n + 1)
                    pool.wait_ge(s_prob, it * TILES + n + 1)
                    nc.gpsimd.tensor_tensor(eS[:], S[:, t, :].rearrange("p (h n) -> p h n", h=H),
                                            top[:, :, 0:1].to_broadcast([P, H, LC]), ALU.subtract).then_inc(s_dif, 1)

                rstd_step(1, 0)
                round_qk(0)
                pool.wait_ge(s_g, it * 16 + 16)
                nc.gpsimd.tensor_tensor(gated_bias[:], gate[:], rows[:, 2:5, :], ALU.mult).then_inc(s_gated, 1)
                pool.wait_ge(s_gated, it * 4 + 1)
                add_bias(1, 0)
                gate_weight(w_so, 0, s_wso, KC)
                rstd_step(1, 1)
                add_bias(1, 1)
                rstd_step(2, 0)
                add_bias(2, 0)
                gate_weight(w_co, 1, s_wco, KC)
                round_qk(1)
                for t in range(W):
                    subtract_max(0, t)
                    if t == 0:
                        gate_weight(w_m2, 2, s_wm2, J)
                rstd_step(2, 1)
                add_bias(2, 1)
                rstd_step(3, 0)
                add_bias(3, 0)
                for t in range(W):
                    subtract_max(1, t)
                    if t == 0:
                        pool.wait_ge(s_kv1, it * 32 + 32)
                        hold(pool)
                        nc.gpsimd.tensor_scalar(kbd1r[:], kbd[:], 1.0, 0.0, ALU.mult, ALU.add).then_inc(s_kr, 1)
                rstd_step(4, 0)
                add_bias(4, 0)
                rstd_step(3, 1)
                add_bias(3, 1)
                round_q3(0)
                out_0 = out[bass.ds(it * L + SHIFT, BT), :].rearrange("(t p) n -> p t n", p=P)
                drained_wait(pool, ("y", 4, 0, 1), it)
                pool.dma_start(out_0, x[:, 0]).then_inc(s_store[0], 16)
                rstd_step(4, 1)
                add_bias(4, 1)
                round_q3(1)
                drained_wait(pool, ("y", 4, 1, 1), it)
                pool.dma_start(out[bass.ds(it * L + BT + SHIFT, BT - P), :].rearrange("(t p) n -> p t n", p=P),
                               x[:, 1, 0:W - 1, :]).then_inc(s_store[1], 16)
                pool.dma_start(out[bass.ds(it * L + L - P + SHIFT, P - SHIFT), :], x[0:P - SHIFT, 1, W - 1, :]).then_inc(s_store[1], 16)
                pool.dma_start(out[bass.ds(it * L, SHIFT), :], x[P - SHIFT:P, 1, W - 1, :]).then_inc(s_store[1], 16)
                own.restart()

        @block.scalar
        def _(act):
            own = Chain(act, s_act)
            act.wait_ge(s_early, 13 * 16)
            nc.scalar.activation(scondT, condT, ACT.Silu).then_inc(s_silu_c, 1)
            for a in range(2):
                if a == 1:
                    act.wait_ge(s_mod, 2)
                    for c in range(KC):
                        filled_wait(act, ("Tc", c), 0)
                        for b in range(B):
                            r = slice(b * LC, (b + 1) * LC)
                            i = nc.scalar.activation(modT[:, c, r], ps(("Tc", c))[:, r], ACT.Identity,
                                                     bias=mod[:, 0, XKV, c, b:b + 1], scale=mod[:, 1, XKV, c, b:b + 1])
                        drain(i, ("Tc", c))
                    act.wait_ge(s_keys, B)
                for c in range(KC):
                    filled_wait(act, ("kT", a, c), 0)
                    n = CB["k0" if a == 0 else "k1"] + c
                    drain(nc.scalar.activation(keysT[:, c, :], ps(("kT", a, c))[:, 0:B * LC], ACT.Identity,
                                               bias=chan[:, n:n + 1]), ("kT", a, c))
            with act.Fori(0, B) as it:
                def modulated(n, b):
                    for c in range(KC):
                        filled_wait(act, ("T", n, b, c), it)
                        m = MOD_OF[n]
                        drain(nc.scalar.activation(hT[:, c, :], ps(("T", n, b, c)), ACT.Identity,
                                                   bias=cur[:, 0, m, c:c + 1], scale=cur[:, 1, m, c:c + 1]), ("T", n, b, c))

                def biased(dst, key, n):
                    filled_wait(act, key, it)
                    drain(nc.scalar.activation(dst, ps(key), ACT.Identity, bias=chan[:, n:n + 1]), key)

                def project_qk(b):
                    for c in range(KC):
                        biased(qk[:, c, :], ("qk", b, c), CB["qk"] + c)
                    for c in range(KC):
                        biased(kT[:, c, :], ("qk", b, KC + c), CB["qk"] + KC + c)

                def project_q2(b):
                    filled_wait(act, ("q2", b, KC - 1), it)
                    for c in range(KC):
                        biased(q2T[:, c, :], ("q2", b, c), CB["q2"] + c)

                def self_denominator(b, w):
                    filled_wait(act, ("PV", b, w), it)
                    if w >= 2:
                        drained_wait(act, ("PV", b, w - 2), it)
                    r = rden[:, w % 2, 0:KC * P]
                    own.step(nc.scalar.activation(r, ps(("PV", b, w))[:, KC * P:], ACT.Ln))
                    own.wait()
                    nc.scalar.activation(r, r, ACT.Exp, scale=-1.0).then_inc(s_rd1, 1)

                def window(b, w):
                    key = ("mT", b, w)
                    filled_wait(act, key, it)
                    drain(nc.scalar.activation(mTs[:, w * P:(w + 1) * P], ps(key)[:, 0:P // 2].bitcast(BF16), ACT.Copy), key)
                    for g in range(4):
                        key = ("B", b, w, g)
                        filled_wait(act, key, it)
                        drain(nc.scalar.activation(pT_self[:, w % 2, 4 * g:4 * g + 4, :], ps(key).rearrange("p (h q) -> p h q", h=4),
                                                   ACT.Exp, scale=SCORE_SCALE), key)
                    if w:
                        self_denominator(b, w - 1)

                def topk_exp(b, t):
                    act.wait_ge(s_dif, it * TILES + b * W + t + 1)
                    nc.scalar.activation(eS[:], eS[:], ACT.Exp, scale=SCORE_SCALE).then_inc(s_exp, 1)

                def take_scores(b):
                    for t in range(W):
                        for c in range(KC):
                            key = ("S", b, t, c)
                            filled_wait(act, key, it)
                            drain(nc.scalar.activation(S[:, t, c * BT:(c + 1) * BT], ps(key), ACT.Copy), key)

                def take_probs(b):
                    for t in range(W):
                        for c in range(KC):
                            key = ("TP", b, t, c)
                            filled_wait(act, key, it)
                            drain(nc.scalar.activation(pT_cross[:, 4 * c:4 * c + 4, t * P:(t + 1) * P],
                                                       ps(key).rearrange("p (h q) -> p h q", h=4), ACT.Copy), key)

                def cross_denominator(n, b):
                    for c in range(KC):
                        key = ("D", n, b, c)
                        filled_wait(act, key, it)
                        drain(nc.scalar.activation(rden[:, c, :], ps(key), ACT.Ln), key)
                        drained_wait(act, key, it)
                        nc.scalar.activation(rden[:, c, :], rden[:, c, :], ACT.Exp, scale=-1.0).then_inc(s_rd, 1)

                def silu(b, j):
                    if j >= 2:
                        drained_wait(act, ("ub", b, j - 2), it)
                    key = ("ua", b, j)
                    filled_wait(act, key, it)
                    drain(nc.scalar.activation(sa[:, j % 2, :], ps(key), ACT.Silu, bias=chan[:, CB["m1"] + j:CB["m1"] + j + 1]), key)

                def last_cross(b):
                    modulated(4, b)
                    for c in range(KC):
                        biased(qk[:, c, :], ("q3", b, c), CB["q3"] + c)
                    key = ("mT3", b)
                    filled_wait(act, key, it)
                    drain(nc.scalar.activation(mTs[:], ps(key)[:, 0:BT // 2].bitcast(BF16), ACT.Copy), key)
                    for p in range(PAIRS):
                        key = ("B3", b, p)
                        filled_wait(act, key, it)
                        drain(nc.scalar.activation(pT_cross[:, p, :], ps(key), ACT.Exp, scale=SCORE_SCALE), key)
                    cross_denominator(4, b)

                act.wait_ge(s_cur, it + 1)
                modulated(1, 0)
                project_qk(0)
                for w in range(W):
                    window(0, w)
                self_denominator(0, W - 1)
                modulated(1, 1)
                project_qk(1)
                modulated(2, 0)
                project_q2(0)
                take_scores(0)
                for w in range(W):
                    window(1, w)
                    topk_exp(0, w)
                self_denominator(1, W - 1)
                take_probs(0)
                cross_denominator(2, 0)
                modulated(2, 1)
                project_q2(1)
                take_scores(1)
                modulated(3, 0)
                for j in range(J):
                    silu(0, j)
                    if j % W == W - 2:
                        topk_exp(1, j // W)
                topk_exp(1, 2)
                topk_exp(1, 3)
                take_probs(1)
                cross_denominator(2, 1)
                last_cross(0)
                modulated(3, 1)
                for j in range(J):
                    silu(1, j)
                last_cross(1)
                own.restart()

        @block.vector
        def _(dve):
            own = Chain(dve, s_dve)

            def moments(src, n):
                for t in range(n):
                    i = nc.vector.bn_stats(stats[:, t, :], src[:, t, :])
                own.step(i)
                own.wait()
                for t in range(n):
                    i = nc.vector.bn_aggr(mv[:, t, :], stats[:, t, :])
                i.then_inc(s_mv, 1)

            def normalise(src, n):
                for t in range(n):
                    nc.vector.tensor_scalar(xh[:, t, :], src[:, t, :], mv[:, t, 0:1], rstd[:, t:t + 1],
                                            ALU.subtract, ALU.mult).then_inc(s_xh, 1)

            dve.sem_inc(s_prob, 1)
            nc.vector.memset(vpad[:], 0.0)
            nc.vector.memset(mst[:], 0.0)
            dve.wait_ge(s_early, 13 * 16)
            moments(ctx_rows, B // 2)

            def double_context(src):
                for k in range(KC):
                    i = nc.vector.tensor_copy(src2[:, k], src[:, k, :].rearrange("p (b n) -> p b n", b=B)
                                              .unsqueeze(2).to_broadcast([P, B, 2, LC]))
                i.then_inc(s_src2, 1)

            double_context(srcT)
            dve.wait_ge(s_rstd, 1)
            normalise(ctx_rows, B // 2)
            dve.wait_ge(s_consts, 5 * 16)
            nc.vector.tensor_copy(identb[:], ident[:])
            nc.vector.tensor_copy(head_rows[:].rearrange("p h n -> p (h n)"), head_rows_f).then_inc(s_const_ready, 1)
            filled_wait(dve, ("mod",), 0)
            half = NMOD * KC
            for s in range(2):
                bias = chan[:, s * half:(s + 1) * half].unsqueeze(2).to_broadcast([P, half, B])
                i = nc.vector.scalar_tensor_tensor(
                    mod[:, s].rearrange("p m c b -> p (m c) b"),
                    ps(("mod",))[:, s * half * B:(s + 1) * half * B].rearrange("p (m b) -> p m b", b=B),
                    float(s), bias, ALU.add, ALU.add)
                i.then_inc(s_mod, 1)
            dve.wait_ge(s_mod, 2)
            dve.sem_inc(drained[PLACE[("mod",)][0]], 1)
            for i in range(2):
                filled_wait(dve, ("gate", i), 0)
                n = (2 - i) * C
                own.step(nc.vector.tensor_tensor(gate_out[:, i * 2 * C:i * 2 * C + n], ps(("gate", i))[0:B, 0:n],
                                                 gate_in[:, i * 2 * C:i * 2 * C + n], ALU.add))
                own.wait()
                dve.sem_inc(drained[PLACE[("gate", i)][0]], 1)
                dve.sem_inc(s_gate, 1)
            for a in range(2):
                if a == 1:
                    drained_wait(dve, ("Tc", 1), 0)
                    double_context(modT)
                    dve.wait_ge(s_keys_stored, B * 16)
                for c in range(KC):
                    drained_wait(dve, ("kT", a, c), 0)
                for b in range(B):
                    for c in range(KC):
                        i = nc.vector.tensor_tensor(
                            keys_out[b][:, c, :].rearrange("p (h n) -> p h n", h=HPC),
                            keysT[:, c, b * LC:(b + 1) * LC].unsqueeze(1).to_broadcast([P, HPC, LC]),
                            head_mask[:].unsqueeze(2).to_broadcast([P, HPC, LC]), ALU.mult)
                    i.then_inc(s_keys, 1)
                for u in range(B // 2):
                    key = ("vc", a, u)
                    filled_wait(dve, key, 0)
                    v = v_out[:, a, 2 * u:2 * u + 2, :]
                    drain(nc.vector.tensor_tensor(v, ps(key).rearrange("p (b n) -> p b n", b=2),
                                                  vrow[a].unsqueeze(1).to_broadcast([P, 2, C]), ALU.add), key)
                    drained_wait(dve, key, 0)
                    v = v.rearrange("p b (h n) -> p (b h) n", n=2 * D)
                    nc.vector.tensor_tensor(v, v, pair_mask[:].unsqueeze(1).to_broadcast([P, 2 * PAIRS, 2 * D]),
                                            ALU.mult).then_inc(s_vals, 1)
            nc.vector.memset(bd[:, 1], 0.0).then_inc(s_zero, 1)
            own.restart()
            with dve.Fori(0, B) as it:
                def layer_norm(n, b):
                    k = LN[n, b]
                    if n == 1:
                        src = xin[:]
                        dve.wait_ge(s_xin, it * 64 + (64 if b else 16))
                    else:
                        src = x[:, b]
                        drained_wait(dve, ("y", n - 1, b, 1), it)
                    moments(src, W)
                    dve.wait_ge(s_rstd, it * NLN + k + 2)
                    if k:
                        filled_wait(dve, ("T", *ORDER[k - 1], 1), it)
                    normalise(src, W)

                def take_values(b):
                    for u in range(2):
                        key = ("v", b, u)
                        filled_wait(dve, key, it)
                        for i in range(2):
                            dst = vpad[:, 2 * u + i].rearrange("p h (s n) -> p h s n", n=D)[:, :, 0:4:3, :]
                            ins = nc.vector.tensor_tensor(
                                dst, ps(key)[:, i * C:(i + 1) * C].rearrange("p (h s n) -> p h s n", s=2, n=D),
                                rows[:, 0, :].rearrange("p (h s n) -> p h s n", s=2, n=D), ALU.add)
                        drain(ins, key)

                def split_max(slot, done):
                    own.step(nc.vector.tensor_copy(mst[:, slot, 0:H], negm[:, slot]))
                    own.wait()
                    nc.vector.tensor_tensor(mst[:, slot, H:2 * H], negm[:, slot], mst[:, slot, 0:H], ALU.subtract).then_inc(done, 1)

                def window_max(b, w):
                    for g in range(4):
                        key = ("A", b, w, g)
                        filled_wait(dve, key, it)
                        drain(nc.vector.tensor_reduce(negm[:, w, 4 * g:4 * g + 4], ps(key).rearrange("p (h n) -> p h n", h=4),
                                                      AX_X, ALU.max, negate=True), key)
                    drained_wait(dve, ("A", b, w, 3), it)
                    split_max(w, s_mst)

                def window_divide(b, w):
                    key = ("PV", b, w)
                    dve.wait_ge(s_rd1, (it * BLKS + b) * W + w + 1)
                    drain(nc.vector.tensor_tensor(oT[:, :, w * P:(w + 1) * P], ps(key)[:, 0:KC * P].rearrange("p (c n) -> p c n", c=KC),
                                                  rden[:, w % 2, 0:KC * P].rearrange("p (c n) -> p c n", c=KC), ALU.mult), key)

                def cross_divide(n, b):
                    for c in range(KC):
                        key = ("O", n, b, c)
                        filled_wait(dve, key, it)
                        dve.wait_ge(s_rd, (it * 4 + {(2, 0): 0, (2, 1): 1, (4, 0): 2, (4, 1): 3}[n, b]) * KC + c + 1)
                        drain(nc.vector.tensor_tensor(oT[:, c, :], ps(key), rden[:, c, :], ALU.mult), key)

                def residual(n, b):
                    dve.wait_ge(s_xb, it * NLN + LN[n, b] + 2)
                    for u in range(2):
                        key = ("y", n, b, u)
                        filled_wait(dve, key, it)
                        v = x[:, b, 2 * u:2 * u + 2, :]
                        drain(nc.vector.tensor_tensor(v, ps(key).rearrange("p (t n) -> p t n", t=2), v, ALU.add), key)

                def topk_step(b, t, s):
                    Sh = S[:, t, :].rearrange("p (h n) -> p h n", h=H)
                    if s == 0:
                        drained_wait(dve, ("S", b, t, KC - 1), it)
                    elif s == 1:
                        dve.wait_ge(s_top8, it * TILES + b * W + t + 1)
                    if s:
                        own.wait()
                    hold(dve)
                    for h in range(H):
                        eight = top[:, h, 0:8] if s < 2 else top[:, h, 8:16]
                        src = Sh[:, h, :] if s < 2 else left[:, h, :]
                        if s % 2 == 0:
                            i = nc.vector.max(eight, src)
                        else:
                            i = nc.vector.match_replace(left[:, h, :], eight, src, REPLACED)
                    if s == 0:
                        i.then_inc(s_top8, 1)
                    else:
                        own.step(i)
                    if s == 3:
                        own.wait()
                        dve.wait_ge(s_exp, it * TILES + b * W + t + 1)
                        nc.vector.scalar_tensor_tensor(Sh, left[:], REPLACED, eS[:], ALU.is_equal, ALU.mult).then_inc(s_prob, 1)

                def gated_linear(b, j):
                    drained_wait(dve, ("ua", b, j), it)
                    key = ("ub", b, j)
                    filled_wait(dve, key, it)
                    n = CB["m1"] + J + j
                    drain(nc.vector.scalar_tensor_tensor(hid[:, j, :], ps(key), chan[:, n:n + 1], sa[:, j % 2, :],
                                                         ALU.add, ALU.mult), key)

                def last_cross(b):
                    for t in range(W):
                        for c in range(KC):
                            key = ("A3", b, t, c)
                            filled_wait(dve, key, it)
                            drain(nc.vector.tensor_reduce(negm[:, t, HPC * c:HPC * (c + 1)], ps(key).rearrange("p (h n) -> p h n", h=HPC),
                                                          AX_X, ALU.max, negate=True), key)
                        drained_wait(dve, ("A3", b, t, KC - 1), it)
                        split_max(t, s_mst3)
                    cross_divide(4, b)
                    residual(4, b)

                nc.vector.tensor_copy(cur[:].rearrange("p s m c -> p (s m c)").unsqueeze(2),
                                      mod[:].rearrange("p s m c b -> p (s m c) b")[:, :, bass.ds(it, 1)]).then_inc(s_cur, 1)
                layer_norm(1, 0)
                take_values(0)
                window_max(0, 0)
                for w in range(W):
                    if w + 1 < W:
                        window_max(0, w + 1)
                    if w:
                        window_divide(0, w - 1)
                    if w == 2:
                        layer_norm(1, 1)
                window_divide(0, W - 1)
                residual(1, 0)
                layer_norm(2, 0)
                take_values(1)
                window_max(1, 0)
                for w in range(W):
                    if w + 1 < W:
                        window_max(1, w + 1)
                    if w:
                        window_divide(1, w - 1)
                    for s in range(4):
                        topk_step(0, w, s)
                window_divide(1, W - 1)
                residual(1, 1)
                layer_norm(2, 1)
                cross_divide(2, 0)
                residual(2, 0)
                layer_norm(3, 0)
                for j in range(J):
                    topk_step(1, j // 4, j % 4)
                    gated_linear(0, j)
                for j in range(J, 4 * W):
                    topk_step(1, j // 4, j % 4)
                residual(3, 0)
                layer_norm(4, 0)
                cross_divide(2, 1)
                residual(2, 1)
                layer_norm(3, 1)
                last_cross(0)
                for j in range(J):
                    gated_linear(1, j)
                residual(3, 1)
                layer_norm(4, 1)
                last_cross(1)
                own.restart()

        @block.tensor
        def _(pe):
            def mm(dst, lhsT, rhs, start, stop):
                return nc.tensor.matmul(dst, lhsT, rhs, start=start, stop=stop)

            def channels(key, dst, weights, rhs, it):
                fill_wait(pe, key, it)
                for k in range(KC):
                    i = mm(dst, weights(k), rhs(k), k == 0, k == KC - 1)
                return i

            pe.wait_ge(s_early, 13 * 16)
            pe.wait_ge(s_silu_c, 1)
            for s in range(2):
                for m in range(NMOD):
                    for c in range(KC):
                        if m <= MLP:
                            w, col = w_ada, (3 * m + s) * C + c * P
                        else:
                            w, col = w_ss[m - XQ], (1 - s) * C + c * P
                        at = ((s * NMOD + m) * KC + c) * B
                        for k in range(KC):
                            i = mm(ps(("mod",))[:, at:at + B], w[:, k, col:col + P], scondT[:, k, :], k == 0, k == KC - 1)
            fill(i, ("mod",))
            for i_ in range(2):
                for m in ((MSA, MCA), (MLP,))[i_]:
                    at = (m - 2 * i_) * C
                    for k in range(KC):
                        i = mm(ps(("gate", i_))[0:B, at:at + C], scondT[:, k, :], w_ada[:, k, (3 * m + 2) * C:(3 * m + 3) * C],
                               k == 0, k == KC - 1)
                fill(i, ("gate", i_))
            for a in range(2):
                if a == 1:
                    pe.wait_ge(s_xh, B // 2)
                    pe.wait_ge(s_const_ready, 1)
                    for c in range(KC):
                        fill_wait(pe, ("Tc", c), 0)
                        for t in range(B // 2):
                            i = nc.tensor.transpose(ps(("Tc", c))[:, t * P:(t + 1) * P], xh[:, t, c * P:(c + 1) * P], ident[:])
                        fill(i, ("Tc", c))
                    for c in range(KC):
                        drained_wait(pe, ("Tc", c), 0)
                src = (srcT, modT)[a]
                for c in range(KC):
                    key = ("kT", a, c)
                    fill(channels(key, ps(key)[:, 0:B * LC], lambda k: w_kv[a][:, k, c * P:(c + 1) * P],
                                  lambda k: src[:, k, :], 0), key)
                pe.wait_ge(s_src2, a + 1)
                for u in range(B // 2):
                    key = ("vc", a, u)
                    for i_ in range(2):
                        i = channels(key, ps(key)[:, i_ * C:(i_ + 1) * C],
                                     lambda k: src2[:, k, 2 * u + i_].rearrange("p d n -> p (d n)"),
                                     lambda k: w_kv[a][:, k, C:2 * C], 0)
                    fill(i, key)
            pe.wait_ge(s_weights, 5 * 16)
            with pe.Fori(0, B) as it:
                def transposed(n, b):
                    for c in range(KC):
                        key = ("T", n, b, c)
                        fill_wait(pe, key, it)
                        for t in range(W):
                            if c == 0:
                                pe.wait_ge(s_xh, (it * NLN + LN[n, b]) * W + t + 3)
                            i = nc.tensor.transpose(ps(key)[:, t * P:(t + 1) * P], xh[:, t, c * P:(c + 1) * P], ident[:])
                        fill(i, key)
                    drained_wait(pe, ("T", n, b, KC - 1), it)

                def heads_in(b):
                    transposed(1, b)
                    for i_ in range(2 * KC):
                        key = ("qk", b, i_)
                        fill(channels(key, ps(key), lambda k: w_qkv[:, k, i_ * P:(i_ + 1) * P], lambda k: hT[:, k, :], it), key)
                    for u in range(2):
                        key = ("v", b, u)
                        for i_ in range(2):
                            t = 2 * u + i_
                            i = channels(key, ps(key)[:, i_ * C:(i_ + 1) * C], lambda k: hT[:, k, t * P:(t + 1) * P],
                                         lambda k: w_qkv[:, k, 2 * C:3 * C], it)
                        fill(i, key)

                def scores_for_max(b, w):
                    pe.wait_ge(s_bd[w % 2], ((it * BLKS + b) * 2 + w // 2) * HPC * 16 + HPC * 16)
                    for g in range(4):
                        key = ("A", b, w, g)
                        fill_wait(pe, key, it)
                        c, h = g // 2, (g % 2) * 4
                        fill(mm(ps(key), qr[:, c, w * P:(w + 1) * P], bd[:, w % 2, h:h + 4, KC + c, :].bitcast(F32R), True, True), key)

                def scores_minus_max(b, w):
                    key = ("mT", b, w)
                    fill_wait(pe, key, it)
                    pe.wait_ge(s_mst, (it * BLKS + b) * W + w + 1)
                    fill(nc.tensor.transpose(ps(key)[:, 0:P // 2].bitcast(BF16), mst[:, w, :], identb[:]), key)
                    for g in range(4):
                        key = ("B", b, w, g)
                        fill_wait(pe, key, it)
                        c, h = g // 2, (g % 2) * 4
                        mm(ps(key), kT[:, c, w * P:(w + 1) * P], bd[:, w % 2, h:h + 4, c, :], True, False)
                        if g == 0:
                            drained_wait(pe, ("mT", b, w), it)
                        for i_ in range(4):
                            i = mm(ps(key)[:, i_ * P:(i_ + 1) * P], head_rows[:, 4 * g + i_, :], mTs[:, w * P:(w + 1) * P],
                                   False, i_ == 3)
                        fill(i, key)

                def window_values(b, w):
                    key = ("PV", b, w)
                    fill_wait(pe, key, it)
                    drained_wait(pe, ("B", b, w, 3), it)
                    for c in range(KC):
                        for s in range(2):
                            for p in range(4):
                                i = mm(ps(key)[32 * p:32 * p + 32, c * P:(c + 1) * P], vpad[:, w, 4 * c + p, 2 * D * s:2 * D * (s + 1)],
                                       pT_self[:, w % 2, HPC * c + 2 * p + s, :], s == 0, s == 1)
                    for c in range(KC):
                        for s in range(2):
                            for p in range(4):
                                i = mm(ps(key)[32 * p:32 * p + 32, (KC + c) * P:(KC + c + 1) * P], ones_half[:, s, :],
                                       pT_self[:, w % 2, HPC * c + 2 * p + s, :], s == 0, s == 1)
                    fill(i, key)

                def project(n, b):
                    w, src, chunks = {1: (w_so, oT, KC), 2: (w_co, oT, KC), 3: (w_m2, hid, J), 4: (w_p, oT, KC)}[n]
                    if n <= 3:
                        pe.wait_ge(s_gated, it * 4 + n + 1)
                    if n == 1:
                        drained_wait(pe, ("PV", b, W - 1), it)
                    elif n == 3:
                        drained_wait(pe, ("ub", b, J - 1), it)
                    else:
                        drained_wait(pe, ("O", n, b, KC - 1), it)
                    for u in range(2):
                        key = ("y", n, b, u)
                        fill_wait(pe, key, it)
                        for i_ in range(2):
                            t = 2 * u + i_
                            for k in range(chunks):
                                i = mm(ps(key)[:, i_ * C:(i_ + 1) * C], src[:, k, t * P:(t + 1) * P], w[:, k, :],
                                       k == 0, k == chunks - 1)
                        fill(i, key)

                def windows(b):
                    drained_wait(pe, ("v", b, 1), it)
                    scores_for_max(b, 0)
                    for w in range(W):
                        if w + 1 < W:
                            scores_for_max(b, w + 1)
                        scores_minus_max(b, w)
                        if w:
                            window_values(b, w - 1)
                    window_values(b, W - 1)
                    project(1, b)

                def cross_in(b):
                    transposed(2, b)
                    for c in range(KC):
                        key = ("q2", b, c)
                        fill(channels(key, ps(key), lambda k: w_q2[:, k, c * P:(c + 1) * P], lambda k: hT[:, k, :], it), key)

                def scores(b):
                    if b == 0:
                        pe.wait_ge(s_kv0, it * 32 + 32)
                    drained_wait(pe, ("q2", b, KC - 1), it)
                    for t in range(W):
                        for c in range(KC):
                            key = ("S", b, t, c)
                            fill_wait(pe, key, it)
                            fill(mm(ps(key), q2T[:, c, t * P:(t + 1) * P], kbd[:, c, :], True, True), key)

                def values(n, b):
                    vals = vbd0 if n == 2 else vbd1
                    for c in range(KC):
                        key = ("D", n, b, c)
                        fill_wait(pe, key, it)
                        for p in range(4):
                            i = mm(ps(key)[32 * p:32 * p + 32, :], pair_mask[:], pT_cross[:, 4 * c + p, :], True, True)
                        fill(i, key)
                        key = ("O", n, b, c)
                        fill_wait(pe, key, it)
                        for p in range(4):
                            i = mm(ps(key)[32 * p:32 * p + 32, :], vals[:, 4 * c + p, :], pT_cross[:, 4 * c + p, :], True, True)
                        fill(i, key)

                def weigh(b):
                    for t in range(W):
                        pe.wait_ge(s_prob, it * TILES + b * W + t + 2)
                        for c in range(KC):
                            key = ("TP", b, t, c)
                            fill_wait(pe, key, it)
                            for p in range(4):
                                at = (4 * c + p) * P
                                i = nc.tensor.transpose(ps(key)[:, p * P:(p + 1) * P], S[:, t, at:at + P], ident[:])
                            fill(i, key)
                    drained_wait(pe, ("TP", b, W - 1, KC - 1), it)
                    values(2, b)

                def mlp(b):
                    transposed(3, b)
                    for j in range(J):
                        for name, at in (("ua", 0), ("ub", HID)):
                            key = (name, b, j)
                            fill(channels(key, ps(key), lambda k: w_m1[:, k, at + j * P:at + (j + 1) * P],
                                          lambda k: hT[:, k, :], it), key)
                    project(3, b)

                def last(b):
                    transposed(4, b)
                    for c in range(KC):
                        key = ("q3", b, c)
                        fill(channels(key, ps(key), lambda k: w_q3[:, k, c * P:(c + 1) * P], lambda k: hT[:, k, :], it), key)
                    pe.wait_ge(s_kr, it + 1)
                    pe.wait_ge(s_q3r, (it * BLKS + b) * KC + KC)
                    for t in range(W):
                        for c in range(KC):
                            key = ("A3", b, t, c)
                            fill_wait(pe, key, it)
                            fill(mm(ps(key), qr[:, c, t * P:(t + 1) * P], kbd1r[:, c, :], True, True), key)

                    def pair_rows(p):
                        at = 2 * p * P + P - LC
                        return head_rows[:].rearrange("p h n -> p (h n)")[:, at:at + 2 * LC]

                    def products(p):
                        key = ("B3", b, p)
                        fill_wait(pe, key, it)
                        c = p // 4
                        mm(ps(key), kbd[:, c, (p % 4) * P:(p % 4 + 1) * P], qk[:, c, :], True, False)

                    def minus_max(p):
                        fill(mm(ps(("B3", b, p)), pair_rows(p), mTs[:], False, True), ("B3", b, p))

                    for p in range(3):
                        products(p)
                    key = ("mT3", b)
                    fill_wait(pe, key, it)
                    for t in range(W):
                        pe.wait_ge(s_mst3, (it * BLKS + b) * W + t + 1)
                        i = nc.tensor.transpose(ps(key)[:, t * P // 2:(t + 1) * P // 2].bitcast(BF16), mst[:, t, :], identb[:])
                    fill(i, key)
                    drained_wait(pe, key, it)
                    for p in range(3):
                        minus_max(p)
                    for p in range(3, PAIRS):
                        products(p)
                        minus_max(p)
                    drained_wait(pe, ("B3", b, PAIRS - 1), it)
                    values(4, b)
                    project(4, b)

                heads_in(0)
                windows(0)
                heads_in(1)
                cross_in(0)
                scores(0)
                windows(1)
                weigh(0)
                cross_in(1)
                project(2, 0)
                scores(1)
                mlp(0)
                weigh(1)
                project(2, 1)
                last(0)
                mlp(1)
                last(1)


def kernel(**inputs):
    import numpy as np
    import concourse.bacc as bacc
    from concourse.bass_utils import run_bass_kernel_spmd

    def arr(name):
        return np.ascontiguousarray(inputs[name])

    def cols(v):
        return v.reshape(-1, P).T

    a, b = "L0_xcond_", "L1_xcond_"
    ada = arr(a + "b_ada").reshape(3, 3, C)
    ssq, sskv = arr(b + "bss_q").reshape(2, C), arr(b + "bss_kv").reshape(2, C)
    bqkv, bkv, bkv1 = arr(a + "b_qkv"), arr(a + "b_kv"), arr(b + "bkv")
    chan = np.concatenate([
        cols(np.concatenate([ada[0, 0], ada[1, 0], ada[2, 0], ssq[1], sskv[1]])),
        cols(np.concatenate([ada[0, 1], ada[1, 1], ada[2, 1], ssq[0], sskv[0]])),
        cols(bqkv[:2 * C]), cols(arr(a + "b_q")), cols(bkv[:C]), cols(arr(a + "b_m1")), cols(arr(b + "bq")), cols(bkv1[:C])], axis=1)
    rows = np.concatenate([bqkv[2 * C:], arr(b + "bp"), arr(a + "b_so"), arr(a + "b_co"), arr(a + "b_m2"), bkv[C:], bkv1[C:]])[None, :]
    ctx = arr("ctx_1024").reshape(B * LC, C)
    r, one = np.arange(P), np.float32(1)
    head = np.arange(H)
    head_rows = np.zeros((P, H, P), np.float32)
    head_rows[:2 * H] = ((r[:2 * H] % H)[:, None] == head[None, :])[:, :, None]
    arrays = {
        "x": arr("x").reshape(B * L, C),
        "condT": arr("cond_1024").T.reshape(KC, P, B).transpose(1, 0, 2),
        "ctxT": ctx.T.reshape(KC, P, B * LC).transpose(1, 0, 2),
        "ctx_rows": ctx.reshape(B // 2, P, C).transpose(1, 0, 2),
        "chan": chan, "gate_bias": ada[:, 2].reshape(1, 3 * C), "rows": rows,
        "ident": np.eye(P, dtype=np.float32),
        "head_rows": head_rows.reshape(P, H * P),
        "head_mask": (r[:, None] // D == np.arange(HPC)[None, :]).astype(np.float32),
        "pair_mask": (r[:, None] // LC == np.arange(2 * D)[None, :] // D).astype(np.float32),
        "ones_half": np.repeat(np.eye(2, dtype=np.float32), D, axis=1).reshape(1, 4 * D).repeat(P, axis=0),
    }
    for n in ("w_ada", "w_qkv", "w_so", "w_q", "w_kv", "w_co", "w_m1", "w_m2"):
        arrays[n] = arr(a + n)
    for n in ("Wq", "Wkv", "Wp", "Wss_q", "Wss_kv"):
        arrays[n] = arr(b + n)
    arrays = {"in_" + k: np.ascontiguousarray(v) for k, v in arrays.items()}

    nc = bacc.Bacc("TRN2", target_bir_lowering=False, num_devices=1)
    t_in = {k[3:]: nc.dram_tensor(k, v.shape, mybir.dt.from_np(v.dtype), kind="ExternalInput").ap() for k, v in arrays.items()}
    out = nc.dram_tensor("out", [B * L, C], F32, kind="ExternalOutput").ap()
    build(nc, t_in, out)
    res = run_bass_kernel_spmd(nc, [arrays], core_ids=[0])
    return res.results[0]["out"].reshape(B, L, C)
```

```python
from contextlib import ExitStack

import concourse.bass as bass
from concourse import mybir

F32 = mybir.dt.float32
F32R = mybir.dt.float32r
BF16 = mybir.dt.bfloat16
ALU = mybir.AluOpType
ACT = mybir.ActivationFunctionType
AX_X = mybir.AxisListType.X

P = 128
B, L, C = 4, 1024, 256
LC = 64
H, D = 16, 16
SHIFT = 64
HID = 1024
TOPK = 16
KC = C // P
HPC = P // D
PAIRS = H // 2
W = 4
BT = W * P
BLKS = L // BT
J = HID // P
SCORE_SCALE = 1.0 / D ** 0.5
REPLACED = -3.0e38
EPS0, EPS1 = 1e-6, 1e-5

MSA, MCA, MLP, XQ, XKV = range(5)
NMOD = 5

CB = {}
_at = 0
for _name, _n in (("shift", NMOD * KC), ("scale", NMOD * KC), ("qk", 2 * KC), ("q2", KC), ("k0", KC),
                  ("m1", 2 * J), ("q3", KC), ("k1", KC)):
    CB[_name] = _at
    _at += _n
NCB = _at
ROWS = ("v_self", "p", "so", "co", "m2", "v0", "v1")


def before_loop():
    yield ("mod",)
    for i in range(2):
        yield ("gate", i)
    for a in range(2):
        if a == 1:
            for c in range(KC):
                yield ("Tc", c)
        for c in range(KC):
            yield ("kT", a, c)
        for u in range(B // 2):
            yield ("vc", a, u)


def in_loop():
    def transposed(n, b):
        for c in range(KC):
            yield ("T", n, b, c)

    def qk_in(b):
        yield from transposed(1, b)
        for i in range(2 * KC):
            yield ("qk", b, i)

    def v_in(b):
        for u in range(2):
            yield ("v", b, u)

    def heads_in(b):
        yield from qk_in(b)
        yield from v_in(b)

    def windows(b):
        for g in range(4):
            yield ("A", b, 0, g)
        for w in range(W):
            if w + 1 < W:
                for g in range(4):
                    yield ("A", b, w + 1, g)
            yield ("mT", b, w)
            for g in range(4):
                yield ("B", b, w, g)
            if w:
                yield ("PV", b, w - 1)
        yield ("PV", b, W - 1)
        for u in range(2):
            yield ("y", 1, b, u)

    def cross_in(b):
        yield from transposed(2, b)
        for c in range(KC):
            yield ("q2", b, c)

    def scores(b, tiles):
        for t in tiles:
            for c in range(KC):
                yield ("S", b, t, c)

    def weigh(b):
        for t in range(W):
            for c in range(KC):
                yield ("TP", b, t, c)
        yield from values(2, b)

    def values(n, b):
        for c in range(KC):
            yield ("D", n, b, c)
            yield ("O", n, b, c)

    def project(n, b):
        for u in range(2):
            yield ("y", n, b, u)

    def mlp(b):
        yield from transposed(3, b)
        for j in range(J):
            yield ("ua", b, j)
            yield ("ub", b, j)
        yield from project(3, b)

    def last_in(b):
        yield from transposed(4, b)
        for c in range(KC):
            yield ("q3", b, c)
        for t in range(W):
            for c in range(KC):
                yield ("A3", b, t, c)

    def last_scores(b):
        for p in range(PAIRS):
            yield ("B3", b, p)
            if p == 2:
                yield ("mT3", b)

    yield from windows(0)
    yield from heads_in(1)
    yield from cross_in(0)
    yield from scores(0, range(W))
    yield from windows(1)
    yield from cross_in(1)
    yield from weigh(0)
    yield from scores(1, range(0, 2))
    yield from project(2, 0)
    yield from scores(1, range(2, W))
    yield from mlp(0)
    yield from weigh(1)
    yield from project(2, 1)
    yield from last_in(0)
    yield from last_scores(0)
    yield from mlp(1)
    yield from values(4, 0)
    yield from project(4, 0)
    yield from last_in(1)
    yield from qk_in(0)
    yield from last_scores(1)
    yield from values(4, 1)
    yield from v_in(0)
    yield from project(4, 1)


NB = 8
LOOP = list(in_loop())
TAIL = LOOP[LOOP.index(("T", 1, 0, 0)):]
AHEAD = {key for key in TAIL if key[:3] == ("T", 1, 0) or key[:2] in (("qk", 0), ("v", 0))}
PRE = list(before_loop())
PRE += [("skip", n) for n in range((len(LOOP) - len(TAIL) - len(PRE)) % NB)]
SKIPPED = [key for key in PRE if key[0] == "skip"]
PRE_USES = [len((PRE + TAIL)[n::NB]) for n in range(NB)]
ROUNDS = [len(LOOP[n::NB]) for n in range(NB)]
PLACE = {key: (n % NB, n // NB) for n, key in enumerate(PRE)}
PLACE.update({key: (n % NB, PRE_USES[n % NB] + n // NB) for n, key in enumerate(LOOP)})
assert len(PLACE) == len(PRE) + len(LOOP)
assert all(PLACE[key][1] - ROUNDS[PLACE[key][0]] == (len(PRE) + n) // NB and PLACE[key][0] == (len(PRE) + n) % NB
           for n, key in enumerate(TAIL))


class Chain:

    def __init__(self, eng, sem):
        self.eng, self.sem, self.n = eng, sem, 0

    def step(self, instruction):
        self.n += 1
        instruction.then_inc(self.sem, 1)

    def wait(self):
        self.eng.wait_ge(self.sem, self.n)

    def restart(self):
        self.eng.wait_ge(self.sem, self.n)
        self.eng.sem_clear(self.sem)
        self.n = 0


def build(nc, t_in, out):
    ctx = ExitStack()
    with ctx:
        def sb(name, shape, dt=F32):
            return ctx.enter_context(nc.sbuf_tensor(name, shape, dt))

        def sem(name):
            return ctx.enter_context(nc.semaphore(name))

        gate_d = nc.dram_tensor("gate_rows", [B, 3 * C], F32, kind="Internal").ap()
        kbd_d = nc.dram_tensor("keys_by_head", [2, B, P, KC * HPC * LC], F32, kind="Internal").ap()
        vbd_d = nc.dram_tensor("values_by_pair", [2, B, P, C], F32, kind="Internal").ap()

        w_qkv = sb("w_qkv", [P, KC, 3 * C])
        w_q2 = sb("w_q2", [P, KC, C])
        w_m1 = sb("w_m1", [P, KC, 2 * HID])
        w_q3 = sb("w_q3", [P, KC, C])
        w_p = sb("w_p", [P, KC, C])
        w_so = sb("w_so", [P, KC, C])
        w_co = sb("w_co", [P, KC, C])
        w_m2 = sb("w_m2", [P, J, C])
        chan = sb("chan", [P, NCB])
        rows = sb("rows", [P, 5, C])
        gate = sb("gate", [P, 3, C])
        gated_bias = sb("gated_bias", [P, 3, C])
        mod = sb("mod", [P, 2, NMOD, KC, B])
        cur = sb("cur", [P, 2, NMOD, KC])
        cur_msa = sb("cur_msa", [P, 2, KC])
        ident = sb("ident", [P, P])
        identb = sb("identb", [P, P], BF16)
        head_rows = sb("head_rows", [P, H, P], BF16)
        head_mask = sb("head_mask", [P, HPC])
        pair_mask = sb("pair_mask", [P, 2 * D])
        ones_half = sb("ones_half", [P, 2, 2 * D])
        minus_half = sb("minus_half", [P, W])
        xin = sb("xin", [P, W, C])
        x = sb("x", [P, BLKS, W, C])
        xh = sb("xh", [P, W, C])
        hT = sb("hT", [P, KC, BT])
        qk = sb("qk", [P, 2 * KC, BT])
        qr = sb("qr", [P, KC, BT], F32R)
        q_by_head = sb("q_by_head", [P, 2, HPC, KC, P])
        k_by_head = sb("k_by_head", [P, 2, KC, HPC, P], F32R)
        vpad = sb("vpad", [P, W, PAIRS, 4 * D])
        arena = sb("arena", [P, 12288])
        oT = sb("oT", [P, KC, BT])
        stats = sb("stats", [P, W, 6])
        mv = sb("mv", [P, W, 2])
        veps = sb("veps", [P, W])
        rstd = sb("rstd", [P, W])
        negm = sb("negm", [P, W, H])
        mst = sb("mst", [P, W, P], BF16)
        mTs = sb("mTs", [P, BT], BF16)
        rden = sb("rden", [P, 2, BT])
        top = sb("top", [P, H, TOPK])
        left = sb("left", [P, H, LC])
        eS = sb("eS", [P, H, LC])
        kbd = sb("kbd", [P, KC, HPC * LC])
        kbd1r = sb("kbd1r", [P, KC, HPC * LC], F32R)
        vbd0 = sb("vbd0", [P, PAIRS, 2 * D])
        vbd1 = sb("vbd1", [P, PAIRS, 2 * D])

        pT = arena[:, 0:4096]
        pT_self = pT.rearrange("p (n h q) -> p n h q", n=2, h=H)
        pT_cross = pT.rearrange("p (h q) -> p h q", h=PAIRS)
        S = arena[:, 4096:8192].rearrange("p (t n) -> p t n", t=W)
        hid = arena[:, 8192:12288].rearrange("p (j n) -> p j n", j=J)
        kT = hid[:, 0:KC, :]
        sa = rden
        q2T = hT
        at = [0]

        def early(n):
            at[0] += n
            return arena[:, at[0] - n:at[0]]

        w_ada = early(KC * 9 * C).rearrange("p (k n) -> p k n", k=KC)
        w_ss = [early(KC * 2 * C).rearrange("p (k n) -> p k n", k=KC) for _ in range(2)]
        w_kv = [early(KC * 2 * C).rearrange("p (k n) -> p k n", k=KC) for _ in range(2)]
        v_out = early(2 * B * C).rearrange("p (a b n) -> p a b n", a=2, b=B)
        src2 = early(KC * B * 2 * LC).rearrange("p (k b d n) -> p k b d n", k=KC, b=B, d=2)
        keysT = early(KC * B * LC).rearrange("p (k n) -> p k n", k=KC)
        srcT = hT[:, 0, :].rearrange("p (k n) -> p k n", k=KC)
        modT = hT[:, 1, :].rearrange("p (k n) -> p k n", k=KC)
        x_keys = x[:, 0].rearrange("p t n -> p (t n)").rearrange("p (c n) -> p c n", c=KC)
        keys_out = [kbd[:], x_keys, left[:].rearrange("p (c h) n -> p c (h n)", c=KC),
                    eS[:].rearrange("p (c h) n -> p c (h n)", c=KC)]
        ctx_rows = xin[:, 0:2, :]
        condT = rden[:, 0, 0:KC * B].rearrange("p (k b) -> p k b", k=KC)
        scondT = rden[:, 0, 16:16 + KC * B].rearrange("p (k b) -> p k b", k=KC)
        gate_in = oT[0:B, :, :].rearrange("p k n -> p (k n)")[:, 0:3 * C]
        gate_out = qk[0:B, 0:2, :].rearrange("p k n -> p (k n)")[:, 0:3 * C]
        vrow = [qk[:, KC, 0:C], qk[:, KC, C:2 * C]]
        head_rows_f = x[:].rearrange("p b t n -> p (b t n)")

        bank = [ctx.enter_context(nc.psum_tensor(f"bank{i}", [P, BT], F32)) for i in range(NB)]

        filled = [sem(f"filled{i}") for i in range(NB)]
        drained = [sem(f"drained{i}") for i in range(NB)]
        s_early = sem("early_inputs_loaded")
        s_consts = sem("constants_loaded")
        s_weights = sem("weights_loaded")
        s_silu_c = sem("condition_silu_done")
        s_mod = sem("modulations_done")
        s_gate = sem("gate_rows_done")
        s_src2 = sem("context_doubled")
        s_keys = sem("early_keys_done")
        s_keys_stored = sem("early_keys_stored")
        s_vals = sem("early_values_done")
        s_gate_stored = sem("gate_rows_stored")
        s_zero = sem("head_blocks_zeroed")
        s_const_ready = sem("constants_rounded")
        s_half = sem("exponent_set")
        s_xin = sem("x_loaded")
        s_g = sem("gate_loaded")
        s_wso, s_wco, s_wm2 = sem("w_so_loaded"), sem("w_co_loaded"), sem("w_m2_loaded")
        s_kv0, s_kv1 = sem("keys_values0_loaded"), sem("keys_values1_loaded")
        s_cur = sem("modulations_of_batch")
        s_gated = sem("gated_done")
        s_kr = sem("keys1_rounded")
        s_mv = sem("moments_done")
        s_rstd = sem("rstd_done")
        s_xh = sem("tiles_normalised")
        s_xb = sem("bias_added")
        s_qkr = sem("qk_rounded")
        s_q3r = sem("q3_rounded")
        s_qbh = [sem("q_by_head_even"), sem("q_by_head_odd")]
        s_kbh0, s_kbh = sem("k_by_head_first"), sem("k_by_head")
        s_cur_msa = sem("msa_modulations_of_batch")
        s_mst = sem("self_max_split")
        s_mst3 = sem("cross_max_split")
        s_rd1 = sem("self_denominators")
        s_rd = sem("cross_denominators")
        s_top8 = sem("top8_done")
        s_dif = sem("max_subtracted")
        s_exp = sem("topk_exp_done")
        s_prob = sem("topk_probs_done")
        s_store = [sem("stored0"), sem("stored1")]
        s_held = {nc.vector: sem("vector_held"), nc.gpsimd: sem("gpsimd_held")}
        s_dve, s_act, s_pool = sem("vector_step"), sem("scalar_step"), sem("gpsimd_step")

        def hold(eng):
            eng.sem_inc(s_held[eng], 1)

        def ps(key):
            return bank[PLACE[key][0]][:]

        def fill_wait(pe, key, it):
            b, n = PLACE[key]
            if n:
                pe.wait_ge(drained[b], it * ROUNDS[b] + n)

        def filled_wait(eng, key, it, ago=0):
            b, n = PLACE[key]
            eng.wait_ge(filled[b], it * ROUNDS[b] + (n + 1 - ago * ROUNDS[b]))

        def drained_wait(eng, key, it, ago=0):
            b, n = PLACE[key]
            eng.wait_ge(drained[b], it * ROUNDS[b] + (n + 1 - ago * ROUNDS[b]))

        def fill(ins, key):
            ins.then_inc(filled[PLACE[key][0]], 1)

        def drain(ins, key):
            ins.then_inc(drained[PLACE[key][0]], 1)

        ORDER = [(1, 1), (2, 0), (2, 1), (3, 0), (4, 0), (3, 1), (4, 1), (1, 0)]
        LN = {k: n for n, k in enumerate(ORDER)}
        NLN = len(ORDER)
        BIAS = {k: n for n, k in enumerate([(1, 0), (1, 1), (2, 0), (2, 1), (3, 0), (4, 0), (3, 1), (4, 1)])}

        def moments_no(n, b, it):
            return it * NLN + (LN[n, b] + 3)

        def tiles_no(n, b, it, t, ago=0):
            return it * (NLN * W) + ((LN[n, b] - ago * NLN) * W + B // 2 + W + t + 1)
        MOD_OF = {1: MSA, 2: MCA, 3: MLP, 4: XQ}
        TILES = BLKS * W

        block = ctx.enter_context(nc.Block())

        @block.sync
        def _(sp):
            def wv(name):
                return t_in[name].rearrange("(k p) n -> p k n", p=P)

            for dst, src in ((condT, t_in["condT"]), (srcT, t_in["ctxT"]), (ctx_rows, t_in["ctx_rows"]),
                             (chan[:], t_in["chan"]), (gate_in, t_in["gate_bias"].to_broadcast([B, 3 * C])),
                             (rows[:].rearrange("p r n -> p (r n)"), t_in["rows"][:, 0:5 * C].to_broadcast([P, 5 * C])),
                             (vrow[0], t_in["rows"][:, 5 * C:6 * C].to_broadcast([P, C])),
                             (vrow[1], t_in["rows"][:, 6 * C:7 * C].to_broadcast([P, C])),
                             (w_ada, wv("w_ada")), (w_ss[0], wv("Wss_q")), (w_ss[1], wv("Wss_kv")),
                             (w_kv[0], wv("w_kv")), (w_kv[1], wv("Wkv"))):
                sp.dma_start(dst, src).then_inc(s_early, 16)
            for dst, src in ((ident[:], t_in["ident"]), (head_rows_f, t_in["head_rows"]),
                             (head_mask[:], t_in["head_mask"]),
                             (pair_mask[:], t_in["pair_mask"]),
                             (ones_half[:].rearrange("p s n -> p (s n)"), t_in["ones_half"])):
                sp.dma_start(dst, src).then_inc(s_consts, 16)
            for dst, name in ((w_qkv, "w_qkv"), (w_q2, "w_q"), (w_m1, "w_m1"), (w_q3, "Wq"), (w_p, "Wp")):
                sp.dma_start(dst[:], wv(name)).then_inc(s_weights, 16)
            sp.wait_ge(s_gate, 2)
            sp.dma_start(gate_d, gate_out).then_inc(s_gate_stored, 16)
            for a in range(2):
                for b in range(B):
                    sp.wait_ge(s_keys, a * B + b + 1)
                    sp.dma_start(kbd_d[a, b].rearrange("p (c n) -> p c n", c=KC), keys_out[b]).then_inc(s_keys_stored, 16)
            sp.wait_ge(s_gate_stored, 16)
            sp.wait_ge(s_keys_stored, 2 * B * 16)
            sp.wait_ge(s_store[0], 16)
            sp.wait_ge(s_store[1], 16)
            sp.wait_ge(s_zero, 2)
            x_d = t_in["x"]

            def load_x_first(token):
                sp.dma_start(xin[:], x_d[bass.ds(token + SHIFT, BT), :].rearrange("(t p) n -> p t n", p=P)).then_inc(s_xin, 16)

            def one_pass(it, more):
                def load_q(b, w):
                    if w >= 2:
                        filled_wait(sp, ("B", b, w - 2, 3), it)
                    elif w == 0:
                        drained_wait(sp, ("qk", b, KC - 1), it, 0 if b else 1)
                    for h in range(HPC):
                        r = slice(h * D, (h + 1) * D)
                        sp.dma_start(q_by_head[r, w % 2, h, :, :], qk[r, 0:KC, w * P:(w + 1) * P]).then_inc(s_qbh[w % 2], 16)

                def load(dst, src, done):
                    sp.dma_start(dst, src).then_inc(done, 16)

                def of_batch(a):
                    return a[bass.ds(it, 1)].rearrange("a p n -> (a p) n")

                load_q(0, 0)
                load_q(0, 1)
                filled_wait(sp, ("y", 4, 1, 1), it, 1)
                load(gate[:].rearrange("p g n -> p (g n)"), gate_d[bass.ds(it, 1), :].to_broadcast([P, 3 * C]), s_g)
                load(w_so[:], wv("w_so"), s_wso)
                load(kbd[:].rearrange("p c n -> p (c n)"), of_batch(kbd_d[0]), s_kv0)
                load(vbd0[:].rearrange("p c n -> p (c n)"), of_batch(vbd_d[0]), s_kv0)
                load_q(0, 2)
                sp.wait_ge(s_xb, it * NLN + BIAS[1, 0] + 2)
                load(xin[:, 0:W - 1, :], x_d[bass.ds(it * L + BT + SHIFT, BT - P), :].rearrange("(t p) n -> p t n", p=P), s_xin)
                load(xin[0:P - SHIFT, W - 1, :], x_d[bass.ds(it * L + L - P + SHIFT, P - SHIFT), :], s_xin)
                load(xin[P - SHIFT:P, W - 1, :], x_d[bass.ds(it * L, SHIFT), :], s_xin)
                load_q(0, 3)
                load(w_co[:], wv("w_co"), s_wco)
                load_q(1, 0)
                load_q(1, 1)
                load(w_m2[:], wv("w_m2"), s_wm2)
                load_q(1, 2)
                load_q(1, 3)
                if more:
                    sp.wait_ge(s_xb, it * NLN + BIAS[1, 1] + 2)
                    load_x_first(it * L + L)
                filled_wait(sp, ("S", 1, W - 1, KC - 1), it)
                load(kbd[:].rearrange("p c n -> p (c n)"), of_batch(kbd_d[1]), s_kv1)
                load(vbd1[:].rearrange("p c n -> p (c n)"), of_batch(vbd_d[1]), s_kv1)

            load_x_first(0)
            with sp.Fori(0, B - 1) as it:
                one_pass(it, True)
            one_pass(B - 1, False)
            sp.wait_ge(s_store[0], (B + 1) * 16)
            sp.wait_ge(s_store[1], (3 * B + 1) * 16)

        @block.gpsimd
        def _(pool):
            own = Chain(pool, s_pool)

            def rstd_of(n, eps):
                hold(pool)
                own.step(nc.gpsimd.tensor_scalar(veps[:, 0:n], mv[:, 0:n, 1], eps, 0.0, ALU.add, ALU.add))
                own.wait()
                nc.gpsimd.tensor_tensor(rstd[:, 0:n], veps[:, 0:n], minus_half[:, 0:n], ALU.pow).then_inc(s_rstd, 1)

            own.step(nc.gpsimd.memset(minus_half[:], -0.5))
            own.wait()
            nc.gpsimd.memset(q_by_head[:, 0], 0.0).then_inc(s_zero, 1)
            pool.sem_inc(s_xb, 1)
            pool.wait_ge(s_mv, 1)
            rstd_of(B // 2, EPS1)
            for a in range(2):
                pool.wait_ge(s_vals, 2 * (a + 1))
                pool.dma_start(vbd_d[a].rearrange("b p n -> p b n"), v_out[:, a]).then_inc(s_store[a], 16)

            def rstd_step(n, b, it):
                pool.wait_ge(s_mv, moments_no(n, b, it))
                rstd_of(W, EPS1 if n == 4 else EPS0)

            def round_q(key, src, done, it):
                for c in range(KC):
                    drained_wait(pool, (*key, c), it)
                    hold(pool)
                    nc.gpsimd.tensor_scalar(qr[:, c, :], qk[:, src + c, :], 1.0, 0.0, ALU.mult, ALU.add).then_inc(done, 1)

            def one_pass(it, more):
                def add_bias(n, b):
                    pool.wait_ge(s_xh, tiles_no(n, b, it, W - 1, 1 if (n, b) == (1, 0) else 0))
                    src = x[:, b]
                    if n == 1:
                        src = xin[:]
                        pool.wait_ge(s_store[b], it * (48 if b else 16) + 16)
                    row = rows[:, 1, :] if n == 4 else gated_bias[:, n - 1, :]
                    nc.gpsimd.tensor_tensor(x[:, b], src, row.unsqueeze(1).to_broadcast([P, W, C]), ALU.add).then_inc(s_xb, 1)

                def keys_by_head(b, w):
                    if w >= 2:
                        filled_wait(pool, ("A", b, w - 2, 3), it)
                    elif b:
                        filled_wait(pool, ("A", b - 1, w + 2, 3), it)
                    drained_wait(pool, ("qk", b, 2 * KC - 1), it, 0 if b else 1)
                    for c in range(KC):
                        i = nc.gpsimd.tensor_tensor(k_by_head[:, w % 2, c], kT[:, c, w * P:(w + 1) * P].unsqueeze(1).to_broadcast([P, HPC, P]),
                                                    head_mask[:].unsqueeze(2).to_broadcast([P, HPC, P]), ALU.mult)
                    i.then_inc(s_kbh, 1)

                def gate_weight(w, layer, loaded, n):
                    pool.wait_ge(loaded, it * 16 + 16)
                    for k in range(0, n, KC):
                        i = nc.gpsimd.tensor_tensor(w[:, k:k + KC, :], w[:, k:k + KC, :],
                                                    gate[:, layer, :].unsqueeze(1).to_broadcast([P, KC, C]), ALU.mult)
                    i.then_inc(s_gated, 1)

                def subtract_max(b, t):
                    n = b * W + t
                    pool.wait_ge(s_top8, it * TILES + n + 1)
                    pool.wait_ge(s_prob, it * TILES + n + 1)
                    nc.gpsimd.tensor_tensor(eS[:], S[:, t, :].rearrange("p (h n) -> p h n", h=H),
                                            top[:, :, 0:1].to_broadcast([P, H, LC]), ALU.subtract).then_inc(s_dif, 1)

                keys_by_head(0, 1)
                pool.wait_ge(s_g, it * 16 + 16)
                nc.gpsimd.tensor_tensor(gated_bias[:], gate[:], rows[:, 2:5, :], ALU.mult).then_inc(s_gated, 1)
                pool.wait_ge(s_gated, it * 4 + 1)
                add_bias(1, 0)
                keys_by_head(0, 2)
                gate_weight(w_so, 0, s_wso, KC)
                keys_by_head(0, 3)
                rstd_step(1, 1, it)
                add_bias(1, 1)
                rstd_step(2, 0, it)
                add_bias(2, 0)
                round_q(("qk", 1), 0, s_qkr, it)
                keys_by_head(1, 1)
                subtract_max(0, 0)
                keys_by_head(1, 2)
                subtract_max(0, 1)
                keys_by_head(1, 3)
                subtract_max(0, 2)
                gate_weight(w_co, 1, s_wco, KC)
                rstd_step(2, 1, it)
                add_bias(2, 1)
                subtract_max(0, 3)
                rstd_step(3, 0, it)
                add_bias(3, 0)
                gate_weight(w_m2, 2, s_wm2, J)
                for t in range(W):
                    subtract_max(1, t)
                    if t == 0:
                        pool.wait_ge(s_kv1, it * 32 + 32)
                        hold(pool)
                        nc.gpsimd.tensor_scalar(kbd1r[:], kbd[:], 1.0, 0.0, ALU.mult, ALU.add).then_inc(s_kr, 1)
                rstd_step(4, 0, it)
                add_bias(4, 0)
                rstd_step(3, 1, it)
                add_bias(3, 1)
                round_q(("q3", 0), KC, s_q3r, it)
                rstd_step(4, 1, it)
                add_bias(4, 1)
                if more:
                    rstd_step(1, 0, it)
                round_q(("q3", 1), KC, s_q3r, it)
                drained_wait(pool, ("y", 4, 0, 1), it)
                pool.dma_start(out[bass.ds(it * L + SHIFT, BT), :].rearrange("(t p) n -> p t n", p=P), x[:, 0]).then_inc(s_store[0], 16)
                if more:
                    round_q(("qk", 0), 0, s_qkr, it)
                drained_wait(pool, ("y", 4, 1, 1), it)
                pool.dma_start(out[bass.ds(it * L + BT + SHIFT, BT - P), :].rearrange("(t p) n -> p t n", p=P),
                               x[:, 1, 0:W - 1, :]).then_inc(s_store[1], 16)
                pool.dma_start(out[bass.ds(it * L + L - P + SHIFT, P - SHIFT), :], x[0:P - SHIFT, 1, W - 1, :]).then_inc(s_store[1], 16)
                pool.dma_start(out[bass.ds(it * L, SHIFT), :], x[P - SHIFT:P, 1, W - 1, :]).then_inc(s_store[1], 16)
                own.restart()

            rstd_step(1, 0, -1)
            round_q(("qk", 0), 0, s_qkr, -1)
            own.restart()
            with pool.Fori(0, B - 1) as it:
                one_pass(it, True)
            one_pass(B - 1, False)

        @block.scalar
        def _(act):
            own = Chain(act, s_act)
            act.wait_ge(s_early, 13 * 16)
            nc.scalar.activation(scondT, condT, ACT.Silu).then_inc(s_silu_c, 1)
            for a in range(2):
                if a == 1:
                    act.wait_ge(s_mod, 2)
                    for c in range(KC):
                        filled_wait(act, ("Tc", c), 0)
                        for b in range(B):
                            r = slice(b * LC, (b + 1) * LC)
                            i = nc.scalar.activation(modT[:, c, r], ps(("Tc", c))[:, r], ACT.Identity,
                                                     bias=mod[:, 0, XKV, c, b:b + 1], scale=mod[:, 1, XKV, c, b:b + 1])
                        drain(i, ("Tc", c))
                    act.wait_ge(s_keys, B)
                for c in range(KC):
                    filled_wait(act, ("kT", a, c), 0)
                    n = CB["k0" if a == 0 else "k1"] + c
                    drain(nc.scalar.activation(keysT[:, c, :], ps(("kT", a, c))[:, 0:B * LC], ACT.Identity,
                                               bias=chan[:, n:n + 1]), ("kT", a, c))
            nc.scalar.preload_act_table_set("natural_log_exp_and_others")

            def modulated(n, b, it):
                table = cur_msa if n == 1 else cur[:, :, MOD_OF[n]]
                for c in range(KC):
                    filled_wait(act, ("T", n, b, c), it)
                    drain(nc.scalar.activation(hT[:, c, :], ps(("T", n, b, c)), ACT.Identity,
                                               bias=table[:, 0, c:c + 1], scale=table[:, 1, c:c + 1]), ("T", n, b, c))

            def biased(dst, key, n, it):
                filled_wait(act, key, it)
                drain(nc.scalar.activation(dst, ps(key), ACT.Identity, bias=chan[:, n:n + 1]), key)

            def project_qk(b, it):
                for c in range(KC):
                    biased(qk[:, c, :], ("qk", b, c), CB["qk"] + c, it)
                for c in range(KC):
                    biased(kT[:, c, :], ("qk", b, KC + c), CB["qk"] + KC + c, it)

            def next_first(it):
                act.wait_ge(s_cur_msa, it + 2)
                modulated(1, 0, it)
                project_qk(0, it)

            def one_pass(it, more):
                def project_q2(b):
                    filled_wait(act, ("q2", b, KC - 1), it)
                    for c in range(KC):
                        biased(q2T[:, c, :], ("q2", b, c), CB["q2"] + c, it)

                def self_denominator(b, w):
                    filled_wait(act, ("PV", b, w), it)
                    if w >= 2:
                        drained_wait(act, ("PV", b, w - 2), it)
                    r = rden[:, w % 2, 0:KC * P]
                    own.step(nc.scalar.activation(r, ps(("PV", b, w))[:, KC * P:], ACT.Ln))
                    own.wait()
                    nc.scalar.activation(r, r, ACT.Exp, scale=-1.0).then_inc(s_rd1, 1)

                def window(b, w):
                    key = ("mT", b, w)
                    filled_wait(act, key, it)
                    drain(nc.scalar.activation(mTs[:, w * P:(w + 1) * P], ps(key)[:, 0:P // 2].bitcast(BF16), ACT.Copy), key)
                    for g in range(4):
                        key = ("B", b, w, g)
                        filled_wait(act, key, it)
                        drain(nc.scalar.activation(pT_self[:, w % 2, 4 * g:4 * g + 4, :], ps(key).rearrange("p (h q) -> p h q", h=4),
                                                   ACT.Exp, scale=SCORE_SCALE), key)
                    if w:
                        self_denominator(b, w - 1)

                def topk_exp(b, t):
                    act.wait_ge(s_dif, it * TILES + b * W + t + 1)
                    nc.scalar.activation(eS[:], eS[:], ACT.Exp, scale=SCORE_SCALE).then_inc(s_exp, 1)

                def take_scores(b):
                    for t in range(W):
                        for c in range(KC):
                            key = ("S", b, t, c)
                            filled_wait(act, key, it)
                            drain(nc.scalar.activation(S[:, t, c * BT:(c + 1) * BT], ps(key), ACT.Copy), key)

                def take_probs(b, tiles):
                    for t in tiles:
                        for c in range(KC):
                            key = ("TP", b, t, c)
                            filled_wait(act, key, it)
                            drain(nc.scalar.activation(pT_cross[:, 4 * c:4 * c + 4, t * P:(t + 1) * P],
                                                       ps(key).rearrange("p (h q) -> p h q", h=4), ACT.Copy), key)

                def cross_denominator(n, b):
                    for c in range(KC):
                        key = ("D", n, b, c)
                        filled_wait(act, key, it)
                        drain(nc.scalar.activation(rden[:, c, :], ps(key), ACT.Ln), key)
                        drained_wait(act, key, it)
                        nc.scalar.activation(rden[:, c, :], rden[:, c, :], ACT.Exp, scale=-1.0).then_inc(s_rd, 1)

                def silu(b, j):
                    if j >= 2:
                        drained_wait(act, ("ub", b, j - 2), it)
                    key = ("ua", b, j)
                    filled_wait(act, key, it)
                    drain(nc.scalar.activation(sa[:, j % 2, :], ps(key), ACT.Silu, bias=chan[:, CB["m1"] + j:CB["m1"] + j + 1]), key)

                def last_in(b):
                    modulated(4, b, it)
                    for c in range(KC):
                        biased(qk[:, KC + c, :], ("q3", b, c), CB["q3"] + c, it)

                def last_scores(b):
                    key = ("mT3", b)
                    filled_wait(act, key, it)
                    drain(nc.scalar.activation(mTs[:], ps(key)[:, 0:BT // 2].bitcast(BF16), ACT.Copy), key)
                    for p in range(PAIRS):
                        key = ("B3", b, p)
                        filled_wait(act, key, it)
                        drain(nc.scalar.activation(pT_cross[:, p, :], ps(key), ACT.Exp, scale=SCORE_SCALE), key)

                nc.scalar.preload_act_table_set("natural_log_exp_and_others")
                for w in range(W):
                    window(0, w)
                self_denominator(0, W - 1)
                modulated(1, 1, it)
                project_qk(1, it)
                act.wait_ge(s_cur, it + 1)
                modulated(2, 0, it)
                project_q2(0)
                take_scores(0)
                for w in range(W):
                    if w < W - 1:
                        topk_exp(0, w)
                    window(1, w)
                self_denominator(1, W - 1)
                modulated(2, 1, it)
                project_q2(1)
                take_probs(0, range(W - 1))
                topk_exp(0, W - 1)
                take_probs(0, range(W - 1, W))
                cross_denominator(2, 0)
                take_scores(1)
                modulated(3, 0, it)
                for j in range(J):
                    silu(0, j)
                    if j % W == W - 2:
                        nc.scalar.preload_act_table_set("natural_log_exp_and_others")
                        topk_exp(1, j // W)
                nc.scalar.preload_act_table_set("natural_log_exp_and_others")
                topk_exp(1, 2)
                topk_exp(1, 3)
                take_probs(1, range(W))
                cross_denominator(2, 1)
                last_in(0)
                last_scores(0)
                modulated(3, 1, it)
                for j in range(J):
                    silu(1, j)
                nc.scalar.preload_act_table_set("natural_log_exp_and_others")
                cross_denominator(4, 0)
                last_in(1)
                if more:
                    next_first(it)
                last_scores(1)
                cross_denominator(4, 1)
                own.restart()

            next_first(-1)
            with act.Fori(0, B - 1) as it:
                one_pass(it, True)
            one_pass(B - 1, False)

        @block.vector
        def _(dve):
            own = Chain(dve, s_dve)

            def moments(src, n):
                for t in range(n):
                    i = nc.vector.bn_stats(stats[:, t, :], src[:, t, :])
                own.step(i)
                own.wait()
                for t in range(n):
                    i = nc.vector.bn_aggr(mv[:, t, :], stats[:, t, :])
                i.then_inc(s_mv, 1)

            def normalise(src, n):
                for t in range(n):
                    nc.vector.tensor_scalar(xh[:, t, :], src[:, t, :], mv[:, t, 0:1], rstd[:, t:t + 1],
                                            ALU.subtract, ALU.mult).then_inc(s_xh, 1)

            dve.sem_inc(s_prob, 1)
            nc.vector.memset(vpad[:], 0.0)
            nc.vector.memset(mst[:], 0.0)
            dve.wait_ge(s_early, 13 * 16)
            moments(ctx_rows, B // 2)

            def double_context(src):
                for k in range(KC):
                    i = nc.vector.tensor_copy(src2[:, k], src[:, k, :].rearrange("p (b n) -> p b n", b=B)
                                              .unsqueeze(2).to_broadcast([P, B, 2, LC]))
                i.then_inc(s_src2, 1)

            double_context(srcT)
            dve.wait_ge(s_rstd, 1)
            normalise(ctx_rows, B // 2)
            dve.wait_ge(s_consts, 5 * 16)
            nc.vector.tensor_copy(identb[:], ident[:])
            nc.vector.tensor_copy(head_rows[:].rearrange("p h n -> p (h n)"), head_rows_f).then_inc(s_const_ready, 1)
            filled_wait(dve, ("mod",), 0)
            half = NMOD * KC
            for s in range(2):
                bias = chan[:, s * half:(s + 1) * half].unsqueeze(2).to_broadcast([P, half, B])
                i = nc.vector.scalar_tensor_tensor(
                    mod[:, s].rearrange("p m c b -> p (m c) b"),
                    ps(("mod",))[:, s * half * B:(s + 1) * half * B].rearrange("p (m b) -> p m b", b=B),
                    float(s), bias, ALU.add, ALU.add)
                i.then_inc(s_mod, 1)
            dve.wait_ge(s_mod, 2)
            dve.sem_inc(drained[PLACE[("mod",)][0]], 1)
            for i in range(2):
                filled_wait(dve, ("gate", i), 0)
                n = (2 - i) * C
                own.step(nc.vector.tensor_tensor(gate_out[:, i * 2 * C:i * 2 * C + n], ps(("gate", i))[0:B, 0:n],
                                                 gate_in[:, i * 2 * C:i * 2 * C + n], ALU.add))
                own.wait()
                dve.sem_inc(drained[PLACE[("gate", i)][0]], 1)
                dve.sem_inc(s_gate, 1)
            for a in range(2):
                if a == 1:
                    drained_wait(dve, ("Tc", 1), 0)
                    double_context(modT)
                    dve.wait_ge(s_keys_stored, B * 16)
                for c in range(KC):
                    drained_wait(dve, ("kT", a, c), 0)
                for b in range(B):
                    for c in range(KC):
                        i = nc.vector.tensor_tensor(
                            keys_out[b][:, c, :].rearrange("p (h n) -> p h n", h=HPC),
                            keysT[:, c, b * LC:(b + 1) * LC].unsqueeze(1).to_broadcast([P, HPC, LC]),
                            head_mask[:].unsqueeze(2).to_broadcast([P, HPC, LC]), ALU.mult)
                    i.then_inc(s_keys, 1)
                for u in range(B // 2):
                    key = ("vc", a, u)
                    filled_wait(dve, key, 0)
                    v = v_out[:, a, 2 * u:2 * u + 2, :]
                    drain(nc.vector.tensor_tensor(v, ps(key).rearrange("p (b n) -> p b n", b=2),
                                                  vrow[a].unsqueeze(1).to_broadcast([P, 2, C]), ALU.add), key)
                    drained_wait(dve, key, 0)
                    v = v.rearrange("p b (h n) -> p (b h) n", n=2 * D)
                    nc.vector.tensor_tensor(v, v, pair_mask[:].unsqueeze(1).to_broadcast([P, 2 * PAIRS, 2 * D]),
                                            ALU.mult).then_inc(s_vals, 1)
            nc.vector.memset(q_by_head[:, 1], 0.0).then_inc(s_zero, 1)

            def layer_norm(n, b, it):
                if n == 1:
                    src = xin[:]
                    dve.wait_ge(s_xin, it * 64 + 64 + (0 if b else 16))
                else:
                    src = x[:, b]
                    drained_wait(dve, ("y", n - 1, b, 1), it)
                moments(src, W)
                dve.wait_ge(s_rstd, moments_no(n, b, it))
                if LN[n, b]:
                    filled_wait(dve, ("T", *ORDER[LN[n, b] - 1], 1), it)
                normalise(src, W)

            def take_values(b, it):
                for u in range(2):
                    key = ("v", b, u)
                    filled_wait(dve, key, it)
                    for i in range(2):
                        dst = vpad[:, 2 * u + i].rearrange("p h (s n) -> p h s n", n=D)[:, :, 0:4:3, :]
                        ins = nc.vector.tensor_tensor(
                            dst, ps(key)[:, i * C:(i + 1) * C].rearrange("p (h s n) -> p h s n", s=2, n=D),
                            rows[:, 0, :].rearrange("p (h s n) -> p h s n", s=2, n=D), ALU.add)
                    drain(ins, key)

            def first_keys_by_head(b, it):
                for c in range(KC):
                    drained_wait(dve, ("qk", b, KC + c), it)
                    i = nc.vector.tensor_tensor(k_by_head[:, 0, c], kT[:, c, 0:P].unsqueeze(1).to_broadcast([P, HPC, P]),
                                                head_mask[:].unsqueeze(2).to_broadcast([P, HPC, P]), ALU.mult)
                i.then_inc(s_kbh0, 1)

            def msa_modulations(batch):
                nc.vector.tensor_copy(cur_msa[:].unsqueeze(3), mod[:, :, MSA, :, bass.ds(batch, 1)]).then_inc(s_cur_msa, 1)

            def one_pass(it, more):
                def split_max(slot, done):
                    own.step(nc.vector.tensor_copy(mst[:, slot, 0:H], negm[:, slot]))
                    own.wait()
                    nc.vector.tensor_tensor(mst[:, slot, H:2 * H], negm[:, slot], mst[:, slot, 0:H], ALU.subtract).then_inc(done, 1)

                def window_max(b, w):
                    for g in range(4):
                        key = ("A", b, w, g)
                        filled_wait(dve, key, it)
                        drain(nc.vector.tensor_reduce(negm[:, w, 4 * g:4 * g + 4], ps(key).rearrange("p (h n) -> p h n", h=4),
                                                      AX_X, ALU.max, negate=True), key)
                    drained_wait(dve, ("A", b, w, 3), it)
                    split_max(w, s_mst)

                def window_divide(b, w):
                    key = ("PV", b, w)
                    dve.wait_ge(s_rd1, (it * BLKS + b) * W + w + 1)
                    drain(nc.vector.tensor_tensor(oT[:, :, w * P:(w + 1) * P], ps(key)[:, 0:KC * P].rearrange("p (c n) -> p c n", c=KC),
                                                  rden[:, w % 2, 0:KC * P].rearrange("p (c n) -> p c n", c=KC), ALU.mult), key)

                def cross_divide(n, b):
                    for c in range(KC):
                        key = ("O", n, b, c)
                        filled_wait(dve, key, it)
                        dve.wait_ge(s_rd, (it * 4 + {(2, 0): 0, (2, 1): 1, (4, 0): 2, (4, 1): 3}[n, b]) * KC + c + 1)
                        drain(nc.vector.tensor_tensor(oT[:, c, :], ps(key), rden[:, c, :], ALU.mult), key)

                def residual(n, b):
                    dve.wait_ge(s_xb, it * NLN + BIAS[n, b] + 2)
                    for u in range(2):
                        key = ("y", n, b, u)
                        filled_wait(dve, key, it)
                        v = x[:, b, 2 * u:2 * u + 2, :]
                        drain(nc.vector.tensor_tensor(v, ps(key).rearrange("p (t n) -> p t n", t=2), v, ALU.add), key)

                def topk_step(b, t, s):
                    Sh = S[:, t, :].rearrange("p (h n) -> p h n", h=H)
                    if s == 0:
                        drained_wait(dve, ("S", b, t, KC - 1), it)
                    elif s == 1:
                        dve.wait_ge(s_top8, it * TILES + b * W + t + 1)
                    if s:
                        own.wait()
                    hold(dve)
                    for h in range(H):
                        eight = top[:, h, 0:8] if s < 2 else top[:, h, 8:16]
                        src = Sh[:, h, :] if s < 2 else left[:, h, :]
                        if s % 2 == 0:
                            i = nc.vector.max(eight, src)
                        else:
                            i = nc.vector.match_replace(left[:, h, :], eight, src, REPLACED)
                    if s == 0:
                        i.then_inc(s_top8, 1)
                    else:
                        own.step(i)
                    if s == 3:
                        own.wait()
                        dve.wait_ge(s_exp, it * TILES + b * W + t + 1)
                        nc.vector.scalar_tensor_tensor(Sh, left[:], REPLACED, eS[:], ALU.is_equal, ALU.mult).then_inc(s_prob, 1)

                def gated_linear(b, j):
                    drained_wait(dve, ("ua", b, j), it)
                    key = ("ub", b, j)
                    filled_wait(dve, key, it)
                    n = CB["m1"] + J + j
                    drain(nc.vector.scalar_tensor_tensor(hid[:, j, :], ps(key), chan[:, n:n + 1], sa[:, j % 2, :],
                                                         ALU.add, ALU.mult), key)

                def last_max(b):
                    for t in range(W):
                        for c in range(KC):
                            key = ("A3", b, t, c)
                            filled_wait(dve, key, it)
                            drain(nc.vector.tensor_reduce(negm[:, t, HPC * c:HPC * (c + 1)], ps(key).rearrange("p (h n) -> p h n", h=HPC),
                                                          AX_X, ALU.max, negate=True), key)
                        drained_wait(dve, ("A3", b, t, KC - 1), it)
                        split_max(t, s_mst3)

                nc.vector.tensor_copy(cur[:].rearrange("p s m c -> p (s m c)").unsqueeze(2),
                                      mod[:].rearrange("p s m c b -> p (s m c) b")[:, :, bass.ds(it, 1)]).then_inc(s_cur, 1)
                window_max(0, 0)
                for w in range(W):
                    if w + 1 < W:
                        window_max(0, w + 1)
                    if w:
                        window_divide(0, w - 1)
                    if w == 2:
                        layer_norm(1, 1, it)
                window_divide(0, W - 1)
                residual(1, 0)
                layer_norm(2, 0, it)
                first_keys_by_head(1, it)
                take_values(1, it)
                window_max(1, 0)
                for s in range(4):
                    topk_step(0, 0, s)
                for w in range(W):
                    if w + 1 < W:
                        window_max(1, w + 1)
                    if w < 2:
                        topk_step(0, w + 1, 0)
                        topk_step(0, w + 1, 1)
                    if w:
                        window_divide(1, w - 1)
                    if w < 2:
                        topk_step(0, w + 1, 2)
                        topk_step(0, w + 1, 3)
                window_divide(1, W - 1)
                residual(1, 1)
                layer_norm(2, 1, it)
                for s in range(4):
                    topk_step(0, W - 1, s)
                cross_divide(2, 0)
                residual(2, 0)
                layer_norm(3, 0, it)
                for j in range(J):
                    topk_step(1, j // 4, j % 4)
                    gated_linear(0, j)
                for j in range(J, 4 * W):
                    topk_step(1, j // 4, j % 4)
                residual(3, 0)
                layer_norm(4, 0, it)
                cross_divide(2, 1)
                residual(2, 1)
                layer_norm(3, 1, it)
                last_max(0)
                for j in range(J):
                    gated_linear(1, j)
                residual(3, 1)
                layer_norm(4, 1, it)
                cross_divide(4, 0)
                residual(4, 0)
                if more:
                    msa_modulations(it + 1)
                    layer_norm(1, 0, it)
                last_max(1)
                if more:
                    first_keys_by_head(0, it)
                cross_divide(4, 1)
                if more:
                    take_values(0, it)
                residual(4, 1)
                own.restart()

            msa_modulations(0)
            layer_norm(1, 0, -1)
            first_keys_by_head(0, -1)
            take_values(0, -1)
            own.restart()
            with dve.Fori(0, B - 1) as it:
                one_pass(it, True)
            one_pass(B - 1, False)

        @block.tensor
        def _(pe):
            def mm(dst, lhsT, rhs, start, stop):
                return nc.tensor.matmul(dst, lhsT, rhs, start=start, stop=stop)

            def channels(key, dst, weights, rhs, it):
                fill_wait(pe, key, it)
                for k in range(KC):
                    i = mm(dst, weights(k), rhs(k), k == 0, k == KC - 1)
                return i

            pe.wait_ge(s_early, 13 * 16)
            pe.wait_ge(s_silu_c, 1)
            for s in range(2):
                for m in range(NMOD):
                    for c in range(KC):
                        if m <= MLP:
                            w, col = w_ada, (3 * m + s) * C + c * P
                        else:
                            w, col = w_ss[m - XQ], (1 - s) * C + c * P
                        at = ((s * NMOD + m) * KC + c) * B
                        for k in range(KC):
                            i = mm(ps(("mod",))[:, at:at + B], w[:, k, col:col + P], scondT[:, k, :], k == 0, k == KC - 1)
            fill(i, ("mod",))
            for i_ in range(2):
                for m in ((MSA, MCA), (MLP,))[i_]:
                    at = (m - 2 * i_) * C
                    for k in range(KC):
                        i = mm(ps(("gate", i_))[0:B, at:at + C], scondT[:, k, :], w_ada[:, k, (3 * m + 2) * C:(3 * m + 3) * C],
                               k == 0, k == KC - 1)
                fill(i, ("gate", i_))
            for a in range(2):
                if a == 1:
                    pe.wait_ge(s_xh, B // 2)
                    pe.wait_ge(s_const_ready, 1)
                    for c in range(KC):
                        fill_wait(pe, ("Tc", c), 0)
                        for t in range(B // 2):
                            i = nc.tensor.transpose(ps(("Tc", c))[:, t * P:(t + 1) * P], xh[:, t, c * P:(c + 1) * P], ident[:])
                        fill(i, ("Tc", c))
                    for c in range(KC):
                        drained_wait(pe, ("Tc", c), 0)
                src = (srcT, modT)[a]
                for c in range(KC):
                    key = ("kT", a, c)
                    fill(channels(key, ps(key)[:, 0:B * LC], lambda k: w_kv[a][:, k, c * P:(c + 1) * P],
                                  lambda k: src[:, k, :], 0), key)
                pe.wait_ge(s_src2, a + 1)
                for u in range(B // 2):
                    key = ("vc", a, u)
                    for i_ in range(2):
                        i = channels(key, ps(key)[:, i_ * C:(i_ + 1) * C],
                                     lambda k: src2[:, k, 2 * u + i_].rearrange("p d n -> p (d n)"),
                                     lambda k: w_kv[a][:, k, C:2 * C], 0)
                    fill(i, key)
            pe.wait_ge(s_weights, 5 * 16)

            def transposed(n, b, it):
                for c in range(KC):
                    key = ("T", n, b, c)
                    fill_wait(pe, key, it)
                    for t in range(W):
                        if c == 0:
                            pe.wait_ge(s_xh, tiles_no(n, b, it, t))
                        i = nc.tensor.transpose(ps(key)[:, t * P:(t + 1) * P], xh[:, t, c * P:(c + 1) * P], ident[:])
                    fill(i, key)
                drained_wait(pe, ("T", n, b, KC - 1), it)

            def qk_in(b, it):
                transposed(1, b, it)
                for i_ in range(2 * KC):
                    key = ("qk", b, i_)
                    fill(channels(key, ps(key), lambda k: w_qkv[:, k, i_ * P:(i_ + 1) * P], lambda k: hT[:, k, :], it), key)

            def v_in(b, it):
                for u in range(2):
                    key = ("v", b, u)
                    for i_ in range(2):
                        t = 2 * u + i_
                        i = channels(key, ps(key)[:, i_ * C:(i_ + 1) * C], lambda k: hT[:, k, t * P:(t + 1) * P],
                                     lambda k: w_qkv[:, k, 2 * C:3 * C], it)
                    fill(i, key)

            def one_pass(it, more):
                def scores_for_max(b, w):
                    if w:
                        pe.wait_ge(s_kbh, (it * BLKS + b) * (W - 1) + w)
                    else:
                        pe.wait_ge(s_kbh0, it * BLKS + b + 1)
                        pe.wait_ge(s_qkr, (it * BLKS + b) * KC + KC)
                    for g in range(4):
                        key = ("A", b, w, g)
                        fill_wait(pe, key, it)
                        c, h = g // 2, (g % 2) * 4
                        fill(mm(ps(key), qr[:, c, w * P:(w + 1) * P], k_by_head[:, w % 2, c, h:h + 4, :], True, True), key)

                def scores_minus_max(b, w):
                    key = ("mT", b, w)
                    fill_wait(pe, key, it)
                    pe.wait_ge(s_mst, (it * BLKS + b) * W + w + 1)
                    fill(nc.tensor.transpose(ps(key)[:, 0:P // 2].bitcast(BF16), mst[:, w, :], identb[:]), key)
                    pe.wait_ge(s_qbh[w % 2], ((it * BLKS + b) * 2 + w // 2) * HPC * 16 + HPC * 16)
                    for g in range(4):
                        key = ("B", b, w, g)
                        fill_wait(pe, key, it)
                        c, h = g // 2, (g % 2) * 4
                        mm(ps(key), kT[:, c, w * P:(w + 1) * P], q_by_head[:, w % 2, h:h + 4, c, :], True, False)
                        if g == 0:
                            drained_wait(pe, ("mT", b, w), it)
                        for i_ in range(4):
                            i = mm(ps(key)[:, i_ * P:(i_ + 1) * P], head_rows[:, 4 * g + i_, :], mTs[:, w * P:(w + 1) * P],
                                   False, i_ == 3)
                        fill(i, key)

                def window_values(b, w):
                    key = ("PV", b, w)
                    fill_wait(pe, key, it)
                    drained_wait(pe, ("B", b, w, 3), it)
                    for c in range(KC):
                        for s in range(2):
                            for p in range(4):
                                i = mm(ps(key)[32 * p:32 * p + 32, c * P:(c + 1) * P], vpad[:, w, 4 * c + p, 2 * D * s:2 * D * (s + 1)],
                                       pT_self[:, w % 2, HPC * c + 2 * p + s, :], s == 0, s == 1)
                    for c in range(KC):
                        for s in range(2):
                            for p in range(4):
                                i = mm(ps(key)[32 * p:32 * p + 32, (KC + c) * P:(KC + c + 1) * P], ones_half[:, s, :],
                                       pT_self[:, w % 2, HPC * c + 2 * p + s, :], s == 0, s == 1)
                    fill(i, key)

                def project(n, b):
                    w, src, chunks = {1: (w_so, oT, KC), 2: (w_co, oT, KC), 3: (w_m2, hid, J), 4: (w_p, oT, KC)}[n]
                    if n <= 3:
                        pe.wait_ge(s_gated, it * 4 + n + 1)
                    if n == 1:
                        drained_wait(pe, ("PV", b, W - 1), it)
                    elif n == 3:
                        drained_wait(pe, ("ub", b, J - 1), it)
                    else:
                        drained_wait(pe, ("O", n, b, KC - 1), it)
                    for u in range(2):
                        key = ("y", n, b, u)
                        fill_wait(pe, key, it)
                        for i_ in range(2):
                            t = 2 * u + i_
                            for k in range(chunks):
                                i = mm(ps(key)[:, i_ * C:(i_ + 1) * C], src[:, k, t * P:(t + 1) * P], w[:, k, :],
                                       k == 0, k == chunks - 1)
                        fill(i, key)

                def windows(b):
                    drained_wait(pe, ("v", b, 1), it, 0 if b else 1)
                    scores_for_max(b, 0)
                    for w in range(W):
                        if w + 1 < W:
                            scores_for_max(b, w + 1)
                        scores_minus_max(b, w)
                        if w:
                            window_values(b, w - 1)
                    window_values(b, W - 1)
                    project(1, b)

                def cross_in(b):
                    transposed(2, b, it)
                    for c in range(KC):
                        key = ("q2", b, c)
                        fill(channels(key, ps(key), lambda k: w_q2[:, k, c * P:(c + 1) * P], lambda k: hT[:, k, :], it), key)

                def scores(b, tiles):
                    if b == 0:
                        pe.wait_ge(s_kv0, it * 32 + 32)
                    drained_wait(pe, ("q2", b, KC - 1), it)
                    for t in tiles:
                        for c in range(KC):
                            key = ("S", b, t, c)
                            fill_wait(pe, key, it)
                            fill(mm(ps(key), q2T[:, c, t * P:(t + 1) * P], kbd[:, c, :], True, True), key)

                def values(n, b):
                    vals = vbd0 if n == 2 else vbd1
                    drained_wait(pe, ("TP", b, W - 1, KC - 1) if n == 2 else ("B3", b, PAIRS - 1), it)
                    for c in range(KC):
                        key = ("D", n, b, c)
                        fill_wait(pe, key, it)
                        for p in range(4):
                            i = mm(ps(key)[32 * p:32 * p + 32, :], pair_mask[:], pT_cross[:, 4 * c + p, :], True, True)
                        fill(i, key)
                        key = ("O", n, b, c)
                        fill_wait(pe, key, it)
                        for p in range(4):
                            i = mm(ps(key)[32 * p:32 * p + 32, :], vals[:, 4 * c + p, :], pT_cross[:, 4 * c + p, :], True, True)
                        fill(i, key)

                def weigh(b):
                    for t in range(W):
                        pe.wait_ge(s_prob, it * TILES + b * W + t + 2)
                        for c in range(KC):
                            key = ("TP", b, t, c)
                            fill_wait(pe, key, it)
                            for p in range(4):
                                at = (4 * c + p) * P
                                i = nc.tensor.transpose(ps(key)[:, p * P:(p + 1) * P], S[:, t, at:at + P], ident[:])
                            fill(i, key)
                    values(2, b)

                def mlp(b):
                    transposed(3, b, it)
                    for j in range(J):
                        for name, at in (("ua", 0), ("ub", HID)):
                            key = (name, b, j)
                            fill(channels(key, ps(key), lambda k: w_m1[:, k, at + j * P:at + (j + 1) * P],
                                          lambda k: hT[:, k, :], it), key)
                    project(3, b)

                def last_in(b):
                    transposed(4, b, it)
                    for c in range(KC):
                        key = ("q3", b, c)
                        fill(channels(key, ps(key), lambda k: w_q3[:, k, c * P:(c + 1) * P], lambda k: hT[:, k, :], it), key)
                    pe.wait_ge(s_kr, it + 1)
                    pe.wait_ge(s_q3r, (it * BLKS + b) * KC + KC)
                    for t in range(W):
                        for c in range(KC):
                            key = ("A3", b, t, c)
                            fill_wait(pe, key, it)
                            fill(mm(ps(key), qr[:, c, t * P:(t + 1) * P], kbd1r[:, c, :], True, True), key)

                def last_scores(b):
                    def pair_rows(p):
                        at = 2 * p * P + P - LC
                        return head_rows[:].rearrange("p h n -> p (h n)")[:, at:at + 2 * LC]

                    def products(p):
                        key = ("B3", b, p)
                        fill_wait(pe, key, it)
                        c = p // 4
                        mm(ps(key), kbd[:, c, (p % 4) * P:(p % 4 + 1) * P], qk[:, KC + c, :], True, False)

                    def minus_max(p):
                        fill(mm(ps(("B3", b, p)), pair_rows(p), mTs[:], False, True), ("B3", b, p))

                    for p in range(3):
                        products(p)
                    key = ("mT3", b)
                    fill_wait(pe, key, it)
                    for t in range(W):
                        pe.wait_ge(s_mst3, (it * BLKS + b) * W + t + 1)
                        i = nc.tensor.transpose(ps(key)[:, t * P // 2:(t + 1) * P // 2].bitcast(BF16), mst[:, t, :], identb[:])
                    fill(i, key)
                    drained_wait(pe, key, it)
                    for p in range(3):
                        minus_max(p)
                    for p in range(3, PAIRS):
                        products(p)
                        minus_max(p)

                def skip(keys):
                    for key in keys:
                        pass_over(key, it)

                windows(0)
                qk_in(1, it)
                v_in(1, it)
                cross_in(0)
                scores(0, range(W))
                windows(1)
                cross_in(1)
                weigh(0)
                scores(1, range(0, 2))
                project(2, 0)
                scores(1, range(2, W))
                mlp(0)
                weigh(1)
                project(2, 1)
                last_in(0)
                last_scores(0)
                mlp(1)
                values(4, 0)
                project(4, 0)
                last_in(1)
                if more:
                    qk_in(0, it)
                else:
                    skip(TAIL[:TAIL.index(("qk", 0, 2 * KC - 1)) + 1])
                last_scores(1)
                values(4, 1)
                if more:
                    v_in(0, it)
                else:
                    skip([("v", 0, 0), ("v", 0, 1)])
                project(4, 1)

            def pass_over(key, it):
                fill_wait(pe, key, it)
                pe.sem_inc(filled[PLACE[key][0]], 1)
                pe.sem_inc(drained[PLACE[key][0]], 1)

            for key in SKIPPED:
                pass_over(key, 0)
            for n, key in enumerate(TAIL):
                if key == ("T", 1, 0, 0):
                    qk_in(0, -1)
                elif key == ("v", 0, 0):
                    v_in(0, -1)
                elif key not in AHEAD:
                    pass_over(key, -1)
            with pe.Fori(0, B - 1) as it:
                one_pass(it, True)
            one_pass(B - 1, False)


def kernel(**inputs):
    import numpy as np
    import concourse.bacc as bacc
    from concourse.bass_utils import run_bass_kernel_spmd

    def arr(name):
        return np.ascontiguousarray(inputs[name])

    def cols(v):
        return v.reshape(-1, P).T

    a, b = "L0_xcond_", "L1_xcond_"
    ada = arr(a + "b_ada").reshape(3, 3, C)
    ssq, sskv = arr(b + "bss_q").reshape(2, C), arr(b + "bss_kv").reshape(2, C)
    bqkv, bkv, bkv1 = arr(a + "b_qkv"), arr(a + "b_kv"), arr(b + "bkv")
    chan = np.concatenate([
        cols(np.concatenate([ada[0, 0], ada[1, 0], ada[2, 0], ssq[1], sskv[1]])),
        cols(np.concatenate([ada[0, 1], ada[1, 1], ada[2, 1], ssq[0], sskv[0]])),
        cols(bqkv[:2 * C]), cols(arr(a + "b_q")), cols(bkv[:C]), cols(arr(a + "b_m1")), cols(arr(b + "bq")), cols(bkv1[:C])], axis=1)
    rows = np.concatenate([bqkv[2 * C:], arr(b + "bp"), arr(a + "b_so"), arr(a + "b_co"), arr(a + "b_m2"), bkv[C:], bkv1[C:]])[None, :]
    ctx = arr("ctx_1024").reshape(B * LC, C)
    r, one = np.arange(P), np.float32(1)
    head = np.arange(H)
    head_rows = np.zeros((P, H, P), np.float32)
    head_rows[:2 * H] = ((r[:2 * H] % H)[:, None] == head[None, :])[:, :, None]
    arrays = {
        "x": arr("x").reshape(B * L, C),
        "condT": arr("cond_1024").T.reshape(KC, P, B).transpose(1, 0, 2),
        "ctxT": ctx.T.reshape(KC, P, B * LC).transpose(1, 0, 2),
        "ctx_rows": ctx.reshape(B // 2, P, C).transpose(1, 0, 2),
        "chan": chan, "gate_bias": ada[:, 2].reshape(1, 3 * C), "rows": rows,
        "ident": np.eye(P, dtype=np.float32),
        "head_rows": head_rows.reshape(P, H * P),
        "head_mask": (r[:, None] // D == np.arange(HPC)[None, :]).astype(np.float32),
        "pair_mask": (r[:, None] // LC == np.arange(2 * D)[None, :] // D).astype(np.float32),
        "ones_half": np.repeat(np.eye(2, dtype=np.float32), D, axis=1).reshape(1, 4 * D).repeat(P, axis=0),
    }
    for n in ("w_ada", "w_qkv", "w_so", "w_q", "w_kv", "w_co", "w_m1", "w_m2"):
        arrays[n] = arr(a + n)
    for n in ("Wq", "Wkv", "Wp", "Wss_q", "Wss_kv"):
        arrays[n] = arr(b + n)
    arrays = {"in_" + k: np.ascontiguousarray(v) for k, v in arrays.items()}

    nc = bacc.Bacc("TRN2", target_bir_lowering=False, num_devices=1)
    t_in = {k[3:]: nc.dram_tensor(k, v.shape, mybir.dt.from_np(v.dtype), kind="ExternalInput").ap() for k, v in arrays.items()}
    out = nc.dram_tensor("out", [B * L, C], F32, kind="ExternalOutput").ap()
    build(nc, t_in, out)
    res = run_bass_kernel_spmd(nc, [arrays], core_ids=[0])
    return res.results[0]["out"].reshape(B, L, C)
```

```python
from contextlib import ExitStack

import concourse.bass as bass
from concourse import mybir

F32 = mybir.dt.float32
F32R = mybir.dt.float32r
BF16 = mybir.dt.bfloat16
ALU = mybir.AluOpType
ACT = mybir.ActivationFunctionType
AX_X = mybir.AxisListType.X

P = 128
B, L, C = 4, 1024, 256
LC = 64
H, D = 16, 16
SHIFT = 64
HID = 1024
TOPK = 16
KC = C // P
HPC = P // D
PAIRS = H // 2
W = 4
BT = W * P
BLKS = L // BT
J = HID // P
SCORE_SCALE = 1.0 / D ** 0.5
REPLACED = -3.0e38
EPS0, EPS1 = 1e-6, 1e-5

MSA, MCA, MLP, XQ, XKV = range(5)
NMOD = 5

CB = {}
_at = 0
for _name, _n in (("shift", NMOD * KC), ("scale", NMOD * KC), ("qk", 2 * KC), ("q2", KC), ("k0", KC),
                  ("m1", 2 * J), ("q3", KC), ("k1", KC)):
    CB[_name] = _at
    _at += _n
NCB = _at
ROWS = ("v_self", "p", "so", "co", "m2", "v0", "v1")


def before_loop():
    for a in range(2):
        if a == 1:
            yield ("mod",)
            for i in range(2):
                yield ("gate", i)
            for c in range(KC):
                yield ("Tc", c)
        for c in range(KC):
            yield ("kT", a, c)
        for u in range(B // 2):
            yield ("vc", a, u)


def in_loop():
    def transposed(n, b):
        for c in range(KC):
            yield ("T", n, b, c)

    def qk_in(b):
        for i in range(2 * KC):
            yield ("qk", b, i)

    def v_in(b, halves=(0, 1)):
        for u in halves:
            yield ("v", b, u)

    def windows(b):
        for g in range(4):
            yield ("A", b, 0, g)
        for w in range(W):
            if w + 1 < W:
                for g in range(4):
                    yield ("A", b, w + 1, g)
            yield ("mT", b, w)
            for g in range(4):
                yield ("B", b, w, g)
            if w:
                yield ("PV", b, w - 1)
        yield ("PV", b, W - 1)

    def cross_in(b):
        yield from transposed(2, b)
        for c in range(KC):
            yield ("q2", b, c)

    def scores(b, tiles):
        for t in tiles:
            for c in range(KC):
                yield ("S", b, t, c)

    def probs(b, tiles):
        for t in tiles:
            for c in range(KC):
                yield ("TP", b, t, c)

    def values(n, b):
        for c in range(KC):
            yield ("D", n, b, c)
            yield ("O", n, b, c)

    def project(n, b):
        for u in range(2):
            yield ("y", n, b, u)

    def mlp(b):
        yield from transposed(3, b)
        for j in range(J):
            yield ("ua", b, j)
            yield ("ub", b, j)
        yield from project(3, b)

    def last_in(b):
        for c in range(KC):
            yield ("q3", b, c)

    def last_for_max(b, tiles):
        for t in tiles:
            for c in range(KC):
                yield ("A3", b, t, c)

    def last_scores(b):
        for p in range(PAIRS):
            yield ("B3", b, p)
            if p == LAST_AHEAD - 1:
                yield ("mT3", b)

    yield from windows(0)
    yield from transposed(1, 1)
    yield from project(1, 0)
    yield from qk_in(1)
    yield from cross_in(0)
    yield from v_in(1, (0,))
    yield from scores(0, range(W))
    yield from v_in(1, (1,))
    yield from windows(1)
    yield from probs(0, range(0, 1))
    yield from project(1, 1)
    yield from probs(0, range(1, 3))
    yield from cross_in(1)
    yield from scores(1, range(0, 2))
    yield from probs(0, range(3, W))
    yield from values(2, 0)
    yield from scores(1, range(2, 3))
    yield from project(2, 0)
    yield from scores(1, range(3, W))
    yield from mlp(0)
    yield from probs(1, range(W - 1))
    yield from transposed(4, 0)
    yield from last_in(0)
    yield from probs(1, range(W - 1, W))
    yield from values(2, 1)
    yield from last_for_max(0, range(0, 2))
    yield from project(2, 1)
    yield from last_for_max(0, range(2, W))
    yield from last_scores(0)
    yield from mlp(1)
    yield from values(4, 0)
    yield from transposed(4, 1)
    yield from last_in(1)
    yield from project(4, 0)
    yield from last_for_max(1, range(W))
    yield from transposed(1, 0)
    yield from qk_in(0)
    yield from last_scores(1)
    yield from values(4, 1)
    yield from v_in(0)
    yield from project(4, 1)


NB = 8
QUARTERS = (2, 1, 1, 0, 1, 1, 0, 0)
LAST_AHEAD = 5
LOOP = list(in_loop())
TAIL = LOOP[LOOP.index(("T", 1, 0, 0)):]
AHEAD = {key for key in TAIL if key[:3] == ("T", 1, 0) or key[:2] in (("qk", 0), ("v", 0))}
PRE = list(before_loop())
PRE += [("skip", n) for n in range((len(LOOP) - len(TAIL) - len(PRE)) % NB)]
SKIPPED = [key for key in PRE if key[0] == "skip"]
PRE_USES = [len((PRE + TAIL)[n::NB]) for n in range(NB)]
ROUNDS = [len(LOOP[n::NB]) for n in range(NB)]
PLACE = {key: (n % NB, n // NB) for n, key in enumerate(PRE)}
PLACE.update({key: (n % NB, PRE_USES[n % NB] + n // NB) for n, key in enumerate(LOOP)})
assert len(PLACE) == len(PRE) + len(LOOP)
assert all(PLACE[key][1] - ROUNDS[PLACE[key][0]] == (len(PRE) + n) // NB and PLACE[key][0] == (len(PRE) + n) % NB
           for n, key in enumerate(TAIL))


class Chain:

    def __init__(self, eng, sem):
        self.eng, self.sem, self.n = eng, sem, 0

    def step(self, instruction):
        self.n += 1
        instruction.then_inc(self.sem, 1)

    def wait(self):
        self.eng.wait_ge(self.sem, self.n)

    def restart(self):
        self.eng.wait_ge(self.sem, self.n)
        self.eng.sem_clear(self.sem)
        self.n = 0


def build(nc, t_in, out):
    ctx = ExitStack()
    with ctx:
        def sb(name, shape, dt=F32):
            return ctx.enter_context(nc.sbuf_tensor(name, shape, dt))

        def sem(name):
            return ctx.enter_context(nc.semaphore(name))

        gate_d = nc.dram_tensor("gate_rows", [B, 3 * C], F32, kind="Internal").ap()
        kbd_d = nc.dram_tensor("keys_by_head", [2, B, P, KC * HPC * LC], F32, kind="Internal").ap()
        m1_low_d = nc.dram_tensor("m1_weights_rest", [P, KC * 2 * HID], F32, kind="Internal").ap()
        vbd_d = nc.dram_tensor("values_by_pair", [2, B, P, C], F32, kind="Internal").ap()

        w_qkv = sb("w_qkv", [P, KC, 3 * C])
        w_q2 = sb("w_q2", [P, KC, C])
        w_m1 = sb("w_m1", [P, KC, 2 * HID], F32R)
        w_q3 = sb("w_q3", [P, KC, C])
        w_p = sb("w_p", [P, KC, C])
        w_so = sb("w_so", [P, KC, C])
        w_co = sb("w_co", [P, KC, C])
        w_m2 = sb("w_m2", [P, J, C])
        chan = sb("chan", [P, NCB])
        rows = sb("rows", [P, 5, C])
        gate = sb("gate", [P, 3, C])
        gated_bias = sb("gated_bias", [P, 3, C])
        mod = sb("mod", [P, 2, NMOD, KC, B])
        cur = sb("cur", [P, 2, NMOD, KC])
        cur_msa = sb("cur_msa", [P, 2, KC])
        ident = sb("ident", [P, P])
        identb = sb("identb", [P, P], BF16)
        head_rows = sb("head_rows", [P, H, P], BF16)
        head_select = sb("head_select", [P, H])
        head_mask = sb("head_mask", [P, HPC])
        pair_mask = sb("pair_mask", [P, 2 * D])
        ones_half = sb("ones_half", [P, 2, 2 * D])
        minus_half = sb("minus_half", [P, W])
        xin = sb("xin", [P, W, C])
        x = sb("x", [P, BLKS, W, C])
        xh = sb("xh", [P, W, C])
        hT = sb("hT", [P, KC, BT])
        qk = sb("qk", [P, 2 * KC, BT])
        qr = sb("qr", [P, KC, BT], F32R)
        q_by_head = sb("q_by_head", [P, 2, HPC, KC, P])
        k_by_head = sb("k_by_head", [P, 2, KC, HPC, P], F32R)
        vpad = sb("vpad", [P, W, PAIRS, 4 * D])
        arena = sb("arena", [P, 12288])
        oT = sb("oT", [P, KC, BT])
        stats = sb("stats", [P, W, 6])
        mv = sb("mv", [P, W, 2])
        veps = sb("veps", [P, W])
        rstd = sb("rstd", [P, W])
        negm = sb("negm", [P, W, H])
        mst = sb("mst", [P, W, P], BF16)
        mTs = sb("mTs", [P, BT], BF16)
        rden = sb("rden", [P, 2, BT])
        top = sb("top", [P, H, TOPK])
        left = sb("left", [P, H, LC])
        eS = sb("eS", [P, H, LC])
        kbd = sb("kbd", [P, KC, HPC * LC])
        kbd1r = sb("kbd1r", [P, KC, HPC * LC], F32R)
        vbd0 = sb("vbd0", [P, PAIRS, 2 * D])
        vbd1 = sb("vbd1", [P, PAIRS, 2 * D])

        pT = arena[:, 0:4096]
        pT_self = pT.rearrange("p (n h q) -> p n h q", n=2, h=H)
        pT_cross = pT.rearrange("p (h q) -> p h q", h=PAIRS)
        S = arena[:, 4096:8192].rearrange("p (t n) -> p t n", t=W)
        hid = arena[:, 8192:12288].rearrange("p (j n) -> p j n", j=J)
        kT = hid[:, 0:KC, :]
        sa = rden
        m1_low = k_by_head[:].rearrange("p n c h q -> p (n c h q)").rearrange("p (k n) -> p k n", k=KC)
        h_low = kbd1r
        m1_in = q_by_head[:].rearrange("p n h c q -> p (n h c q)").rearrange("p (k n) -> p k n", k=KC)
        q2T = hT

        def input_of(n, b):
            return qk[:, KC:, :] if (n, b) == (1, 1) else hT

        at = [0]

        def early(n):
            at[0] += n
            return arena[:, at[0] - n:at[0]]

        w_ada = early(KC * 9 * C).rearrange("p (k n) -> p k n", k=KC)
        w_ss = [early(KC * 2 * C).rearrange("p (k n) -> p k n", k=KC) for _ in range(2)]
        w_kv = [early(KC * 2 * C).rearrange("p (k n) -> p k n", k=KC) for _ in range(2)]
        src2 = early(KC * B * 2 * LC).rearrange("p (k b d n) -> p k b d n", k=KC, b=B, d=2)
        v_out = early(2 * B * C).rearrange("p (a b n) -> p a b n", a=2, b=B)
        keysT = early(KC * B * LC).rearrange("p (k n) -> p k n", k=KC)
        x1 = x[:, 1].rearrange("p t n -> p (t n)").rearrange("p (a k n) -> p a k n", a=2, k=KC)
        srcT = x1[:, 0]
        modT = x1[:, 1]
        x_keys = x[:, 0].rearrange("p t n -> p (t n)").rearrange("p (c n) -> p c n", c=KC)
        keys_out = [kbd[:], x_keys, left[:].rearrange("p (c h) n -> p c (h n)", c=KC),
                    eS[:].rearrange("p (c h) n -> p c (h n)", c=KC)]
        ctx_rows = rden[:, 1, :].rearrange("p (t n) -> p t n", t=B // 2)
        condT = rden[:, 0, 0:KC * B].rearrange("p (k b) -> p k b", k=KC)
        scondT = rden[:, 0, 16:16 + KC * B].rearrange("p (k b) -> p k b", k=KC)
        gate_in = oT[0:B, :, :].rearrange("p k n -> p (k n)")[:, 0:3 * C]
        gate_out = qk[0:B, 0:2, :].rearrange("p k n -> p (k n)")[:, 0:3 * C]
        vrow = [qk[:, KC, 0:C], qk[:, KC, C:2 * C]]

        bank = [ctx.enter_context(nc.psum_tensor(f"bank{i}", [P, BT], F32)) for i in range(NB)]

        filled = [sem(f"filled{i}") for i in range(NB)]
        drained = [sem(f"drained{i}") for i in range(NB)]
        s_context = sem("context_and_weights_loaded")
        s_early = sem("early_inputs_loaded")
        s_consts = sem("constants_loaded")
        s_weights = sem("weights_loaded")
        s_m1_in, s_m1_split = sem("m1_weights_loaded"), sem("m1_weights_split")
        s_m1_stored, s_m1_low = sem("m1_weights_rest_stored"), sem("m1_weights_rest_loaded")
        s_h_low = sem("m1_input_rest_done")
        s_silu_c = sem("condition_silu_done")
        s_mod = sem("modulations_done")
        s_gate = sem("gate_rows_done")
        s_src2 = sem("context_doubled")
        s_keys = sem("early_keys_done")
        s_keys_stored = sem("early_keys_stored")
        s_vals = sem("early_values_done")
        s_gate_stored = sem("gate_rows_stored")
        s_zero = sem("head_blocks_zeroed")
        s_const_ready = sem("constants_rounded")
        s_xin = sem("x_loaded")
        s_g = sem("gate_loaded")
        s_wso, s_wco, s_wm2 = sem("w_so_loaded"), sem("w_co_loaded"), sem("w_m2_loaded")
        s_kv0, s_kv1 = sem("keys_values0_loaded"), sem("keys_values1_loaded")
        s_cur = sem("modulations_of_batch")
        s_gated = sem("gated_done")
        s_kr = sem("keys1_rounded")
        s_mv = sem("moments_done")
        s_rstd = sem("rstd_done")
        s_xh = sem("tiles_normalised")
        s_xb = sem("bias_added")
        s_qbh = [sem("q_by_head_even"), sem("q_by_head_odd")]
        s_kbh0, s_kbh = sem("k_by_head_first"), sem("k_by_head")
        s_cur_msa = sem("msa_modulations_of_batch")
        s_mst = sem("self_max_split")
        s_mst3 = sem("cross_max_split")
        s_rd1 = sem("self_denominators")
        s_rd = sem("cross_denominators")
        s_top8 = sem("top8_done")
        s_dif = sem("max_subtracted")
        s_exp = sem("topk_exp_done")
        s_prob = sem("topk_probs_done")
        s_store = [sem("stored0"), sem("stored1")]
        s_held = {nc.vector: sem("vector_held"), nc.gpsimd: sem("gpsimd_held")}
        s_dve, s_act, s_pool = sem("vector_step"), sem("scalar_step"), sem("gpsimd_step")

        def hold(eng):
            eng.sem_inc(s_held[eng], 1)

        def ps(key):
            return bank[PLACE[key][0]][:]

        def fill_wait(pe, key, it):
            b, n = PLACE[key]
            if n:
                pe.wait_ge(drained[b], it * ROUNDS[b] + n)

        def filled_wait(eng, key, it, ago=0):
            b, n = PLACE[key]
            eng.wait_ge(filled[b], it * ROUNDS[b] + (n + 1 - ago * ROUNDS[b]))

        def drained_wait(eng, key, it, ago=0):
            b, n = PLACE[key]
            eng.wait_ge(drained[b], it * ROUNDS[b] + (n + 1 - ago * ROUNDS[b]))

        def fill(ins, key):
            ins.then_inc(filled[PLACE[key][0]], 1)

        def drain(ins, key):
            ins.then_inc(drained[PLACE[key][0]], 1)

        ORDER = [(1, 1), (2, 0), (2, 1), (3, 0), (4, 0), (3, 1), (4, 1), (1, 0)]
        LN = {k: n for n, k in enumerate(ORDER)}
        NLN = len(ORDER)
        BIAS = {k: n for n, k in enumerate([(1, 0), (1, 1), (2, 0), (2, 1), (3, 0), (4, 0), (3, 1), (4, 1)])}

        def moments_no(n, b, it):
            return it * NLN + (LN[n, b] + 3)

        def tiles_no(n, b, it, t, ago=0):
            return it * (NLN * W) + ((LN[n, b] - ago * NLN) * W + B // 2 + W + t + 1)
        MOD_OF = {1: MSA, 2: MCA, 3: MLP, 4: XQ}
        TILES = BLKS * W

        block = ctx.enter_context(nc.Block())

        @block.sync
        def _(sp):
            def wv(name):
                return t_in[name].rearrange("(k p) n -> p k n", p=P)

            for dst, src in ((condT, t_in["condT"]), (srcT, t_in["ctxT"]), (ctx_rows, t_in["ctx_rows"]),
                             (chan[:], t_in["chan"]), (w_kv[0], wv("w_kv")),
                             (head_mask[:], t_in["head_mask"]), (pair_mask[:], t_in["pair_mask"]),
                             (vrow[0], t_in["rows"][:, 5 * C:6 * C].to_broadcast([P, C]))):
                sp.dma_start(dst, src).then_inc(s_context, 16)
            x_d = t_in["x"]

            def load_x_first(token):
                sp.dma_start(xin[:], x_d[bass.ds(token + SHIFT, BT), :].rearrange("(t p) n -> p t n", p=P)).then_inc(s_xin, 16)

            load_x_first(0)
            for dst, src in ((w_ada, wv("w_ada")), (w_ss[0], wv("Wss_q")), (w_ss[1], wv("Wss_kv")),
                             (gate_in, t_in["gate_bias"].to_broadcast([B, 3 * C])), (ident[:], t_in["ident"]),
                             (w_kv[1], wv("Wkv")), (vrow[1], t_in["rows"][:, 6 * C:7 * C].to_broadcast([P, C]))):
                sp.dma_start(dst, src).then_inc(s_early, 16)
            sp.dma_start(m1_in, wv("w_m1")).then_inc(s_m1_in, 16)
            for dst, src in ((head_select[:], t_in["head_select"]),
                             (ones_half[:].rearrange("p s n -> p (s n)"), t_in["ones_half"]),
                             (rows[:].rearrange("p r n -> p (r n)"), t_in["rows"][:, 0:5 * C].to_broadcast([P, 5 * C]))):
                sp.dma_start(dst, src).then_inc(s_consts, 16)
            for dst, name in ((w_qkv, "w_qkv"), (w_q2, "w_q"), (w_q3, "Wq"), (w_p, "Wp")):
                sp.dma_start(dst[:], wv(name)).then_inc(s_weights, 16)
            sp.wait_ge(s_m1_split, 1)
            sp.dma_start(m1_low_d, m1_low.rearrange("p k n -> p (k n)").bitcast(F32)).then_inc(s_m1_stored, 16)
            sp.wait_ge(s_gate, 2)
            sp.dma_start(gate_d, gate_out).then_inc(s_gate_stored, 16)
            for a in range(2):
                for b in range(B):
                    sp.wait_ge(s_keys, a * B + b + 1)
                    sp.dma_start(kbd_d[a, b].rearrange("p (c n) -> p c n", c=KC), keys_out[b]).then_inc(s_keys_stored, 16)
            sp.wait_ge(s_gate_stored, 16)
            sp.wait_ge(s_keys_stored, 2 * B * 16)
            sp.wait_ge(s_store[0], 16)
            sp.wait_ge(s_store[1], 16)
            sp.wait_ge(s_zero, 2)
            def one_pass(it, more):
                def load_q(b, w):
                    if w >= 2:
                        filled_wait(sp, ("B", b, w - 2, 3), it)
                    elif w == 0:
                        drained_wait(sp, ("qk", b, KC - 1), it, 0 if b else 1)
                    for h in range(HPC):
                        r = slice(h * D, (h + 1) * D)
                        sp.dma_start(q_by_head[r, w % 2, h, :, :], qk[r, 0:KC, w * P:(w + 1) * P]).then_inc(s_qbh[w % 2], 16)

                def load(dst, src, done):
                    sp.dma_start(dst, src).then_inc(done, 16)

                def of_batch(a):
                    return a[bass.ds(it, 1)].rearrange("a p n -> (a p) n")

                load_q(0, 0)
                load_q(0, 1)
                filled_wait(sp, ("y", 4, 1, 1), it, 1)
                load(gate[:].rearrange("p g n -> p (g n)"), gate_d[bass.ds(it, 1), :].to_broadcast([P, 3 * C]), s_g)
                load(w_so[:], wv("w_so"), s_wso)
                load(kbd[:].rearrange("p c n -> p (c n)"), of_batch(kbd_d[0]), s_kv0)
                load(vbd0[:].rearrange("p c n -> p (c n)"), of_batch(vbd_d[0]), s_kv0)
                load_q(0, 2)
                sp.wait_ge(s_xb, it * NLN + BIAS[1, 0] + 2)
                load(xin[:, 0:W - 1, :], x_d[bass.ds(it * L + BT + SHIFT, BT - P), :].rearrange("(t p) n -> p t n", p=P), s_xin)
                load(xin[0:P - SHIFT, W - 1, :], x_d[bass.ds(it * L + L - P + SHIFT, P - SHIFT), :], s_xin)
                load(xin[P - SHIFT:P, W - 1, :], x_d[bass.ds(it * L, SHIFT), :], s_xin)
                load_q(0, 3)
                load(w_co[:], wv("w_co"), s_wco)
                load_q(1, 0)
                load_q(1, 1)
                load(w_m2[:], wv("w_m2"), s_wm2)
                load_q(1, 2)
                load_q(1, 3)
                filled_wait(sp, ("A", 1, W - 1, 3), it)
                load(m1_low.rearrange("p k n -> p (k n)").bitcast(F32), m1_low_d, s_m1_low)
                if more:
                    sp.wait_ge(s_xb, it * NLN + BIAS[1, 1] + 2)
                    load_x_first(it * L + L)
                filled_wait(sp, ("S", 1, W - 1, KC - 1), it)
                load(kbd[:].rearrange("p c n -> p (c n)"), of_batch(kbd_d[1]), s_kv1)
                load(vbd1[:].rearrange("p c n -> p (c n)"), of_batch(vbd_d[1]), s_kv1)

            with sp.Fori(0, B - 1) as it:
                one_pass(it, True)
            one_pass(B - 1, False)
            sp.wait_ge(s_store[0], (B + 1) * 16)
            sp.wait_ge(s_store[1], (3 * B + 1) * 16)

        @block.gpsimd
        def _(pool):
            own = Chain(pool, s_pool)

            def rstd_of(n, eps):
                hold(pool)
                own.step(nc.gpsimd.tensor_scalar(veps[:, 0:n], mv[:, 0:n, 1], eps, 0.0, ALU.add, ALU.add))
                own.wait()
                nc.gpsimd.tensor_tensor(rstd[:, 0:n], veps[:, 0:n], minus_half[:, 0:n], ALU.pow).then_inc(s_rstd, 1)

            own.step(nc.gpsimd.memset(minus_half[:], -0.5))
            own.wait()
            pool.sem_inc(s_xb, 1)
            pool.wait_ge(s_mv, 1)
            rstd_of(B // 2, EPS1)
            def rstd_step(n, b, it):
                pool.wait_ge(s_mv, moments_no(n, b, it))
                rstd_of(W, EPS1 if n == 4 else EPS0)

            def keys_by_head(b, w, it, ago=0):
                if w >= 2:
                    filled_wait(pool, ("A", b, w - 2, 3), it)
                else:
                    drained_wait(pool, ("qk", b, 2 * KC - 1), it, ago)
                for c in range(KC):
                    i = nc.gpsimd.tensor_tensor(k_by_head[:, w % 2, c], kT[:, c, w * P:(w + 1) * P].unsqueeze(1).to_broadcast([P, HPC, P]),
                                                head_mask[:].unsqueeze(2).to_broadcast([P, HPC, P]), ALU.mult)
                i.then_inc(s_kbh, 1)

            def one_pass(it, more):
                def add_bias(n, b):
                    pool.wait_ge(s_xh, tiles_no(n, b, it, W - 1, 1 if (n, b) == (1, 0) else 0))
                    src = x[:, b]
                    if n == 1:
                        src = xin[:]
                        pool.wait_ge(s_store[b], it * (48 if b else 16) + 16)
                    row = rows[:, 1, :] if n == 4 else gated_bias[:, n - 1, :]
                    nc.gpsimd.tensor_tensor(x[:, b], src, row.unsqueeze(1).to_broadcast([P, W, C]), ALU.add).then_inc(s_xb, 1)

                def gate_weight(w, layer, loaded, n):
                    pool.wait_ge(loaded, it * 16 + 16)
                    for k in range(0, n, KC):
                        i = nc.gpsimd.tensor_tensor(w[:, k:k + KC, :], w[:, k:k + KC, :],
                                                    gate[:, layer, :].unsqueeze(1).to_broadcast([P, KC, C]), ALU.mult)
                    i.then_inc(s_gated, 1)

                def round_keys(b):
                    filled_wait(pool, ("ub", b, J - 1), it)
                    hold(pool)
                    nc.gpsimd.tensor_scalar(kbd1r[:], kbd[:], 1.0, 0.0, ALU.mult, ALU.add).then_inc(s_kr, 1)

                def subtract_max(b, t):
                    n = b * W + t
                    pool.wait_ge(s_top8, it * TILES + n + 1)
                    pool.wait_ge(s_prob, it * TILES + n + 1)
                    nc.gpsimd.tensor_tensor(eS[:], S[:, t, :].rearrange("p (h n) -> p h n", h=H),
                                            top[:, :, 0:1].to_broadcast([P, H, LC]), ALU.subtract).then_inc(s_dif, 1)

                keys_by_head(0, 2, it)
                pool.wait_ge(s_g, it * 16 + 16)
                nc.gpsimd.tensor_tensor(gated_bias[:], gate[:], rows[:, 2:5, :], ALU.mult).then_inc(s_gated, 1)
                pool.wait_ge(s_gated, it * 4 + 1)
                add_bias(1, 0)
                gate_weight(w_so, 0, s_wso, KC)
                keys_by_head(0, 3, it)
                rstd_step(1, 1, it)
                add_bias(1, 1)
                rstd_step(2, 0, it)
                keys_by_head(1, 1, it)
                add_bias(2, 0)
                subtract_max(0, 0)
                keys_by_head(1, 2, it)
                subtract_max(0, 1)
                keys_by_head(1, 3, it)
                subtract_max(0, 2)
                gate_weight(w_co, 1, s_wco, KC)
                rstd_step(2, 1, it)
                add_bias(2, 1)
                subtract_max(0, 3)
                subtract_max(1, 0)
                rstd_step(3, 0, it)
                add_bias(3, 0)
                gate_weight(w_m2, 2, s_wm2, J)
                for t in range(1, W):
                    if t == W - 1:
                        pool.wait_ge(s_kv1, it * 32 + 32)
                        round_keys(0)
                    subtract_max(1, t)
                rstd_step(4, 0, it)
                add_bias(4, 0)
                rstd_step(3, 1, it)
                add_bias(3, 1)
                round_keys(1)
                rstd_step(4, 1, it)
                add_bias(4, 1)
                if more:
                    rstd_step(1, 0, it)
                drained_wait(pool, ("y", 4, 0, 1), it)
                pool.dma_start(out[bass.ds(it * L + SHIFT, BT), :].rearrange("(t p) n -> p t n", p=P), x[:, 0]).then_inc(s_store[0], 16)
                if more:
                    keys_by_head(0, 1, it)
                drained_wait(pool, ("y", 4, 1, 1), it)
                pool.dma_start(out[bass.ds(it * L + BT + SHIFT, BT - P), :].rearrange("(t p) n -> p t n", p=P),
                               x[:, 1, 0:W - 1, :]).then_inc(s_store[1], 16)
                pool.dma_start(out[bass.ds(it * L + L - P + SHIFT, P - SHIFT), :], x[0:P - SHIFT, 1, W - 1, :]).then_inc(s_store[1], 16)
                pool.dma_start(out[bass.ds(it * L, SHIFT), :], x[P - SHIFT:P, 1, W - 1, :]).then_inc(s_store[1], 16)
                own.restart()

            rstd_step(1, 0, -1)
            pool.wait_ge(s_m1_split, 1)
            nc.gpsimd.memset(q_by_head[:, 0], 0.0).then_inc(s_zero, 1)
            for a in range(2):
                pool.wait_ge(s_vals, 2 * (a + 1))
                pool.dma_start(vbd_d[a].rearrange("b p n -> p b n"), v_out[:, a]).then_inc(s_store[a], 16)
            pool.wait_ge(s_m1_stored, 16)
            keys_by_head(0, 1, -1)
            own.restart()
            with pool.Fori(0, B - 1) as it:
                one_pass(it, True)
            one_pass(B - 1, False)

        @block.scalar
        def _(act):
            own = Chain(act, s_act)
            act.wait_ge(s_context, 8 * 16)
            nc.scalar.activation(scondT, condT, ACT.Silu).then_inc(s_silu_c, 1)
            for a in range(2):
                if a == 1:
                    act.wait_ge(s_mod, 2)
                    for c in range(KC):
                        filled_wait(act, ("Tc", c), 0)
                        for b in range(B):
                            r = slice(b * LC, (b + 1) * LC)
                            i = nc.scalar.activation(modT[:, c, r], ps(("Tc", c))[:, r], ACT.Identity,
                                                     bias=mod[:, 0, XKV, c, b:b + 1], scale=mod[:, 1, XKV, c, b:b + 1])
                        drain(i, ("Tc", c))
                    act.wait_ge(s_keys, B)
                for c in range(KC):
                    filled_wait(act, ("kT", a, c), 0)
                    n = CB["k0" if a == 0 else "k1"] + c
                    drain(nc.scalar.activation(keysT[:, c, :], ps(("kT", a, c))[:, 0:B * LC], ACT.Identity,
                                               bias=chan[:, n:n + 1]), ("kT", a, c))
            nc.scalar.preload_act_table_set("natural_log_exp_and_others")

            def modulated(n, b, it):
                table = cur_msa if n == 1 else cur[:, :, MOD_OF[n]]
                for c in range(KC):
                    filled_wait(act, ("T", n, b, c), it)
                    if n == 3:
                        nc.scalar.activation(qr[:, c, :], ps(("T", n, b, c)), ACT.Identity,
                                             bias=table[:, 0, c:c + 1], scale=table[:, 1, c:c + 1])
                    drain(nc.scalar.activation(input_of(n, b)[:, c, :], ps(("T", n, b, c)), ACT.Identity,
                                               bias=table[:, 0, c:c + 1], scale=table[:, 1, c:c + 1]), ("T", n, b, c))

            def biased(dst, key, n, it):
                filled_wait(act, key, it)
                drain(nc.scalar.activation(dst, ps(key), ACT.Identity, bias=chan[:, n:n + 1]), key)

            def both(dst, rounded, key, n, it):
                filled_wait(act, key, it)
                nc.scalar.activation(rounded, ps(key), ACT.Identity, bias=chan[:, n:n + 1])
                drain(nc.scalar.activation(dst, ps(key), ACT.Identity, bias=chan[:, n:n + 1]), key)

            def project_qk(b, it):
                for c in range(KC):
                    both(qk[:, c, :], qr[:, c, :], ("qk", b, c), CB["qk"] + c, it)
                for c in range(KC):
                    biased(kT[:, c, :], ("qk", b, KC + c), CB["qk"] + KC + c, it)

            def next_first(it):
                act.wait_ge(s_cur_msa, it + 2)
                modulated(1, 0, it)
                project_qk(0, it)

            def one_pass(it, more):
                def project_q2(b):
                    filled_wait(act, ("q2", b, KC - 1), it)
                    for c in range(KC):
                        biased(q2T[:, c, :], ("q2", b, c), CB["q2"] + c, it)

                def self_denominator(b, w):
                    filled_wait(act, ("PV", b, w), it)
                    if w >= 2:
                        drained_wait(act, ("PV", b, w - 2), it)
                    r = rden[:, w % 2, 0:KC * P]
                    own.step(nc.scalar.activation(r, ps(("PV", b, w))[:, KC * P:], ACT.Ln))
                    own.wait()
                    nc.scalar.activation(r, r, ACT.Exp, scale=-1.0).then_inc(s_rd1, 1)

                def window(b, w):
                    key = ("mT", b, w)
                    filled_wait(act, key, it)
                    drain(nc.scalar.activation(mTs[:, w * P:(w + 1) * P], ps(key)[:, 0:P // 2].bitcast(BF16), ACT.Copy), key)
                    for g in range(4):
                        key = ("B", b, w, g)
                        filled_wait(act, key, it)
                        drain(nc.scalar.activation(pT_self[:, w % 2, 4 * g:4 * g + 4, :], ps(key).rearrange("p (h q) -> p h q", h=4),
                                                   ACT.Exp, scale=SCORE_SCALE), key)
                    if w:
                        self_denominator(b, w - 1)

                def topk_exp(b, t):
                    act.wait_ge(s_dif, it * TILES + b * W + t + 1)
                    nc.scalar.activation(eS[:], eS[:], ACT.Exp, scale=SCORE_SCALE).then_inc(s_exp, 1)

                def take_scores(b, tiles):
                    for t in tiles:
                        for c in range(KC):
                            key = ("S", b, t, c)
                            filled_wait(act, key, it)
                            drain(nc.scalar.activation(S[:, t, c * BT:(c + 1) * BT], ps(key), ACT.Copy), key)

                def take_probs(b, tiles):
                    for t in tiles:
                        for c in range(KC):
                            key = ("TP", b, t, c)
                            filled_wait(act, key, it)
                            drain(nc.scalar.activation(pT_cross[:, 4 * c:4 * c + 4, t * P:(t + 1) * P],
                                                       ps(key).rearrange("p (h q) -> p h q", h=4), ACT.Copy), key)

                def cross_denominator(n, b):
                    for c in range(KC):
                        key = ("D", n, b, c)
                        filled_wait(act, key, it)
                        drain(nc.scalar.activation(rden[:, c, :], ps(key), ACT.Ln), key)
                        drained_wait(act, key, it)
                        nc.scalar.activation(rden[:, c, :], rden[:, c, :], ACT.Exp, scale=-1.0).then_inc(s_rd, 1)

                def silu(b, j):
                    if j >= 2:
                        drained_wait(act, ("ub", b, j - 2), it)
                    key = ("ua", b, j)
                    filled_wait(act, key, it)
                    drain(nc.scalar.activation(sa[:, j % 2, :], ps(key), ACT.Silu, bias=chan[:, CB["m1"] + j:CB["m1"] + j + 1]), key)

                def last_in(b):
                    for c in range(KC):
                        both(qk[:, KC + c, :], qr[:, c, :], ("q3", b, c), CB["q3"] + c, it)

                def last_scores(b):
                    key = ("mT3", b)
                    filled_wait(act, key, it)
                    drain(nc.scalar.activation(mTs[:], ps(key)[:, 0:BT // 2].bitcast(BF16), ACT.Copy), key)
                    for p in range(PAIRS):
                        key = ("B3", b, p)
                        filled_wait(act, key, it)
                        drain(nc.scalar.activation(pT_cross[:, p, :], ps(key), ACT.Exp, scale=SCORE_SCALE), key)

                nc.scalar.preload_act_table_set("natural_log_exp_and_others")
                for w in range(W):
                    window(0, w)
                self_denominator(0, W - 1)
                modulated(1, 1, it)
                project_qk(1, it)
                act.wait_ge(s_cur, it + 1)
                modulated(2, 0, it)
                project_q2(0)
                take_scores(0, range(W))
                topk_exp(0, 0)
                for w in range(W):
                    window(1, w)
                    if w % 2:
                        topk_exp(0, 1 + w // 2)
                self_denominator(1, W - 1)
                take_probs(0, range(0, 3))
                modulated(2, 1, it)
                project_q2(1)
                topk_exp(0, W - 1)
                take_scores(1, range(0, 2))
                take_probs(0, range(3, W))
                cross_denominator(2, 0)
                topk_exp(1, 0)
                take_scores(1, range(2, W))
                modulated(3, 0, it)
                for j in range(J):
                    silu(0, j)
                    if j == 3:
                        nc.scalar.preload_act_table_set("natural_log_exp_and_others")
                        topk_exp(1, 1)
                nc.scalar.preload_act_table_set("natural_log_exp_and_others")
                topk_exp(1, 2)
                take_probs(1, range(W - 1))
                modulated(4, 0, it)
                topk_exp(1, 3)
                last_in(0)
                take_probs(1, range(W - 1, W))
                cross_denominator(2, 1)
                last_scores(0)
                modulated(3, 1, it)
                for j in range(J):
                    silu(1, j)
                nc.scalar.preload_act_table_set("natural_log_exp_and_others")
                cross_denominator(4, 0)
                modulated(4, 1, it)
                last_in(1)
                if more:
                    next_first(it)
                last_scores(1)
                cross_denominator(4, 1)
                own.restart()

            act.wait_ge(s_gate_stored, 16)
            next_first(-1)
            with act.Fori(0, B - 1) as it:
                one_pass(it, True)
            one_pass(B - 1, False)

        @block.vector
        def _(dve):
            own = Chain(dve, s_dve)

            def moments_of(src, tiles):
                for t in tiles:
                    i = nc.vector.bn_stats(stats[:, t, :], src[:, t, :])
                own.step(i)

            def moments_done(n):
                own.wait()
                for t in range(n):
                    i = nc.vector.bn_aggr(mv[:, t, :], stats[:, t, :])
                i.then_inc(s_mv, 1)

            def moments(src, n):
                moments_of(src, range(n))
                moments_done(n)

            def normalise(dst, src, n):
                for t in range(n):
                    nc.vector.tensor_scalar(dst[:, t, :], src[:, t, :], mv[:, t, 0:1], rstd[:, t:t + 1],
                                            ALU.subtract, ALU.mult).then_inc(s_xh, 1)

            dve.sem_inc(s_prob, 1)
            nc.vector.memset(vpad[:], 0.0)
            nc.vector.memset(mst[:], 0.0)
            dve.wait_ge(s_context, 8 * 16)
            moments(ctx_rows, B // 2)

            def double_context(src):
                for k in range(KC):
                    i = nc.vector.tensor_copy(src2[:, k], src[:, k, :].rearrange("p (b n) -> p b n", b=B)
                                              .unsqueeze(2).to_broadcast([P, B, 2, LC]))
                i.then_inc(s_src2, 1)

            def early_keys(a):
                if a:
                    dve.wait_ge(s_keys_stored, B * 16)
                for c in range(KC):
                    drained_wait(dve, ("kT", a, c), 0)
                for b in range(B):
                    for c in range(KC):
                        i = nc.vector.tensor_tensor(
                            keys_out[b][:, c, :].rearrange("p (h n) -> p h n", h=HPC),
                            keysT[:, c, b * LC:(b + 1) * LC].unsqueeze(1).to_broadcast([P, HPC, LC]),
                            head_mask[:].unsqueeze(2).to_broadcast([P, HPC, LC]), ALU.mult)
                    i.then_inc(s_keys, 1)

            def early_values(a):
                for u in range(B // 2):
                    key = ("vc", a, u)
                    filled_wait(dve, key, 0)
                    v = v_out[:, a, 2 * u:2 * u + 2, :]
                    drain(nc.vector.tensor_tensor(v, ps(key).rearrange("p (b n) -> p b n", b=2),
                                                  vrow[a].unsqueeze(1).to_broadcast([P, 2, C]), ALU.add), key)
                    drained_wait(dve, key, 0)
                    v = v.rearrange("p b (h n) -> p (b h) n", n=2 * D)
                    nc.vector.tensor_tensor(v, v, pair_mask[:].unsqueeze(1).to_broadcast([P, 2 * PAIRS, 2 * D]),
                                            ALU.mult).then_inc(s_vals, 1)

            def modulations_and_gates():
                filled_wait(dve, ("mod",), 0)
                half = NMOD * KC
                for s in range(2):
                    bias = chan[:, s * half:(s + 1) * half].unsqueeze(2).to_broadcast([P, half, B])
                    i = nc.vector.scalar_tensor_tensor(
                        mod[:, s].rearrange("p m c b -> p (m c) b"),
                        ps(("mod",))[:, s * half * B:(s + 1) * half * B].rearrange("p (m b) -> p m b", b=B),
                        float(s), bias, ALU.add, ALU.add)
                    i.then_inc(s_mod, 1)
                dve.wait_ge(s_mod, 2)
                dve.sem_inc(drained[PLACE[("mod",)][0]], 1)
                for i in range(2):
                    filled_wait(dve, ("gate", i), 0)
                    n = (2 - i) * C
                    own.step(nc.vector.tensor_tensor(gate_out[:, i * 2 * C:i * 2 * C + n], ps(("gate", i))[0:B, 0:n],
                                                     gate_in[:, i * 2 * C:i * 2 * C + n], ALU.add))
                    own.wait()
                    dve.sem_inc(drained[PLACE[("gate", i)][0]], 1)
                    dve.sem_inc(s_gate, 1)

            def residual(n, b, it, after=None):
                dve.wait_ge(s_xb, it * NLN + BIAS[n, b] + 2)
                for u in range(2):
                    key = ("y", n, b, u)
                    filled_wait(dve, key, it)
                    v = x[:, b, 2 * u:2 * u + 2, :]
                    drain(nc.vector.tensor_tensor(v, ps(key).rearrange("p (t n) -> p t n", t=2), v, ALU.add), key)
                    if after:
                        drained_wait(dve, key, it)
                        after(u)

            def layer_norm(n, b, it):
                if n == 1:
                    src = xin[:]
                    dve.wait_ge(s_xin, it * 64 + 64 + (0 if b else 16))
                    moments(src, W)
                else:
                    src = x[:, b]
                    residual(n - 1, b, it, lambda u: moments_of(src, range(2 * u, 2 * u + 2)))
                    moments_done(W)
                normalise_for(n, b, it)

            def normalise_for(n, b, it):
                src = xin[:] if n == 1 else x[:, b]
                dve.wait_ge(s_rstd, moments_no(n, b, it))
                if LN[n, b]:
                    filled_wait(dve, ("T", *ORDER[LN[n, b] - 1], 1), it)
                normalise(xh, src, W)

            def take_values(b, it, halves=(0, 1)):
                for u in halves:
                    key = ("v", b, u)
                    filled_wait(dve, key, it)
                    for i in range(2):
                        dst = vpad[:, 2 * u + i].rearrange("p h (s n) -> p h s n", n=D)[:, :, 0:4:3, :]
                        ins = nc.vector.tensor_tensor(
                            dst, ps(key)[:, i * C:(i + 1) * C].rearrange("p (h s n) -> p h s n", s=2, n=D),
                            rows[:, 0, :].rearrange("p (h s n) -> p h s n", s=2, n=D), ALU.add)
                    drain(ins, key)

            def first_keys_by_head(b, it):
                for c in range(KC):
                    drained_wait(dve, ("qk", b, KC + c), it)
                    i = nc.vector.tensor_tensor(k_by_head[:, 0, c], kT[:, c, 0:P].unsqueeze(1).to_broadcast([P, HPC, P]),
                                                head_mask[:].unsqueeze(2).to_broadcast([P, HPC, P]), ALU.mult)
                i.then_inc(s_kbh0, 1)

            def msa_modulations(batch):
                nc.vector.tensor_copy(cur_msa[:].unsqueeze(3), mod[:, :, MSA, :, bass.ds(batch, 1)]).then_inc(s_cur_msa, 1)

            def one_pass(it, more):
                def split_max(slot, done):
                    own.step(nc.vector.tensor_copy(mst[:, slot, 0:H], negm[:, slot]))
                    own.wait()
                    nc.vector.tensor_tensor(mst[:, slot, H:2 * H], negm[:, slot], mst[:, slot, 0:H], ALU.subtract).then_inc(done, 1)

                def window_max(b, w):
                    for g in range(4):
                        key = ("A", b, w, g)
                        filled_wait(dve, key, it)
                        drain(nc.vector.tensor_reduce(negm[:, w, 4 * g:4 * g + 4], ps(key).rearrange("p (h n) -> p h n", h=4),
                                                      AX_X, ALU.max, negate=True), key)
                    drained_wait(dve, ("A", b, w, 3), it)
                    split_max(w, s_mst)

                def window_divide(b, w):
                    key = ("PV", b, w)
                    dve.wait_ge(s_rd1, (it * BLKS + b) * W + w + 1)
                    drain(nc.vector.tensor_tensor(oT[:, :, w * P:(w + 1) * P], ps(key)[:, 0:KC * P].rearrange("p (c n) -> p c n", c=KC),
                                                  rden[:, w % 2, 0:KC * P].rearrange("p (c n) -> p c n", c=KC), ALU.mult), key)

                def cross_divide(n, b):
                    for c in range(KC):
                        key = ("O", n, b, c)
                        filled_wait(dve, key, it)
                        dve.wait_ge(s_rd, (it * 4 + {(2, 0): 0, (2, 1): 1, (4, 0): 2, (4, 1): 3}[n, b]) * KC + c + 1)
                        drain(nc.vector.tensor_tensor(oT[:, c, :], ps(key), rden[:, c, :], ALU.mult), key)

                def topk_step(b, t, s):
                    Sh = S[:, t, :].rearrange("p (h n) -> p h n", h=H)
                    if s == 0:
                        drained_wait(dve, ("S", b, t, KC - 1), it)
                    elif s == 1:
                        dve.wait_ge(s_top8, it * TILES + b * W + t + 1)
                    if s:
                        own.wait()
                    if s == 4:
                        dve.wait_ge(s_exp, it * TILES + b * W + t + 1)
                        nc.vector.scalar_tensor_tensor(Sh, left[:], REPLACED, eS[:], ALU.is_equal, ALU.mult).then_inc(s_prob, 1)
                        return
                    hold(dve)
                    for h in range(H):
                        eight = top[:, h, 0:8] if s < 2 else top[:, h, 8:16]
                        src = Sh[:, h, :] if s < 2 else left[:, h, :]
                        if s % 2 == 0:
                            i = nc.vector.max(eight, src)
                        else:
                            i = nc.vector.match_replace(left[:, h, :], eight, src, REPLACED)
                    if s == 0:
                        i.then_inc(s_top8, 1)
                    else:
                        own.step(i)

                def input_rest(b):
                    for c in range(KC):
                        drained_wait(dve, ("T", 3, b, c), it)
                        nc.vector.tensor_tensor(h_low[:, c, :], hT[:, c, :], qr[:, c, :], ALU.subtract).then_inc(s_h_low, 1)

                def topk_quarter(n):
                    topk_step(1, n // 4, n % 4)
                    if n % 4 == 3:
                        topk_step(1, n // 4, 4)

                def gated_linear(b, j):
                    drained_wait(dve, ("ua", b, j), it)
                    key = ("ub", b, j)
                    filled_wait(dve, key, it)
                    n = CB["m1"] + J + j
                    drain(nc.vector.scalar_tensor_tensor(hid[:, j, :], ps(key), chan[:, n:n + 1], sa[:, j % 2, :],
                                                         ALU.add, ALU.mult), key)

                def last_max(b):
                    for t in range(W):
                        for c in range(KC):
                            key = ("A3", b, t, c)
                            filled_wait(dve, key, it)
                            drain(nc.vector.tensor_reduce(negm[:, t, HPC * c:HPC * (c + 1)], ps(key).rearrange("p (h n) -> p h n", h=HPC),
                                                          AX_X, ALU.max, negate=True), key)
                        drained_wait(dve, ("A3", b, t, KC - 1), it)
                        split_max(t, s_mst3)

                nc.vector.tensor_copy(cur[:].rearrange("p s m c -> p (s m c)").unsqueeze(2),
                                      mod[:].rearrange("p s m c b -> p (s m c) b")[:, :, bass.ds(it, 1)]).then_inc(s_cur, 1)
                window_max(0, 0)
                for w in range(W):
                    if w + 1 < W:
                        window_max(0, w + 1)
                    if w:
                        window_divide(0, w - 1)
                    if w == 2:
                        layer_norm(1, 1, it)
                window_divide(0, W - 1)
                layer_norm(2, 0, it)
                first_keys_by_head(1, it)
                take_values(1, it, (0,))
                for s in range(2):
                    topk_step(0, 0, s)
                take_values(1, it, (1,))
                topk_step(0, 0, 2)
                window_max(1, 0)
                topk_step(0, 0, 3)
                for w in range(W):
                    if w + 1 < W:
                        window_max(1, w + 1)
                    if w % 2 == 0:
                        topk_step(0, w // 2, 4)
                    for s in (2 * (w % 2), 2 * (w % 2) + 1):
                        topk_step(0, 1 + w // 2, s)
                    if w:
                        window_divide(1, w - 1)
                topk_step(0, W - 2, 4)
                window_divide(1, W - 1)
                layer_norm(2, 1, it)
                for s in range(5):
                    topk_step(0, W - 1, s)
                topk_quarter(0)
                topk_quarter(1)
                cross_divide(2, 0)
                topk_quarter(2)
                layer_norm(3, 0, it)
                input_rest(0)
                n = 3
                for j, quarters in enumerate(QUARTERS):
                    for n in range(n, n + quarters):
                        topk_quarter(n)
                    n += bool(quarters)
                    gated_linear(0, j)
                for n in range(n, 14):
                    topk_quarter(n)
                layer_norm(4, 0, it)
                for n in range(14, 4 * W):
                    topk_quarter(n)
                cross_divide(2, 1)
                residual(2, 1, it, lambda u: moments_of(x[:, 1], range(2 * u, 2 * u + 2)))
                moments_done(W)
                last_max(0)
                normalise_for(3, 1, it)
                input_rest(1)
                for j in range(J):
                    gated_linear(1, j)
                layer_norm(4, 1, it)
                cross_divide(4, 0)
                if more:
                    msa_modulations(it + 1)
                    layer_norm(1, 0, it)
                residual(4, 0, it)
                last_max(1)
                if more:
                    first_keys_by_head(0, it)
                cross_divide(4, 1)
                if more:
                    take_values(0, it)
                residual(4, 1, it)
                own.restart()

            double_context(srcT)
            dve.wait_ge(s_rstd, 1)
            normalise(ctx_rows, ctx_rows, B // 2)
            layer_norm(1, 0, -1)
            early_values(0)
            early_keys(0)
            dve.wait_ge(s_early, 7 * 16)
            nc.vector.tensor_copy(identb[:], ident[:])
            dve.wait_ge(s_consts, 3 * 16)
            nc.vector.tensor_copy(head_rows[:], head_select[:].unsqueeze(2).to_broadcast([P, H, P])).then_inc(s_const_ready, 1)
            dve.wait_ge(s_m1_in, 16)
            own.step(nc.vector.tensor_copy(w_m1[:], m1_in))
            own.wait()
            nc.vector.tensor_tensor(m1_low, m1_in, w_m1[:], ALU.subtract).then_inc(s_m1_split, 1)
            dve.wait_ge(s_m1_split, 1)
            nc.vector.memset(q_by_head[:, 1], 0.0).then_inc(s_zero, 1)
            modulations_and_gates()
            msa_modulations(0)
            drained_wait(dve, ("Tc", 1), 0)
            double_context(modT)
            early_values(1)
            early_keys(1)
            dve.wait_ge(s_m1_stored, 16)
            first_keys_by_head(0, -1)
            take_values(0, -1)
            own.restart()
            with dve.Fori(0, B - 1) as it:
                one_pass(it, True)
            one_pass(B - 1, False)

        @block.tensor
        def _(pe):
            def mm(dst, lhsT, rhs, start, stop):
                return nc.tensor.matmul(dst, lhsT, rhs, start=start, stop=stop)

            def layer_inputs(n, b, outputs, it):
                for first in range(0, len(outputs), 2):
                    for k in range(KC):
                        if first == 0:
                            drained_wait(pe, ("T", n, b, k), it)
                        for key, w, at in outputs[first:first + 2]:
                            if k == 0:
                                fill_wait(pe, key, it)
                            i = mm(ps(key), w[:, k, at:at + P], input_of(n, b)[:, k, :], k == 0, k == KC - 1)
                            if k == KC - 1:
                                fill(i, key)

            def channels(key, dst, weights, rhs, it):
                fill_wait(pe, key, it)
                for k in range(KC):
                    i = mm(dst, weights(k), rhs(k), k == 0, k == KC - 1)
                return i

            pe.wait_ge(s_context, 8 * 16)
            for a in range(2):
                if a == 1:
                    pe.wait_ge(s_early, 7 * 16)
                    pe.wait_ge(s_silu_c, 1)
                    fill_wait(pe, ("mod",), 0)
                    for s in range(2):
                        for m in range(NMOD):
                            for c in range(KC):
                                if m <= MLP:
                                    w, col = w_ada, (3 * m + s) * C + c * P
                                else:
                                    w, col = w_ss[m - XQ], (1 - s) * C + c * P
                                at = ((s * NMOD + m) * KC + c) * B
                                for k in range(KC):
                                    i = mm(ps(("mod",))[:, at:at + B], w[:, k, col:col + P], scondT[:, k, :], k == 0, k == KC - 1)
                    fill(i, ("mod",))
                    for i_ in range(2):
                        fill_wait(pe, ("gate", i_), 0)
                        for m in ((MSA, MCA), (MLP,))[i_]:
                            at = (m - 2 * i_) * C
                            for k in range(KC):
                                i = mm(ps(("gate", i_))[0:B, at:at + C], scondT[:, k, :], w_ada[:, k, (3 * m + 2) * C:(3 * m + 3) * C],
                                       k == 0, k == KC - 1)
                        fill(i, ("gate", i_))
                    pe.wait_ge(s_xh, B // 2)
                    pe.wait_ge(s_const_ready, 1)
                    for c in range(KC):
                        fill_wait(pe, ("Tc", c), 0)
                        for t in range(B // 2):
                            i = nc.tensor.transpose(ps(("Tc", c))[:, t * P:(t + 1) * P], ctx_rows[:, t, c * P:(c + 1) * P], ident[:])
                        fill(i, ("Tc", c))
                    for c in range(KC):
                        drained_wait(pe, ("Tc", c), 0)
                src = (srcT, modT)[a]
                for c in range(KC):
                    key = ("kT", a, c)
                    fill(channels(key, ps(key)[:, 0:B * LC], lambda k: w_kv[a][:, k, c * P:(c + 1) * P],
                                  lambda k: src[:, k, :], 0), key)
                pe.wait_ge(s_src2, a + 1)
                for u in range(B // 2):
                    key = ("vc", a, u)
                    for i_ in range(2):
                        i = channels(key, ps(key)[:, i_ * C:(i_ + 1) * C],
                                     lambda k: src2[:, k, 2 * u + i_].rearrange("p d n -> p (d n)"),
                                     lambda k: w_kv[a][:, k, C:2 * C], 0)
                    fill(i, key)
            pe.wait_ge(s_weights, 4 * 16)
            pe.wait_ge(s_m1_split, 1)

            def transposed(n, b, it):
                for c in range(KC):
                    key = ("T", n, b, c)
                    fill_wait(pe, key, it)
                    for t in range(W):
                        if c == 0:
                            pe.wait_ge(s_xh, tiles_no(n, b, it, t))
                        i = nc.tensor.transpose(ps(key)[:, t * P:(t + 1) * P], xh[:, t, c * P:(c + 1) * P], ident[:])
                    fill(i, key)

            def qk_in(b, it):
                layer_inputs(1, b, [(("qk", b, i_), w_qkv, i_ * P) for i_ in range(2 * KC)], it)

            def v_in(b, it, halves=(0, 1)):
                for u in halves:
                    key = ("v", b, u)
                    for i_ in range(2):
                        t = 2 * u + i_
                        i = channels(key, ps(key)[:, i_ * C:(i_ + 1) * C], lambda k: input_of(1, b)[:, k, t * P:(t + 1) * P],
                                     lambda k: w_qkv[:, k, 2 * C:3 * C], it)
                    fill(i, key)

            def one_pass(it, more):
                def scores_for_max(b, w):
                    if w:
                        pe.wait_ge(s_kbh, (it * BLKS + b) * (W - 1) + w)
                    else:
                        pe.wait_ge(s_kbh0, it * BLKS + b + 1)
                    for g in range(4):
                        key = ("A", b, w, g)
                        fill_wait(pe, key, it)
                        c, h = g // 2, (g % 2) * 4
                        fill(mm(ps(key), qr[:, c, w * P:(w + 1) * P], k_by_head[:, w % 2, c, h:h + 4, :], True, True), key)

                def scores_minus_max(b, w):
                    key = ("mT", b, w)
                    fill_wait(pe, key, it)
                    pe.wait_ge(s_mst, (it * BLKS + b) * W + w + 1)
                    fill(nc.tensor.transpose(ps(key)[:, 0:P // 2].bitcast(BF16), mst[:, w, :], identb[:]), key)
                    pe.wait_ge(s_qbh[w % 2], ((it * BLKS + b) * 2 + w // 2) * HPC * 16 + HPC * 16)
                    for g in range(4):
                        key = ("B", b, w, g)
                        fill_wait(pe, key, it)
                        c, h = g // 2, (g % 2) * 4
                        mm(ps(key), kT[:, c, w * P:(w + 1) * P], q_by_head[:, w % 2, h:h + 4, c, :], True, False)
                        if g == 0:
                            drained_wait(pe, ("mT", b, w), it)
                        for i_ in range(4):
                            i = mm(ps(key)[:, i_ * P:(i_ + 1) * P], head_rows[:, 4 * g + i_, :], mTs[:, w * P:(w + 1) * P],
                                   False, i_ == 3)
                        fill(i, key)

                def window_values(b, w):
                    key = ("PV", b, w)
                    fill_wait(pe, key, it)
                    drained_wait(pe, ("B", b, w, 3), it)
                    for c in range(KC):
                        for s in range(2):
                            for p in range(4):
                                i = mm(ps(key)[32 * p:32 * p + 32, c * P:(c + 1) * P], vpad[:, w, 4 * c + p, 2 * D * s:2 * D * (s + 1)],
                                       pT_self[:, w % 2, HPC * c + 2 * p + s, :], s == 0, s == 1)
                    for s in range(2):
                        for p in range(4):
                            i = mm(ps(key)[32 * p:32 * p + 32, KC * P:], ones_half[:, s, :],
                                   pT_self[:, w % 2, 2 * p + s::HPC, :], s == 0, s == 1)
                    fill(i, key)

                def project(n, b):
                    w, src, chunks = {1: (w_so, oT, KC), 2: (w_co, oT, KC), 3: (w_m2, hid, J), 4: (w_p, oT, KC)}[n]
                    if n <= 3:
                        pe.wait_ge(s_gated, it * 4 + n + 1)
                    if n == 1:
                        drained_wait(pe, ("PV", b, W - 1), it)
                    elif n == 3:
                        drained_wait(pe, ("ub", b, J - 1), it)
                    else:
                        drained_wait(pe, ("O", n, b, KC - 1), it)
                    for u in range(2):
                        key = ("y", n, b, u)
                        fill_wait(pe, key, it)
                        for i_ in range(2):
                            t = 2 * u + i_
                            for k in range(chunks):
                                i = mm(ps(key)[:, i_ * C:(i_ + 1) * C], src[:, k, t * P:(t + 1) * P], w[:, k, :],
                                       k == 0, k == chunks - 1)
                        fill(i, key)

                def windows(b):
                    drained_wait(pe, ("v", b, 1), it, 0 if b else 1)
                    scores_for_max(b, 0)
                    for w in range(W):
                        if w + 1 < W:
                            scores_for_max(b, w + 1)
                        scores_minus_max(b, w)
                        if w:
                            window_values(b, w - 1)
                    window_values(b, W - 1)

                def cross_in(b):
                    transposed(2, b, it)
                    layer_inputs(2, b, [(("q2", b, c), w_q2, c * P) for c in range(KC)], it)

                def scores(b, tiles):
                    if b == 0:
                        pe.wait_ge(s_kv0, it * 32 + 32)
                    drained_wait(pe, ("q2", b, KC - 1), it)
                    for t in tiles:
                        for c in range(KC):
                            key = ("S", b, t, c)
                            fill_wait(pe, key, it)
                            fill(mm(ps(key), q2T[:, c, t * P:(t + 1) * P], kbd[:, c, :], True, True), key)

                def values(n, b):
                    vals = vbd0 if n == 2 else vbd1
                    drained_wait(pe, ("TP", b, W - 1, KC - 1) if n == 2 else ("B3", b, PAIRS - 1), it)
                    for c in range(KC):
                        key = ("D", n, b, c)
                        fill_wait(pe, key, it)
                        for p in range(4):
                            i = mm(ps(key)[32 * p:32 * p + 32, :], pair_mask[:], pT_cross[:, 4 * c + p, :], True, True)
                        fill(i, key)
                        key = ("O", n, b, c)
                        fill_wait(pe, key, it)
                        for p in range(4):
                            i = mm(ps(key)[32 * p:32 * p + 32, :], vals[:, 4 * c + p, :], pT_cross[:, 4 * c + p, :], True, True)
                        fill(i, key)

                def probs(b, tiles):
                    for t in tiles:
                        pe.wait_ge(s_prob, it * TILES + b * W + t + 2)
                        for c in range(KC):
                            key = ("TP", b, t, c)
                            fill_wait(pe, key, it)
                            for p in range(4):
                                at = (4 * c + p) * P
                                i = nc.tensor.transpose(ps(key)[:, p * P:(p + 1) * P], S[:, t, at:at + P], ident[:])
                            fill(i, key)

                def mlp(b):
                    transposed(3, b, it)
                    if b == 0:
                        pe.wait_ge(s_m1_low, it * 16 + 16)

                    def rounded_input(key, at, wait):
                        fill_wait(pe, key, it)
                        for w in (w_m1, m1_low):
                            for k in range(KC):
                                if wait and w is w_m1:
                                    drained_wait(pe, ("T", 3, b, k), it)
                                mm(ps(key), w[:, k, at:at + P], qr[:, k, :], w is w_m1 and k == 0, False)

                    def rest_of_input(key, at, wait):
                        for k in range(KC):
                            if wait:
                                pe.wait_ge(s_h_low, (it * BLKS + b) * KC + k + 1)
                            i = mm(ps(key), w_m1[:, k, at:at + P], h_low[:, k, :], False, k == KC - 1)
                        fill(i, key)

                    for j in range(J):
                        rounded_input(("ua", b, j), j * P, j == 0)
                        rounded_input(("ub", b, j), HID + j * P, False)
                        rest_of_input(("ua", b, j), j * P, j == 0)
                        rest_of_input(("ub", b, j), HID + j * P, False)
                    project(3, b)

                def last_in(b):
                    layer_inputs(4, b, [(("q3", b, c), w_q3, c * P) for c in range(KC)], it)

                def last_for_max(b, tiles):
                    pe.wait_ge(s_kr, it * BLKS + b + 1)
                    drained_wait(pe, ("q3", b, KC - 1), it)
                    for t in tiles:
                        for c in range(KC):
                            key = ("A3", b, t, c)
                            fill_wait(pe, key, it)
                            fill(mm(ps(key), qr[:, c, t * P:(t + 1) * P], kbd1r[:, c, :], True, True), key)

                def last_scores(b):
                    def pair_rows(p):
                        at = 2 * p * P + P - LC
                        return head_rows[:].rearrange("p h n -> p (h n)")[:, at:at + 2 * LC]

                    def products(p):
                        key = ("B3", b, p)
                        fill_wait(pe, key, it)
                        c = p // 4
                        mm(ps(key), kbd[:, c, (p % 4) * P:(p % 4 + 1) * P], qk[:, KC + c, :], True, False)

                    def minus_max(p):
                        fill(mm(ps(("B3", b, p)), pair_rows(p), mTs[:], False, True), ("B3", b, p))

                    for p in range(LAST_AHEAD):
                        products(p)
                    key = ("mT3", b)
                    fill_wait(pe, key, it)
                    for t in range(W):
                        pe.wait_ge(s_mst3, (it * BLKS + b) * W + t + 1)
                        i = nc.tensor.transpose(ps(key)[:, t * P // 2:(t + 1) * P // 2].bitcast(BF16), mst[:, t, :], identb[:])
                    fill(i, key)
                    drained_wait(pe, key, it)
                    for p in range(LAST_AHEAD):
                        minus_max(p)
                    for p in range(LAST_AHEAD, PAIRS):
                        products(p)
                        minus_max(p)

                def skip(keys):
                    for key in keys:
                        pass_over(key, it)

                windows(0)
                transposed(1, 1, it)
                project(1, 0)
                qk_in(1, it)
                cross_in(0)
                v_in(1, it, (0,))
                scores(0, range(W))
                v_in(1, it, (1,))
                windows(1)
                probs(0, range(0, 1))
                project(1, 1)
                probs(0, range(1, 3))
                cross_in(1)
                scores(1, range(0, 2))
                probs(0, range(3, W))
                values(2, 0)
                scores(1, range(2, 3))
                project(2, 0)
                scores(1, range(3, W))
                mlp(0)
                probs(1, range(W - 1))
                transposed(4, 0, it)
                last_in(0)
                probs(1, range(W - 1, W))
                values(2, 1)
                last_for_max(0, range(0, 2))
                project(2, 1)
                last_for_max(0, range(2, W))
                last_scores(0)
                mlp(1)
                values(4, 0)
                transposed(4, 1, it)
                last_in(1)
                project(4, 0)
                last_for_max(1, range(W))
                if more:
                    transposed(1, 0, it)
                    qk_in(0, it)
                else:
                    skip(TAIL[:TAIL.index(("qk", 0, 2 * KC - 1)) + 1])
                last_scores(1)
                values(4, 1)
                if more:
                    v_in(0, it)
                else:
                    skip([("v", 0, 0), ("v", 0, 1)])
                project(4, 1)

            def pass_over(key, it):
                fill_wait(pe, key, it)
                pe.sem_inc(filled[PLACE[key][0]], 1)
                pe.sem_inc(drained[PLACE[key][0]], 1)

            for key in SKIPPED:
                pass_over(key, 0)
            for n, key in enumerate(TAIL):
                if key == ("T", 1, 0, 0):
                    transposed(1, 0, -1)
                elif key == ("qk", 0, 0):
                    qk_in(0, -1)
                elif key == ("v", 0, 0):
                    v_in(0, -1)
                elif key not in AHEAD:
                    pass_over(key, -1)
            with pe.Fori(0, B - 1) as it:
                one_pass(it, True)
            one_pass(B - 1, False)


def kernel(**inputs):
    import numpy as np
    import concourse.bacc as bacc
    from concourse.bass_utils import run_bass_kernel_spmd

    def arr(name):
        return np.ascontiguousarray(inputs[name])

    def cols(v):
        return v.reshape(-1, P).T

    a, b = "L0_xcond_", "L1_xcond_"
    ada = arr(a + "b_ada").reshape(3, 3, C)
    ssq, sskv = arr(b + "bss_q").reshape(2, C), arr(b + "bss_kv").reshape(2, C)
    bqkv, bkv, bkv1 = arr(a + "b_qkv"), arr(a + "b_kv"), arr(b + "bkv")
    chan = np.concatenate([
        cols(np.concatenate([ada[0, 0], ada[1, 0], ada[2, 0], ssq[1], sskv[1]])),
        cols(np.concatenate([ada[0, 1], ada[1, 1], ada[2, 1], ssq[0], sskv[0]])),
        cols(bqkv[:2 * C]), cols(arr(a + "b_q")), cols(bkv[:C]), cols(arr(a + "b_m1")), cols(arr(b + "bq")), cols(bkv1[:C])], axis=1)
    rows = np.concatenate([bqkv[2 * C:], arr(b + "bp"), arr(a + "b_so"), arr(a + "b_co"), arr(a + "b_m2"), bkv[C:], bkv1[C:]])[None, :]
    ctx = arr("ctx_1024").reshape(B * LC, C)
    r = np.arange(P)
    head = np.arange(H)
    head_select = np.zeros((P, H), np.float32)
    head_select[:2 * H] = (r[:2 * H] % H)[:, None] == head[None, :]
    arrays = {
        "x": arr("x").reshape(B * L, C),
        "condT": arr("cond_1024").T.reshape(KC, P, B).transpose(1, 0, 2),
        "ctxT": ctx.T.reshape(KC, P, B * LC).transpose(1, 0, 2),
        "ctx_rows": ctx.reshape(B // 2, P, C).transpose(1, 0, 2),
        "chan": chan, "gate_bias": ada[:, 2].reshape(1, 3 * C), "rows": rows,
        "ident": np.eye(P, dtype=np.float32),
        "head_select": head_select,
        "head_mask": (r[:, None] // D == np.arange(HPC)[None, :]).astype(np.float32),
        "pair_mask": (r[:, None] // LC == np.arange(2 * D)[None, :] // D).astype(np.float32),
        "ones_half": np.repeat(np.eye(2, dtype=np.float32), D, axis=1).reshape(1, 4 * D).repeat(P, axis=0),
    }
    for n in ("w_ada", "w_qkv", "w_so", "w_q", "w_kv", "w_co", "w_m1", "w_m2"):
        arrays[n] = arr(a + n)
    for n in ("Wq", "Wkv", "Wp", "Wss_q", "Wss_kv"):
        arrays[n] = arr(b + n)
    arrays = {"in_" + k: np.ascontiguousarray(v) for k, v in arrays.items()}

    nc = bacc.Bacc("TRN2", target_bir_lowering=False, num_devices=1)
    t_in = {k[3:]: nc.dram_tensor(k, v.shape, mybir.dt.from_np(v.dtype), kind="ExternalInput").ap() for k, v in arrays.items()}
    out = nc.dram_tensor("out", [B * L, C], F32, kind="ExternalOutput").ap()
    build(nc, t_in, out)
    res = run_bass_kernel_spmd(nc, [arrays], core_ids=[0])
    return res.results[0]["out"].reshape(B, L, C)
```
